# Optimizing a Trainium2 kernel written in Bass

```python
import numpy as np
import jax
import jax.numpy as jnp

def _softmax(x, axis=-1):
    return jax.nn.softmax(x, axis=axis)

def _gelu(x):
    return jax.nn.gelu(x, approximate=True)

def _silu(x):
    return jax.nn.silu(x)

def _sigmoid(x):
    return jax.nn.sigmoid(x)

def _layernorm(x, axis=-1, eps=1e-05):
    m = jnp.mean(x, axis=axis, keepdims=True)
    v = jnp.var(x, axis=axis, keepdims=True)
    return (x - m) / jnp.sqrt(v + eps)

def _scatter_add(tgt, idx, src, axis=0):
    return tgt.at[idx].add(src)

def _segment_sum(src, seg, n):
    return jax.ops.segment_sum(src, seg, n)
kernel_name = 'mk_gnn_resnorm_d2_gnn_r64_b99cff'

def setup_inputs(seed: int=0):
    np.random.seed(seed)
    _w = jnp.asarray

    def _rec_inputs():
        import jax
        import jax.numpy as jnp
        _gk = jax.random.key(seed)
        x = -0.000202 + 1 * jax.random.normal(jax.random.fold_in(_gk, 1), (50000, 128), jnp.float32)
        src = jax.random.randint(jax.random.fold_in(_gk, 2), (25000,), 0, 50000, jnp.int32)
        dst = jax.random.randint(jax.random.fold_in(_gk, 3), (25000,), 0, 50000, jnp.int32)
        _o = jnp.argsort(dst, stable=True)
        src = src[_o]
        dst = dst[_o]
        return (x, src, dst)
    x, src, dst = _rec_inputs()

    def _L0_gnn_setup():
        import jax, jax.numpy as jnp
        import numpy as np
        from jax.ops import segment_sum
        N_NODES = 50000
        N_EDGES = 12500
        IN_DIM, HID_DIM, OUT_DIM = (128, 256, 128)

        def _glorot(key, shape):
            lim = np.sqrt(6.0 / (shape[0] + shape[1]))
            return jax.random.uniform(key, shape, jnp.float32, -lim, lim)

        def gcn_conv(x, W, b, src, dst, n_nodes):
            h = x @ W
            deg = segment_sum(jnp.ones_like(src, dtype=h.dtype), dst, num_segments=n_nodes) + 1.0
            dinv = jax.lax.rsqrt(deg)
            norm = dinv[src] * dinv[dst]
            msg = h[src] * norm[:, None]
            agg = segment_sum(msg, dst, num_segments=n_nodes)
            agg = agg + h * (dinv * dinv)[:, None]
            return agg + b
        key = jax.random.key(seed)
        ks = jax.random.split(key, 4)
        x = jax.random.normal(ks[0], (N_NODES, IN_DIM), jnp.float32)
        edge_index = jax.random.randint(ks[1], (2, N_EDGES), 0, N_NODES, jnp.int64)
        W1 = _glorot(ks[2], (IN_DIM, HID_DIM))
        b1 = jnp.zeros((HID_DIM,), jnp.float32)
        W2 = _glorot(ks[3], (HID_DIM, OUT_DIM))
        b2 = jnp.zeros((OUT_DIM,), jnp.float32)
        return {'x': x, 'edge_index': edge_index, 'W1': W1, 'b1': b1, 'W2': W2, 'b2': b2}
    _L0_gnn_all = _L0_gnn_setup()
    _L0_gnn_in = {k: v for k, v in _L0_gnn_all.items() if k in ('W1', 'b1', 'W2', 'b2')}
    del _L0_gnn_all

    def _L1_gnn_setup():
        import jax, jax.numpy as jnp
        import numpy as np
        N_NODES = 50000
        N_EDGES = 12500
        DIM = 128
        BN_EPS = 1e-05
        key = jax.random.key(seed)
        ks = jax.random.split(key, 12)
        d = DIM
        s = 1.0 / np.sqrt(d)
        x = jax.random.normal(ks[0], (N_NODES, d), dtype=jnp.float32)
        edge_index = jax.random.randint(ks[1], (2, N_EDGES), 0, N_NODES, dtype=jnp.int64)
        W_msg = jax.random.uniform(ks[2], (d, d), jnp.float32, -s, s)
        b_msg = jax.random.uniform(ks[3], (d,), jnp.float32, -s, s)
        sa = 1.0 / np.sqrt(2 * d)
        W_att = jax.random.uniform(ks[4], (2 * d, 1), jnp.float32, -sa, sa)
        b_att = jax.random.uniform(ks[5], (1,), jnp.float32, -sa, sa)
        W_ih = jax.random.uniform(ks[6], (3 * d, d), jnp.float32, -s, s)
        b_ih = jax.random.uniform(ks[7], (3 * d,), jnp.float32, -s, s)
        W_hh = jax.random.uniform(ks[8], (3 * d, d), jnp.float32, -s, s)
        b_hh = jax.random.uniform(ks[9], (3 * d,), jnp.float32, -s, s)
        gamma = jnp.ones((d,), jnp.float32)
        beta = jnp.zeros((d,), jnp.float32)
        return {'x': x, 'edge_index': edge_index, 'W_msg': W_msg, 'b_msg': b_msg, 'W_att': W_att, 'b_att': b_att, 'W_ih': W_ih, 'b_ih': b_ih, 'W_hh': W_hh, 'b_hh': b_hh, 'gamma': gamma, 'beta': beta}
    _L1_gnn_all = _L1_gnn_setup()
    _L1_gnn_in = {k: v for k, v in _L1_gnn_all.items() if k in ('W_msg', 'b_msg', 'W_att', 'b_att', 'W_ih', 'b_ih', 'W_hh', 'b_hh', 'gamma', 'beta')}
    del _L1_gnn_all
    return {'x': x, 'src': src, 'dst': dst, 'L0_gnn_W1': _L0_gnn_in['W1'], 'L0_gnn_b1': _L0_gnn_in['b1'], 'L0_gnn_W2': _L0_gnn_in['W2'], 'L0_gnn_b2': _L0_gnn_in['b2'], 'L1_gnn_W_msg': _L1_gnn_in['W_msg'], 'L1_gnn_b_msg': _L1_gnn_in['b_msg'], 'L1_gnn_W_att': _L1_gnn_in['W_att'], 'L1_gnn_b_att': _L1_gnn_in['b_att'], 'L1_gnn_W_ih': _L1_gnn_in['W_ih'], 'L1_gnn_b_ih': _L1_gnn_in['b_ih'], 'L1_gnn_W_hh': _L1_gnn_in['W_hh'], 'L1_gnn_b_hh': _L1_gnn_in['b_hh'], 'L1_gnn_gamma': _L1_gnn_in['gamma'], 'L1_gnn_beta': _L1_gnn_in['beta']}

def reference(x, src, dst, L0_gnn_W1, L0_gnn_b1, L0_gnn_W2, L0_gnn_b2, L1_gnn_W_msg, L1_gnn_b_msg, L1_gnn_W_att, L1_gnn_b_att, L1_gnn_W_ih, L1_gnn_b_ih, L1_gnn_W_hh, L1_gnn_b_hh, L1_gnn_gamma, L1_gnn_beta):
    import jax
    import jax.numpy as jnp

    def _L0_gnn_ref(x, edge_index, W1, b1, W2, b2):
        import jax, jax.numpy as jnp
        import numpy as np
        from jax.ops import segment_sum
        N_NODES = 50000
        N_EDGES = 12500
        IN_DIM, HID_DIM, OUT_DIM = (128, 256, 128)

        def _glorot(key, shape):
            lim = np.sqrt(6.0 / (shape[0] + shape[1]))
            return jax.random.uniform(key, shape, jnp.float32, -lim, lim)

        def gcn_conv(x, W, b, src, dst, n_nodes):
            h = x @ W
            deg = segment_sum(jnp.ones_like(src, dtype=h.dtype), dst, num_segments=n_nodes) + 1.0
            dinv = jax.lax.rsqrt(deg)
            norm = dinv[src] * dinv[dst]
            msg = h[src] * norm[:, None]
            agg = segment_sum(msg, dst, num_segments=n_nodes)
            agg = agg + h * (dinv * dinv)[:, None]
            return agg + b
        src, dst = (edge_index[0], edge_index[1])
        h = gcn_conv(x, W1, b1, src, dst, N_NODES)
        h = jax.nn.relu(h)
        out = gcn_conv(h, W2, b2, src, dst, N_NODES)
        return out

    def _L1_gnn_ref(x, edge_index, W_msg, b_msg, W_att, b_att, W_ih, b_ih, W_hh, b_hh, gamma, beta):
        import jax, jax.numpy as jnp
        import numpy as np
        N_NODES = 50000
        N_EDGES = 12500
        DIM = 128
        BN_EPS = 1e-05
        num_nodes, d = x.shape
        src = edge_index[0]
        dst = edge_index[1]
        xs = x[src]
        xd = x[dst]
        att = jax.nn.sigmoid(xs @ W_att[:d] + xd @ W_att[d:] + b_att)
        messages = (xs @ W_msg + b_msg) * att
        aggregated = jax.ops.segment_sum(messages, dst, num_segments=num_nodes)
        gi = aggregated @ W_ih.T + b_ih
        gh = x @ W_hh.T + b_hh
        i_r, i_z, i_n = jnp.split(gi, 3, axis=1)
        h_r, h_z, h_n = jnp.split(gh, 3, axis=1)
        r = jax.nn.sigmoid(i_r + h_r)
        z = jax.nn.sigmoid(i_z + h_z)
        n = jnp.tanh(i_n + r * h_n)
        h_new = (1.0 - z) * n + z * x
        mean = jnp.mean(h_new, axis=0)
        var = jnp.var(h_new, axis=0)
        return gamma * (h_new - mean) * jax.lax.rsqrt(var + BN_EPS) + beta
    edge_index = jnp.stack([src, dst])
    x = _layernorm(x + _L0_gnn_ref(x, edge_index, L0_gnn_W1, L0_gnn_b1, L0_gnn_W2, L0_gnn_b2), axis=-1)
    x = _layernorm(x + _L1_gnn_ref(x, edge_index, L1_gnn_W_msg, L1_gnn_b_msg, L1_gnn_W_att, L1_gnn_b_att, L1_gnn_W_ih, L1_gnn_b_ih, L1_gnn_W_hh, L1_gnn_b_hh, L1_gnn_gamma, L1_gnn_beta), axis=-1)
    return x

_drawn_inputs = setup_inputs


def setup_inputs(seed=0):
    import zlib

    import numpy as np

    out = dict(_drawn_inputs(seed))
    spreads = {'L0_gnn_b1': (0.0, 0.1),
     'L0_gnn_b2': (0.0, 0.1),
     'L1_gnn_gamma': (1.0, 0.2),
     'L1_gnn_beta': (0.0, 0.1)}
    factors = {'L1_gnn_b_msg': 8.0, 'L1_gnn_W_att': 3.107, 'L1_gnn_b_ih': 5.182, 'L1_gnn_b_hh': 6.134}
    for name, (base, spread) in spreads.items():
        noise = np.random.default_rng([zlib.crc32(name.encode()), seed]).standard_normal(out[name].shape)
        drawn = base * np.exp(spread * noise) if base else spread * noise
        out[name] = jnp.asarray(drawn.astype(out[name].dtype))
    for name, factor in factors.items():
        out[name] = (out[name] * factor).astype(out[name].dtype)
    return out
```

```python
from contextlib import ExitStack

import concourse.bass as bass
import numpy as np
from concourse import mybir

N = 50000
E = 25000
D = 128
P = 128
J = 4
GN = J * P
NG = -(-N // GN)
NP = NG * GN
NT = NG * J
TAIL = N - (NG - 1) * GN
ET = -(-E // P)
EP = ET * P
EL = EP + P
QC = 4
QT = NT // QC
DM = D + 2
PAD_DST = 65535
SKIP = 1 << 20
SURE = 1e30
LN_EPS = 1e-5
BN_EPS = 1e-5

ALU = mybir.AluOpType
ACT = mybir.ActivationFunctionType
AX_X = mybir.AxisListType.X
F32 = mybir.dt.float32
I32 = mybir.dt.int32
F16 = mybir.dt.float16
BF16 = mybir.dt.bfloat16


class Group:

    def __init__(self, i, c):
        self.i, self.c, self.slot = i, c, c % 2
        self.index = i * 2 + c
        self.fixed = isinstance(i, int)

    def done(self):
        return self.i * 2 + (self.c + 1)

    def freed(self):
        return self.i * 2 + (self.c - 1)

    def dma(self, n=1):
        return self.i * (16 * n) + (self.c // 2 + 1) * 16 * n

    def dma_freed(self, n=1):
        return self.i * (16 * n) + (self.c // 2) * 16 * n


def wait(eng, sem, value):
    if isinstance(value, int) and value <= 0:
        return
    eng.wait_ge(sem, value)


def in_register(eng, value):
    return value if isinstance(value, int) else eng.to_reg(value)


def run_pass(eng, step, lag):
    def at(i, u):
        def group_of(stage_lag):
            g = Group(i, u - stage_lag)
            return None if g.fixed and not 0 <= g.index < NG else g
        return group_of

    first = -(-(lag + 2) // 2)
    for i in range(first):
        for u in range(2):
            step(at(i, u))
    with eng.Fori(first, NG // 2) as i:
        for u in range(2):
            step(at(i, u))
    for i in range(NG // 2, NG // 2 + -(-lag // 2)):
        for u in range(2):
            step(at(i, u))


def build_gnn(nc, x, src, dst, w1, b1, w2, b2, wmsg, bmsg, watt, batt, wih, bih, whh, bhh, gamma, beta, out):
    ctx = ExitStack()
    with ctx:
        def sb(name, shape, dt=F32):
            return ctx.enter_context(nc.sbuf_tensor(name, shape, dt))

        def sem(name):
            return ctx.enter_context(nc.semaphore(name))

        def sems(name):
            return [sem(f"{name}{u}") for u in range(2)]

        XP = nc.dram_tensor("XP", [NG, P, J * D], F32).ap()
        G2 = nc.dram_tensor("G2", [NG, P, J * D], F32).ap()
        MT = nc.dram_tensor("MT", [NG, P, J * DM], F32).ap()
        SUM = nc.dram_tensor("SUM", [NG, P, J * D], F32).ap()
        SUMM = nc.dram_tensor("SUMM", [NG, P, J * DM], F32).ap()
        YT = nc.dram_tensor("YT", [NG, P, GN], F32).ap()
        HT = nc.dram_tensor("HT", [NG, P, GN], F32).ap()
        AD = nc.dram_tensor("AD", [NG, GN], F32).ap()
        xp_rows = XP.rearrange("g p (j d) -> (g p j) d", d=D)
        g2_rows = G2.rearrange("g p (j d) -> (g p j) d", d=D)
        mt_rows = MT.rearrange("g p (j d) -> (g p j) d", d=DM)
        sum_rows = SUM.rearrange("g p (j d) -> (g p j) d", d=D)
        summ_rows = SUMM.rearrange("g p (j d) -> (g p j) d", d=DM)

        def group_of_table(table, g):
            return table[bass.ds(g.index, 1)].rearrange("a p n -> (a p) n")

        bank = [ctx.enter_context(nc.psum_tensor(f"bank{b}", [P, 512], F32)) for b in range(8)]

        ident = sb("ident", [P, P])
        ones = sb("ones", [P, P])
        before = sb("before", [P, P])
        after = sb("after", [P, P])
        col_n = sb("col_n", [P, P])
        part_n = sb("part_n", [P, 1])
        tile_h = sb("tile_h", [P, NT], F16)
        tile_base = sb("tile_base", [P, NT])
        sum_row = sb("sum_row", [P, NT])
        w1_sb = sb("w1_sb", [P, 2 * P])
        w2_sb = sb("w2_sb", [P, 2, D])
        wm_sb = sb("wm_sb", [P, DM])
        wih_sb = sb("wih_sb", [P, 3 * D])
        whh_sb = sb("whh_sb", [P, 3 * D])
        b1_sb = sb("b1_sb", [P, 2])
        bih_sb = sb("bih_sb", [P, 3])
        bhh_sb = sb("bhh_sb", [P, 3])
        brz_sb = sb("brz_sb", [P, 2])
        gb_sb = sb("gb_sb", [P, 2])
        batt_sb = sb("batt_sb", [P, 1])
        b2_row = sb("b2_row", [P, D])
        bm_row = sb("bm_row", [P, DM])
        eps_sb = sb("eps_sb", [P, 2])

        ROWI = sb("ROWI", [P, NT], I32)
        LOC = sb("LOC", [P, NT])
        DINV = sb("DINV", [P, NT])
        slow = sb("slow", [P, 1])
        fast = sb("fast", [P, 1])
        slow_i = sb("slow_i", [P, 1], I32)

        dst_e = sb("dst_e", [P, ET], I32)
        src_e = sb("src_e", [P, ET], I32)
        hi_i = sb("hi_i", [P, ET], I32)
        lo_i = sb("lo_i", [P, ET], I32)
        hi_f = sb("hi_f", [P, ET])
        lo_f = sb("lo_f", [P, ET])
        oh_hi = sb("oh_hi", [P, 4, NT], BF16)
        oh_lo = sb("oh_lo", [P, 4, P], BF16)
        cnt = sb("cnt", [P, NT])
        deg = sb("deg", [P, NT])
        root = sb("root", [P, NT])
        t_a = sb("t_a", [P, NT])
        t_b = sb("t_b", [P, NT])
        tile_cnt = sb("tile_cnt", [P, QC])
        start_i = sb("start_i", [P, QC], I32)
        win_src = sb("win_src", [P, QC, P], I32)
        win_dst = sb("win_dst", [P, QC, P], I32)
        win_t = sb("win_t", [P, QC, P], I32)
        win_u = sb("win_u", [P, QC, P], I32)
        win_sf = sb("win_sf", [P, QC, P])
        win_df = sb("win_df", [P, QC, P])
        held = sb("held", [P, 1])

        zeros = sb("zeros", [P, J * DM])
        e_src = sb("e_src", [P, ET], I32)
        e_dst = sb("e_dst", [P, ET], I32)
        e_dstf = sb("e_dstf", [P, ET])
        e_rowf = sb("e_rowf", [P, ET])
        one_src = sb("one_src", [P, 1], I32)
        one_tab = sb("one_tab", [P, 1], I32)
        one_out = sb("one_out", [P, 1], I32)
        one_f = sb("one_f", [P, 2])
        e_col = sb("e_col", [P, P])
        e_same = sb("e_same", [P, P])
        e_junk = sb("e_junk", [P, P])
        e_msg = sb("e_msg", [P, DM])
        e_tgt = sb("e_tgt", [P, DM])
        e_sum = sb("e_sum", [P, DM])
        e_new = sb("e_new", [P, DM])
        e_att = sb("e_att", [P, 2])

        def two(name, shape, dt=F32):
            return [sb(f"{name}{u}", shape, dt) for u in range(2)]

        rowi = two("rowi", [P, J], I32)
        gath = two("gath", [P, J, D])
        gathm = two("gathm", [P, J, DM])
        onehot = two("onehot", [P, J, P])
        s_x = two("s_x", [P, J * D])
        s_o = two("s_o", [P, J * D])
        a_x = two("a_x", [P, J * D])
        a_v = two("a_v", [P, J * D])
        a_s = two("a_s", [P, J * D])
        a_T = two("a_T", [P, GN])
        a_h = two("a_h", [P, 2, GN])
        a_g = two("a_g", [P, J * D])
        a_d = two("a_d", [P, J])
        a_e = two("a_e", [P, J])
        n_x = two("n_x", [P, J * D])
        n_g = two("n_g", [P, J * D])
        n_b = two("n_b", [P, J * D])
        n_z = two("n_z", [P, J, D])
        n_y = two("n_y", [P, J, D])
        n_T = two("n_T", [P, GN])
        n_m = two("n_m", [P, J * DM])
        n_r = two("n_r", [1, GN])
        n_d = two("n_d", [P, J])
        st6 = two("st6", [P, J, 6])
        st_s = two("st_s", [P, J])
        st_d = two("st_d", [P, J])
        st_v = two("st_v", [P, J])
        st_q = two("st_q", [P, J])
        st_r = two("st_r", [P, J])
        st_m = two("st_m", [P, J])
        c_y = two("c_y", [P, GN])
        c_ad = two("c_ad", [P, GN])
        c_loc = two("c_loc", [P, J])
        c_junk = sb("c_junk", [P, J, P])
        c_la = two("c_la", [P, J])
        c_l = two("c_l", [P, J])
        c_att = two("c_att", [P, J])
        c_a = two("c_a", [P, GN])
        c_r = two("c_r", [P, GN])
        c_z = two("c_z", [P, GN])
        c_t = two("c_t", [P, GN])
        c_n = two("c_n", [P, GN])
        c_u = two("c_u", [P, GN])
        c_h = two("c_h", [P, GN])
        c_sq = sb("c_sq", [P, GN])
        hsum = sb("hsum", [P, NG])
        hsq = sb("hsq", [P, NG])
        bn = sb("bn", [P, 8])
        o_h = two("o_h", [P, GN])
        o_y = two("o_y", [P, GN])

        loaded = sem("loaded")
        w_loaded = sem("w_loaded")
        consts = sem("consts")
        zeroed = sem("zeroed")
        oh_ready = sem("oh_ready")
        oh_used = sem("oh_used")
        deg_plus = sem("deg_plus")
        rooted = sem("rooted")
        cnt_copied = sem("cnt_copied")
        tile_cnts = sem("tile_cnts")
        tile_cnts_sb = sem("tile_cnts_sb")
        starts = sem("starts")
        starts_sb = sem("starts_sb")
        windows = sem("windows")
        windows_f = sem("windows_f")
        windows_T = sem("windows_T")
        held_rows = sem("held_rows")
        held_sum = sem("held_sum")
        ready = sem("ready")
        dchain = sem("dchain")

        block = ctx.enter_context(nc.Block())

        gen = {k: sem("q_" + k) for k in "clear idx colT rows rows2 msg same prod att attd new out place total".split()}

        s_in, s_st = sems("s_in"), sems("s_st")
        s_done, s_half = sem("s_done"), sem("s_half")
        a_in, a_ga, a_store = sems("a_in"), sems("a_ga"), sems("a_store")
        a_idx, a_oh, a_agg, a_sum, a_scaled, a_tr, a_trc, a_hid, a_relu, a_out, a_outc, a_dd = (
            sem("a_" + k) for k in "idx oh agg sum scaled tr trc hid relu out outc dd".split())
        n_inx, n_ing, n_ga = sems("n_inx"), sems("n_ing"), sems("n_ga")
        n_st = sems("n_st")
        n_idx, n_oh, n_agg, n_xb, n_zz, n_s6, n_sd, n_var, n_root, n_rs, n_yy, n_tr, n_trc, n_mm, n_mc, n_rc, n_dd, n_dq = (
            sem("n_" + k) for k in "idx oh agg xb zz s6 sd var root rs yy tr trc mm mc rc dd dq".split())
        c_iny, c_ina, c_ga, c_st = sems("c_iny"), sems("c_ina"), sems("c_ga"), sems("c_st")
        c_idx, c_dd, c_la_s, c_l_s, c_at, c_oh, c_agg, c_aT, c_pr, c_pz, c_ph, c_pi, c_rs, c_zs, c_t1, c_t2, c_ns, c_d, c_zd, c_hh, c_sqs = (
            sem("c_" + k) for k in "idx dd las ls at oh agg aT pr pz ph pi rs zs t1 t2 ns d zd hh sqs".split())
        bn_v, bn_r, bn_ok = sem("bn_v"), sem("bn_r"), sem("bn_ok")
        o_inh, o_iny, o_st = sems("o_inh"), sems("o_iny"), sems("o_st")
        o_b, o_q, o_tr, o_s6, o_sd, o_dq, o_var, o_root, o_rs, o_oo = (sem("o_" + k) for k in "b q tr s6 sd dq var root rs oo".split())

        W_LOADS = 15
        CONSTS = 9
        CLEARS = 6

        def general_clear(sp, n, table, width):
            flag = sp.value_load(slow_i[0:1, 0:1], min_val=0, max_val=1)
            with sp.If(flag > 0):
                with sp.Fori(0, NG) as g:
                    sp.dma_start(table[bass.ds(g, 1)].rearrange("a p n -> (a p) n"), zeros[:, 0:J * width])\
                      .then_inc(gen["clear"], 16)

        def general_pool(pool, n, rows, sums, width):
            q = gen
            flag = pool.value_load(slow_i[0:1, 0:1], min_val=0, max_val=1)
            with pool.If(flag > 0):
                pool.wait_ge(q["clear"], 16 * NG * (n + 1))
                last_row = pool.to_reg(NP - 1)
                with pool.Fori(0, ET) as t:
                    tiles = in_register(pool, t + (n * ET + 1))
                    pool.wait_ge(ready, 1)
                    pool.wait_ge(q["idx"], tiles)
                    pool.indirect_dma_start(e_msg[:, 0:width], None, rows, bass.IndirectOffsetOnAxis(ap=one_src[:, 0:1], axis=0),
                                            bounds_check=last_row, oob_is_err=False).then_inc(q["rows"], 16)
                    pool.indirect_dma_start(e_sum[:, 0:width], None, sums, bass.IndirectOffsetOnAxis(ap=one_tab[:, 0:1], axis=0),
                                            bounds_check=last_row, oob_is_err=False).then_inc(q["rows2"], 16)
                    if n == 2:
                        pool.indirect_dma_start(e_tgt[:, 0:width], None, rows, bass.IndirectOffsetOnAxis(ap=one_tab[:, 0:1], axis=0),
                                                bounds_check=last_row, oob_is_err=False).then_inc(q["attd"], 16)
                    pool.wait_ge(ready, 1)
                    pool.wait_ge(q["new"], tiles)
                    pool.indirect_dma_start(sums, bass.IndirectOffsetOnAxis(ap=one_out[:, 0:1], axis=0), e_new[:, 0:width], None,
                                            bounds_check=last_row, oob_is_err=False).then_inc(q["out"], 16)
                pool.wait_ge(q["out"], 16 * ET * (n + 1))

        def general_act(act, n):
            flag = act.value_load(slow_i[0:1, 0:1], min_val=0, max_val=1)
            with act.If(flag > 0):
                q = gen
                with act.Fori(0, ET) as t:
                    act.wait_ge(q["msg"], t + 1)
                    nc.scalar.activation(e_att[:, 1:2], e_att[:, 0:1], ACT.Sigmoid, bias=batt_sb[:, 0:1]).then_inc(q["att"], 1)

        def general_tensor(pe, n, width):
            flag = pe.value_load(slow_i[0:1, 0:1], min_val=0, max_val=1)
            q = gen
            with pe.If(flag > 0):
                with pe.Fori(0, ET) as t:
                    pe.wait_ge(q["idx"], t + (n * ET + 1))
                    nc.tensor.transpose(bank[5][:, 0:P], e_col[:], ident[:]).then_inc(q["colT"], 1)
                    pe.wait_ge(q["same"], t + (n * ET + 1))
                    nc.tensor.matmul(bank[6][:, 0:width], e_same[:], e_msg[:, 0:width], start=True, stop=True).then_inc(q["prod"], 1)

        def general_vector(dve, n, width, link):
            flag = dve.value_load(slow_i[0:1, 0:1], min_val=0, max_val=1)
            q = gen
            with dve.If(flag > 0):
                with dve.Fori(0, ET) as t:
                    nc.vector.tensor_copy(one_src[:], e_src[:, bass.ds(t, 1)])
                    nc.vector.tensor_copy(one_tab[:], e_dst[:, bass.ds(t, 1)])
                    nc.vector.tensor_copy(one_f[:, 0:1], e_dstf[:, bass.ds(t, 1)])
                    nc.vector.tensor_scalar(e_col[:], ones[:], e_dstf[:, bass.ds(t, 1)], None, ALU.mult).then_inc(q["idx"], 1)
                    dve.wait_ge(q["colT"], t + (n * ET + 1))
                    dve.wait_ge(q["idx"], t + (n * ET + 1))
                    nc.vector.tensor_scalar(e_same[:], bank[5][:, 0:P], one_f[:, 0:1], None, ALU.is_equal).then_inc(q["place"], 1)
                    dve.wait_ge(q["place"], t * 3 + (3 * n * ET + 1))
                    nc.vector.tensor_tensor_reduce(e_junk[:], e_same[:], after[:], 1.0, 0.0, ALU.mult, ALU.add, one_f[:, 1:2]).then_inc(q["place"], 1)
                    dve.wait_ge(q["place"], t * 3 + (3 * n * ET + 2))
                    nc.vector.scalar_tensor_tensor(one_out[:], one_f[:, 1:2], float(SKIP), e_rowf[:, bass.ds(t, 1)], ALU.mult, ALU.add)\
                      .then_inc(q["place"], 1)
                    dve.wait_ge(q["rows"], t * 16 + (16 * n * ET + 16))
                    dve.wait_ge(q["rows2"], t * 16 + (16 * n * ET + 16))
                    if n == 2:
                        dve.wait_ge(q["attd"], t * 16 + 16)
                        nc.vector.tensor_tensor(e_att[:, 0:1], e_msg[:, D:D + 1], e_tgt[:, D + 1:DM], ALU.add).then_inc(q["msg"], 1)
                        dve.wait_ge(q["msg"], t + 1)
                        dve.wait_ge(q["att"], t + 1)
                        nc.vector.tensor_scalar(e_msg[:, 0:width], e_msg[:, 0:width], e_att[:, 1:2], None, ALU.mult).then_inc(q["same"], 1)
                    else:
                        dve.wait_ge(q["place"], t * 3 + (3 * n * ET + 3))
                        nc.vector.tensor_copy(one_f[:, 1:2], one_f[:, 0:1]).then_inc(q["same"], 1)
                    dve.wait_ge(q["prod"], t + (n * ET + 1))
                    nc.vector.tensor_tensor(e_new[:, 0:width], e_sum[:, 0:width], bank[6][:, 0:width], ALU.add).then_inc(q["total"], 1)
                    dve.wait_ge(q["total"], t + (n * ET + 1))
                    if n == 2:
                        nc.vector.memset(e_new[:, D:D + 1], SURE).then_inc(q["new"], 1)
                    else:
                        nc.vector.memset(one_f[:, 1:2], 0.0).then_inc(q["new"], 1)
                    dve.wait_ge(q["out"], t * 16 + (16 * n * ET + 16))

        @block.sync
        def _(sp):
            sp.dma_start(dst_e[:], dst[0:EP].rearrange("(p k) -> p k", p=P)).then_inc(loaded, 16)
            sp.dma_start(src_e[:], src[0:EP].rearrange("(p k) -> p k", p=P)).then_inc(loaded, 16)
            for t, a in ((w1_sb, w1), (wih_sb, wih), (whh_sb, whh), (b1_sb, b1), (bih_sb, bih), (bhh_sb, bhh)):
                sp.dma_start(t[:], a).then_inc(w_loaded, 16)
            sp.dma_start(w2_sb[:], w2.rearrange("(k p) o -> p k o", k=2)).then_inc(w_loaded, 16)
            sp.dma_start(wm_sb[:, 0:D], wmsg).then_inc(w_loaded, 16)
            sp.dma_start(wm_sb[:, D:D + 1], watt[0:D]).then_inc(w_loaded, 16)
            sp.dma_start(wm_sb[:, D + 1:DM], watt[D:2 * D]).then_inc(w_loaded, 16)
            sp.dma_start(gb_sb[:, 0:1], gamma).then_inc(w_loaded, 16)
            sp.dma_start(gb_sb[:, 1:2], beta).then_inc(w_loaded, 16)
            sp.dma_start(batt_sb[:], batt.partition_broadcast(P)).then_inc(w_loaded, 16)
            sp.dma_start(b2_row[:], b2.partition_broadcast(P)).then_inc(w_loaded, 16)
            sp.wait_ge(zeroed, CLEARS)
            sp.dma_start(bm_row[:, 0:D], bmsg.partition_broadcast(P)).then_inc(w_loaded, 16)

            def scale(group_of):
                if g := group_of(0):
                    wait(sp, s_done, g.freed())
                    wait(sp, s_half, g.freed())
                    sp.dma_start(s_x[g.slot][:], group_of_table(x, g)).then_inc(s_in[g.slot], 16)
                if g := group_of(2):
                    wait(sp, s_done, g.done())
                    wait(sp, s_half, g.done())
                    sp.dma_start(group_of_table(XP, g), s_o[g.slot][:]).then_inc(s_st[g.slot], 16)

            run_pass(sp, scale, 2)
            for u in range(2):
                sp.wait_ge(s_st[u], 16 * NG // 2)
            sp.wait_ge(ready, 1)
            general_clear(sp, 0, SUM, D)

            def conv(group_of):
                if g := group_of(0):
                    wait(sp, a_sum, g.freed())
                    sp.dma_start(a_x[g.slot][:], group_of_table(XP, g)).then_inc(a_in[g.slot], 16)
                if g := group_of(3):
                    wait(sp, a_outc, g.done())
                    sp.dma_start(group_of_table(G2, g), a_g[g.slot][:]).then_inc(a_store[g.slot], 16)

            run_pass(sp, conv, 3)
            for u in range(2):
                sp.wait_ge(a_store[u], 16 * NG // 2)
            general_clear(sp, 1, SUM, D)

            def norm(group_of):
                if g := group_of(0):
                    wait(sp, n_xb, g.freed())
                    sp.dma_start(n_x[g.slot][:], group_of_table(x, g)).then_inc(n_inx[g.slot], 16)
                    wait(sp, n_agg, g.freed())
                    sp.dma_start(n_g[g.slot][:], group_of_table(G2, g)).then_inc(n_ing[g.slot], 16)
                if g := group_of(4):
                    wait(sp, n_trc, g.done())
                    sp.dma_start(group_of_table(YT, g), n_T[g.slot][:]).then_inc(n_st[g.slot], 16)
                    wait(sp, n_rc, g.done())
                    sp.dma_start(AD[bass.ds(g.index, 1)], n_r[g.slot][:]).then_inc(n_st[g.slot], 16)
                    wait(sp, n_mc, g.done())
                    sp.dma_start(group_of_table(MT, g), n_m[g.slot][:]).then_inc(n_st[g.slot], 16)

            run_pass(sp, norm, 4)
            for u in range(2):
                sp.wait_ge(n_st[u], 48 * NG // 2)
            general_clear(sp, 2, SUMM, DM)

            def gru(group_of):
                if g := group_of(0):
                    wait(sp, c_la_s, g.freed())
                    sp.dma_start(c_ad[g.slot][:], AD[bass.ds(g.index, 1)].to_broadcast([P, GN])).then_inc(c_ina[g.slot], 16)
                if g := group_of(1):
                    wait(sp, c_d, g.freed())
                    wait(sp, c_pi, g.freed())
                    sp.dma_start(c_y[g.slot][:], group_of_table(YT, g)).then_inc(c_iny[g.slot], 16)
                if g := group_of(4):
                    wait(sp, c_hh, g.done())
                    sp.dma_start(group_of_table(HT, g), c_h[g.slot][:]).then_inc(c_st[g.slot], 16)

            run_pass(sp, gru, 4)
            for u in range(2):
                sp.wait_ge(c_st[u], 16 * NG // 2)

            def final(group_of):
                if g := group_of(0):
                    wait(sp, o_b, g.freed())
                    sp.dma_start(o_h[g.slot][:], group_of_table(HT, g)).then_inc(o_inh[g.slot], 16)
                    wait(sp, o_q, g.freed())
                    sp.dma_start(o_y[g.slot][:], group_of_table(YT, g)).then_inc(o_iny[g.slot], 16)
                if g := group_of(3):
                    wait(sp, o_oo, g.done())
                    sp.dma_start(group_of_table(out, g), n_y[g.slot][:].rearrange("p j d -> p (j d)")).then_inc(o_st[g.slot], 16)

            run_pass(sp, final, 3)
            for u in range(2):
                sp.wait_ge(o_st[u], 16 * NG // 2)

        @block.gpsimd
        def _(pool):
            exact = dict(allow_small_or_imprecise_dtypes=True)
            nc.gpsimd.iota(tile_h[:], [[1, NT]], base=0, channel_multiplier=0, **exact).then_inc(consts, 1)
            nc.gpsimd.iota(col_n[:], [[1, P]], base=0, channel_multiplier=0, **exact).then_inc(consts, 1)
            nc.gpsimd.iota(part_n[:], [[0, 1]], base=0, channel_multiplier=1, **exact).then_inc(consts, 1)
            nc.gpsimd.iota(tile_base[:], [[P, NT]], base=0, channel_multiplier=0, **exact).then_inc(consts, 1)
            nc.gpsimd.iota(sum_row[:], [[GN, NG], [1, J]], base=0, channel_multiplier=J, **exact).then_inc(consts, 1)
            nc.gpsimd.memset(ones[:], 1.0).then_inc(consts, 1)
            pool.wait_ge(consts, 6)
            for m, op, base, step in ((ident, ALU.is_equal, 0, -1), (before, ALU.is_gt, 0, 1)):
                nc.gpsimd.affine_select(out=m[:], in_=ones[:], compare_op=op, fill=0.0, base=base,
                                        pattern=[[step, P]], channel_multiplier=-step).then_inc(consts, 1)
            nc.gpsimd.affine_select(out=after[:], in_=ones[:], compare_op=ALU.is_gt, fill=0.0, base=0,
                                    pattern=[[-1, P]], channel_multiplier=1).then_inc(consts, 1)

            pool.wait_ge(starts_sb, 1)
            for arr, win in ((src, win_src), (dst, win_dst)):
                flat = arr.rearrange("(a b) -> a b", b=1)
                for c in range(QC):
                    nc.gpsimd.indirect_dma_start(win[0:QT, c, :], None, flat,
                                                 bass.IndirectOffsetOnAxis(ap=start_i[0:QT, c:c + 1], axis=0)).then_inc(windows, 16)

            def gathers(table, sum_table, buf, width, landed, agg_done):
                last_row = pool.to_reg(NP - 1)

                def step(group_of, rows):
                    g = group_of(0)
                    pool.wait_ge(ready, 1)
                    wait(pool, landed[g.slot], g.dma_freed(J))
                    nc.gpsimd.tensor_copy(rowi[g.slot][:], ROWI[:, bass.ds(g.index * J, J)]).then_inc(agg_done[1], 1)
                    copied, used = in_register(pool, g.done()), in_register(pool, g.freed())
                    pool.wait_ge(ready, 1)
                    wait(pool, agg_done[1], copied)
                    wait(pool, agg_done[0], used)
                    for j in range(J):
                        nc.gpsimd.indirect_dma_start(buf[g.slot][:, j, 0:width], None, rows,
                                                     bass.IndirectOffsetOnAxis(ap=rowi[g.slot][:, j:j + 1], axis=0),
                                                     bounds_check=last_row, oob_is_err=False).then_inc(landed[g.slot], 16)

                flag = pool.value_load(slow_i[0:1, 0:1], min_val=0, max_val=1)
                with pool.If(flag < 1):
                    run_pass(pool, lambda group_of: step(group_of, table), 0)
                with pool.If(flag > 0):
                    run_pass(pool, lambda group_of: step(group_of, sum_table), 0)
                for u in range(2):
                    pool.wait_ge(landed[u], 16 * J * NG // 2)

            pool.wait_ge(ready, 1)
            for u in range(2):
                pool.wait_ge(s_st[u], 16 * NG // 2)
            general_pool(pool, 0, xp_rows, sum_rows, D)
            gathers(xp_rows, sum_rows, gath, D, a_ga, (a_agg, a_idx))
            for u in range(2):
                pool.wait_ge(a_store[u], 16 * NG // 2)
            general_pool(pool, 1, g2_rows, sum_rows, D)
            pool.wait_ge(a_agg, NG)
            gathers(g2_rows, sum_rows, gath, D, n_ga, (n_agg, n_idx))
            for u in range(2):
                pool.wait_ge(n_st[u], 48 * NG // 2)
            general_pool(pool, 2, mt_rows, summ_rows, DM)
            gathers(mt_rows, summ_rows, gathm, DM, c_ga, (c_agg, c_idx))

        @block.scalar
        def _(act):
            act.wait_ge(w_loaded, 16 * W_LOADS)
            act.wait_ge(deg_plus, 1)
            nc.scalar.activation(root[:], deg[:], ACT.Sqrt).then_inc(rooted, 1)
            act.wait_ge(ready, 1)

            def scale(group_of):
                if g := group_of(0):
                    wait(act, s_in[g.slot], g.dma())
                    wait(act, s_st[g.slot], g.dma_freed())
                    wait(act, a_dd, g.done())
                    for j in (2, 3):
                        last = nc.scalar.activation(s_o[g.slot][:, j * D:(j + 1) * D], s_x[g.slot][:, j * D:(j + 1) * D],
                                                    ACT.Copy, scale=a_d[g.slot][:, j:j + 1])
                    last.then_inc(s_half, 1)

            run_pass(act, scale, 0)

            def conv(group_of):
                if g := group_of(1):
                    wait(act, a_tr, g.done())
                    wait(act, a_hid, g.freed())
                    nc.scalar.activation(a_T[g.slot][:], bank[2][:], ACT.Copy).then_inc(a_trc, 1)
                if g := group_of(0):
                    wait(act, a_sum, g.done())
                    wait(act, a_tr, g.freed())
                    for j in range(J):
                        last = nc.scalar.activation(a_s[g.slot][:, j * D:(j + 1) * D], a_v[g.slot][:, j * D:(j + 1) * D],
                                                    ACT.Copy, scale=a_e[g.slot][:, j:j + 1])
                    last.then_inc(a_scaled, 1)
                if g := group_of(1):
                    wait(act, a_out, g.freed())
                    wait(act, a_hid, g.done())
                    for k in range(2):
                        last = nc.scalar.activation(a_h[g.slot][:, k, :], bank[3 + k][:], ACT.Relu, bias=b1_sb[:, k:k + 1])
                    last.then_inc(a_relu, 1)

            run_pass(act, conv, 1)

            def norm(group_of):
                if g := group_of(1):
                    wait(act, n_var, g.done())
                    nc.scalar.activation(st_q[g.slot][:], st_v[g.slot][:], ACT.Sqrt, bias=eps_sb[:, 0:1], scale=1.0 / D).then_inc(n_root, 1)
                if g := group_of(2):
                    wait(act, n_tr, g.done())
                    wait(act, n_st[g.slot], g.dma_freed(3))
                    wait(act, n_mm, g.freed())
                    nc.scalar.activation(n_T[g.slot][:], bank[2 + g.slot][:], ACT.Copy).then_inc(n_trc, 1)
                if g := group_of(1):
                    wait(act, n_rs, g.done())
                    wait(act, n_tr, g.freed())
                    for j in range(J):
                        last = nc.scalar.activation(n_y[g.slot][:, j, :], n_z[g.slot][:, j, :], ACT.Identity,
                                                    bias=st_m[g.slot][:, j:j + 1], scale=st_r[g.slot][:, j:j + 1])
                    last.then_inc(n_yy, 1)
                if g := group_of(3):
                    wait(act, n_mm, g.done())
                    wait(act, n_st[g.slot], g.dma_freed(3))
                    nc.scalar.activation(n_r[g.slot][:], bank[6][0:1, :], ACT.Copy).then_inc(n_rc, 1)

            run_pass(act, norm, 3)
            general_act(act, 2)

            def gru(group_of):
                if g := group_of(3):
                    wait(act, c_hh, g.done())
                    wait(act, c_sqs, g.done() - 1)
                    n = TAIL if g.fixed and g.index == NG - 1 else GN
                    nc.scalar.activation(c_sq[:, 0:n], c_h[g.slot][:, 0:n], ACT.Square,
                                         accum_out=hsq[:, bass.ds(g.index, 1)]).then_inc(c_sqs, 1)
                if g := group_of(1):
                    wait(act, c_agg, g.done())
                    wait(act, c_pi, g.freed())
                    nc.scalar.activation(c_a[g.slot][:], bank[g.slot][:], ACT.Copy).then_inc(c_aT, 1)
                if g := group_of(0):
                    wait(act, c_l_s, g.done())
                    wait(act, c_oh, g.freed())
                    nc.scalar.activation(c_att[g.slot][:], c_l[g.slot][:], ACT.Sigmoid, bias=batt_sb[:, 0:1]).then_inc(c_at, 1)
                if g := group_of(2):
                    wait(act, c_pr, g.done())
                    wait(act, c_t1, g.freed())
                    nc.scalar.activation(c_r[g.slot][:], bank[2][:], ACT.Sigmoid, bias=brz_sb[:, 0:1]).then_inc(c_rs, 1)
                    wait(act, c_pz, g.done())
                    wait(act, c_zd, g.freed())
                    nc.scalar.activation(c_z[g.slot][:], bank[3][:], ACT.Sigmoid, bias=brz_sb[:, 1:2]).then_inc(c_zs, 1)
                    wait(act, c_t2, g.done())
                    wait(act, c_hh, g.freed())
                    nc.scalar.activation(c_n[g.slot][:], c_u[g.slot][:], ACT.Tanh, bias=bih_sb[:, 2:3]).then_inc(c_ns, 1)

            act.wait_ge(bn_ok, 1)
            run_pass(act, gru, 3)
            act.wait_ge(bn_v, 1)
            nc.scalar.activation(bn[:, 3:4], bn[:, 2:3], ACT.Sqrt, bias=eps_sb[:, 1:2]).then_inc(bn_r, 1)
            act.wait_ge(bn_ok, 2)

            def final(group_of):
                if g := group_of(0):
                    wait(act, o_inh[g.slot], g.dma())
                    wait(act, o_q, g.freed())
                    nc.scalar.activation(c_t[g.slot][:], o_h[g.slot][:], ACT.Identity, bias=bn[:, 6:7], scale=bn[:, 5:6]).then_inc(o_b, 1)
                if g := group_of(1):
                    wait(act, o_var, g.done())
                    nc.scalar.activation(st_q[g.slot][:], st_v[g.slot][:], ACT.Sqrt, bias=eps_sb[:, 0:1], scale=1.0 / D).then_inc(o_root, 1)
                if g := group_of(2):
                    wait(act, o_rs, g.done())
                    wait(act, o_st[g.slot], g.dma_freed())
                    for j in range(J):
                        last = nc.scalar.activation(n_y[g.slot][:, j, :], bank[g.slot][:, j * D:(j + 1) * D], ACT.Identity,
                                                    bias=st_m[g.slot][:, j:j + 1], scale=st_r[g.slot][:, j:j + 1])
                    last.then_inc(o_oo, 1)

            run_pass(act, final, 2)

        @block.vector
        def _(dve):
            count = [0]

            def link(ins):
                count[0] += 1
                ins.then_inc(dchain, 1)
                dve.wait_ge(dchain, count[0])

            for u in range(2):
                nc.vector.memset(gath[u][:], 0.0).then_inc(zeroed, 1)
                nc.vector.memset(gathm[u][:], 0.0).then_inc(zeroed, 1)
            nc.vector.memset(zeros[:], 0.0).then_inc(zeroed, 1)
            nc.vector.memset(bm_row[:, D:DM], 0.0).then_inc(zeroed, 1)
            nc.vector.memset(e_msg[:], 0.0)
            nc.vector.memset(e_sum[:], 0.0)
            nc.vector.memset(e_tgt[:], 0.0)
            nc.vector.memset(eps_sb[:, 0:1], LN_EPS)
            link(nc.vector.memset(eps_sb[:, 1:2], BN_EPS))
            dve.wait_ge(loaded, 32)
            nc.vector.tensor_scalar(hi_i[:], dst_e[:], 7, None, ALU.logical_shift_right)
            link(nc.vector.tensor_scalar(lo_i[:], dst_e[:], P - 1, None, ALU.bitwise_and))
            nc.vector.tensor_copy(hi_f[:], hi_i[:])
            link(nc.vector.tensor_copy(lo_f[:], lo_i[:]))
            dve.wait_ge(consts, CONSTS)

            def one_hots(i):
                for c in range(4):
                    wait(dve, oh_used, i * 4 + (c - 3))
                    nc.vector.tensor_scalar(oh_hi[:, c, :], tile_h[:], hi_f[:, bass.ds(i * 4 + c, 1)], None, ALU.is_equal)
                    nc.vector.tensor_scalar(oh_lo[:, c, :], tile_h[:, 0:P], lo_f[:, bass.ds(i * 4 + c, 1)], None, ALU.is_equal)\
                      .then_inc(oh_ready, 1)

            one_hots(0)
            with dve.Fori(1, ET // 4) as i:
                one_hots(i)
            dve.wait_ge(oh_used, ET)
            nc.vector.tensor_scalar(deg[:], bank[0][:, 0:NT], 1.0, None, ALU.add).then_inc(deg_plus, 1)
            nc.vector.tensor_copy(cnt[:], bank[0][:, 0:NT]).then_inc(cnt_copied, 1)
            dve.wait_ge(rooted, 1)
            dve.wait_ge(deg_plus, 1)
            link(nc.vector.reciprocal(DINV[:], root[:]))
            link(nc.vector.tensor_tensor(t_a[:], DINV[:], DINV[:], ALU.mult))
            link(nc.vector.tensor_tensor(t_b[:], t_a[:], deg[:], ALU.mult))
            link(nc.vector.tensor_scalar(t_a[:], t_b[:], -0.5, 1.5, ALU.mult, ALU.add))
            link(nc.vector.tensor_tensor(DINV[:], DINV[:], t_a[:], ALU.mult))
            dve.wait_ge(tile_cnts, 1)
            nc.vector.tensor_copy(tile_cnt[0:QT, :], bank[1][0:QT, 0:QC]).then_inc(tile_cnts_sb, 1)
            dve.wait_ge(starts, 1)
            nc.vector.tensor_copy(start_i[0:QT, :], bank[2][0:QT, 0:QC]).then_inc(starts_sb, 1)
            dve.wait_ge(windows, 16 * 2 * QC)
            q = slice(0, QT)

            def table_row(to, of, tmp):
                link(nc.vector.tensor_scalar(to, of, P - 1, 2, ALU.bitwise_and, ALU.logical_shift_left))
                link(nc.vector.tensor_scalar(tmp, of, 7, J - 1, ALU.logical_shift_right, ALU.bitwise_and))
                link(nc.vector.tensor_tensor(to, to, tmp, ALU.bitwise_or))
                link(nc.vector.tensor_scalar(tmp, of, 9, 9, ALU.logical_shift_right, ALU.logical_shift_left))
                link(nc.vector.tensor_tensor(to, to, tmp, ALU.bitwise_or))

            table_row(win_t[q], win_src[q], win_u[q])
            nc.vector.tensor_copy(win_sf[q], win_t[q])
            nc.vector.tensor_copy(win_df[q], win_dst[q]).then_inc(windows_f, 1)
            dve.wait_ge(windows_T, 1)
            link(nc.vector.tensor_tensor(LOC[:], bank[4][:, 0:NT], tile_base[:], ALU.subtract))
            link(nc.vector.tensor_scalar(t_a[:], LOC[:], 0.0, None, ALU.is_ge))
            link(nc.vector.scalar_tensor_tensor(t_b[:], LOC[:], float(P), t_a[:], ALU.is_lt, ALU.mult))
            nc.vector.tensor_reduce(held[:], t_b[:], AX_X, ALU.add).then_inc(held_rows, 1)
            link(nc.vector.scalar_tensor_tensor(t_a[:], t_b[:], -float(SKIP), bank[3][:, 0:NT], ALU.mult, ALU.add))
            link(nc.vector.tensor_scalar(t_a[:], t_a[:], float(SKIP), None, ALU.add))
            dve.wait_ge(held_sum, 1)
            nc.vector.tensor_scalar(slow[:], bank[5][:, 0:1], float(E), None, ALU.not_equal)
            nc.vector.tensor_scalar(slow_i[:], bank[5][:, 0:1], float(E), None, ALU.not_equal)
            link(nc.vector.tensor_scalar(fast[:], bank[5][:, 0:1], float(E), None, ALU.is_equal))
            link(nc.vector.tensor_scalar(t_b[:], sum_row[:], slow[:, 0:1], None, ALU.mult))
            link(nc.vector.scalar_tensor_tensor(ROWI[:], t_a[:], fast[:, 0:1], t_b[:], ALU.mult, ALU.add))
            link(nc.vector.tensor_scalar(held[:], part_n[:], slow[:, 0:1], None, ALU.mult))
            link(nc.vector.tensor_scalar(LOC[:], LOC[:], fast[:, 0:1], held[:, 0:1], ALU.mult, ALU.add))
            dve.wait_ge(w_loaded, 16 * W_LOADS)
            nc.vector.tensor_tensor(brz_sb[:], bih_sb[:, 0:2], bhh_sb[:, 0:2], ALU.add).then_inc(bn_ok, 1)
            table_row(e_src[:], src_e[:], hi_i[:])
            table_row(e_dst[:], dst_e[:], hi_i[:])
            nc.vector.tensor_copy(e_rowf[:], e_dst[:])
            link(nc.vector.tensor_copy(e_dstf[:], dst_e[:]))
            nc.vector.memset(held[:], 0.0).then_inc(ready, 1)

            def scale(group_of):
                if g := group_of(0):
                    wait(dve, s_half, g.freed())
                    wait(dve, s_done, g.freed())
                    nc.vector.tensor_copy(a_d[g.slot][:], DINV[:, bass.ds(g.index * J, J)]).then_inc(a_dd, 1)
                    wait(dve, s_in[g.slot], g.dma())
                    wait(dve, s_st[g.slot], g.dma_freed())
                    wait(dve, a_dd, g.done())
                    for j in (0, 1):
                        last = nc.vector.tensor_scalar(s_o[g.slot][:, j * D:(j + 1) * D], s_x[g.slot][:, j * D:(j + 1) * D],
                                                       a_d[g.slot][:, j:j + 1], None, ALU.mult)
                    last.then_inc(s_done, 1)

            run_pass(dve, scale, 0)
            general_vector(dve, 0, D, link)

            tile_of_slot = col_n[:].unsqueeze(1).to_broadcast([P, J, P])

            def one_hot(g, used, made):
                wait(dve, used, g.freed())
                nc.vector.tensor_tensor(onehot[g.slot][:], tile_of_slot,
                                        LOC[:, bass.ds(g.index * J, J)].unsqueeze(2).to_broadcast([P, J, P]),
                                        ALU.is_equal).then_inc(made, 1)

            def conv(group_of):
                if g := group_of(0):
                    one_hot(g, a_agg, a_oh)
                if g := group_of(1):
                    wait(dve, a_agg, g.done())
                    wait(dve, a_in[g.slot], g.dma())
                    wait(dve, a_scaled, g.freed())
                    nc.vector.tensor_copy(a_e[g.slot][:], DINV[:, bass.ds(g.index * J, J)])
                    nc.vector.tensor_tensor(a_v[g.slot][:], bank[g.slot][:], a_x[g.slot][:], ALU.add).then_inc(a_sum, 1)
                if g := group_of(3):
                    wait(dve, a_out, g.done())
                    wait(dve, a_store[g.slot], g.dma_freed())
                    nc.vector.tensor_tensor(a_g[g.slot][:].rearrange("p (j d) -> p j d", j=J),
                                            bank[5 + g.slot][:].rearrange("p (j d) -> p j d", j=J),
                                            DINV[:, bass.ds(g.index * J, J)].unsqueeze(2).to_broadcast([P, J, D]),
                                            ALU.mult).then_inc(a_outc, 1)

            run_pass(dve, conv, 3)
            general_vector(dve, 1, D, link)
            row_b2 = b2_row[:].unsqueeze(1).to_broadcast([P, J, D])

            def norm(group_of):
                if g := group_of(0):
                    one_hot(g, n_agg, n_oh)
                    wait(dve, n_inx[g.slot], g.dma())
                    wait(dve, n_zz, g.freed())
                    nc.vector.tensor_tensor(n_b[g.slot][:].rearrange("p (j d) -> p j d", j=J),
                                            n_x[g.slot][:].rearrange("p (j d) -> p j d", j=J), row_b2, ALU.add).then_inc(n_xb, 1)
                if g := group_of(1):
                    nc.vector.tensor_copy(n_d[g.slot][:], DINV[:, bass.ds(g.index * J, J)]).then_inc(n_dd, 1)
                    wait(dve, n_agg, g.done())
                    wait(dve, n_xb, g.done())
                    wait(dve, n_dd, g.done())
                    wait(dve, n_yy, g.freed())
                    for j in range(J):
                        last = nc.vector.scalar_tensor_tensor(n_z[g.slot][:, j, :], bank[g.slot][:, j * D:(j + 1) * D], n_d[g.slot][:, j:j + 1],
                                                              n_b[g.slot][:, j * D:(j + 1) * D], ALU.mult, ALU.add)
                    last.then_inc(n_zz, 1)
                    wait(dve, n_zz, g.done())
                    normaliser_a(g, lambda j: n_z[g.slot][:, j, :], n_s6, n_sd, n_dq, n_var)
                if g := group_of(3):
                    wait(dve, n_mm, g.done())
                    wait(dve, n_st[g.slot], g.dma_freed(3))
                    m = n_m[g.slot][:].rearrange("p (j d) -> p j d", j=J)
                    for h in range(2):
                        last = nc.vector.tensor_tensor(m[:, 2 * h:2 * h + 2, :],
                                                       bank[4 + h][:, 0:2 * DM].rearrange("p (j d) -> p j d", j=2),
                                                       bm_row[:].unsqueeze(1).to_broadcast([P, 2, DM]), ALU.add)
                    last.then_inc(n_mc, 1)
                if g := group_of(1):
                    normaliser_b(g, n_root, n_dq, n_rs)

            def normaliser_a(g, rows_of, s6, sd, dq, var):
                for j in range(J):
                    last = nc.vector.bn_stats(st6[g.slot][:, j, :], rows_of(j))
                last.then_inc(s6, 1)
                wait(dve, s6, g.done())
                part = [st6[g.slot][:, :, k:k + 1].rearrange("p j a -> p (j a)") for k in range(6)]
                nc.vector.tensor_tensor(st_s[g.slot][:], part[1], part[4], ALU.add)
                nc.vector.tensor_tensor(st_v[g.slot][:], part[2], part[5], ALU.add)
                nc.vector.tensor_tensor(st_d[g.slot][:], part[1], part[4], ALU.subtract).then_inc(sd, 1)
                wait(dve, sd, g.done())
                nc.vector.tensor_tensor(st_d[g.slot][:], st_d[g.slot][:], st_d[g.slot][:], ALU.mult).then_inc(dq, 1)
                wait(dve, dq, g.i * 4 + (2 * g.c + 1))
                nc.vector.scalar_tensor_tensor(st_v[g.slot][:], st_d[g.slot][:], D / 4.0, st_v[g.slot][:], ALU.mult, ALU.add).then_inc(var, 1)

            def normaliser_b(g, rooted_, dq, rs):
                wait(dve, rooted_, g.done())
                nc.vector.reciprocal(st_r[g.slot][:], st_q[g.slot][:]).then_inc(dq, 1)
                wait(dve, dq, g.i * 4 + (2 * g.c + 2))
                nc.vector.scalar_tensor_tensor(st_m[g.slot][:], st_s[g.slot][:], -0.5, st_r[g.slot][:], ALU.mult, ALU.mult).then_inc(rs, 1)

            run_pass(dve, norm, 3)
            general_vector(dve, 2, DM, link)

            def gru(group_of):
                if g := group_of(0):
                    wait(dve, c_oh, g.freed())
                    nc.vector.tensor_copy(c_loc[g.slot][:], LOC[:, bass.ds(g.index * J, J)]).then_inc(c_dd, 1)
                    wait(dve, c_ina[g.slot], g.dma())
                    wait(dve, c_dd, g.done())
                    wait(dve, c_la_s, g.done() - 1)
                    for j in range(J):
                        last = nc.vector.scalar_tensor_tensor(c_junk[:, j, :], col_n[:], c_loc[g.slot][:, j:j + 1],
                                                              c_ad[g.slot][:, j * P:(j + 1) * P], ALU.is_equal, ALU.mult,
                                                              accum_out=c_la[g.slot][:, j:j + 1])
                    last.then_inc(c_la_s, 1)
                    wait(dve, c_la_s, g.done())
                    wait(dve, c_ga[g.slot], g.dma(J))
                    wait(dve, c_at, g.freed())
                    nc.vector.tensor_tensor(c_l[g.slot][:], c_la[g.slot][:],
                                            gathm[g.slot][:, :, D:D + 1].rearrange("p j a -> p (j a)"), ALU.add).then_inc(c_l_s, 1)
                if g := group_of(2):
                    wait(dve, c_rs, g.done())
                    wait(dve, c_ph, g.done())
                    wait(dve, c_zd, g.freed())
                    nc.vector.scalar_tensor_tensor(c_t[g.slot][:], bank[4][:], bhh_sb[:, 2:3], c_r[g.slot][:], ALU.add, ALU.mult).then_inc(c_t1, 1)
                    wait(dve, c_t1, g.done())
                    wait(dve, c_pi, g.done())
                    wait(dve, c_hh, g.freed())
                    nc.vector.tensor_tensor(c_u[g.slot][:], c_t[g.slot][:], bank[5][:], ALU.add).then_inc(c_t2, 1)
                if g := group_of(0):
                    wait(dve, c_at, g.done())
                    wait(dve, c_agg, g.freed())
                    for j in range(J):
                        last = nc.vector.tensor_scalar(onehot[g.slot][:, j, :], col_n[:], c_loc[g.slot][:, j:j + 1],
                                                       c_att[g.slot][:, j:j + 1], ALU.is_equal, ALU.mult)
                    last.then_inc(c_oh, 1)
                if g := group_of(2):
                    wait(dve, c_ns, g.done())
                    wait(dve, c_t2, g.done())
                    nc.vector.tensor_tensor(c_t[g.slot][:], c_y[g.slot][:], c_n[g.slot][:], ALU.subtract).then_inc(c_d, 1)
                    wait(dve, c_d, g.done())
                    wait(dve, c_zs, g.done())
                    nc.vector.tensor_tensor(c_u[g.slot][:], c_t[g.slot][:], c_z[g.slot][:], ALU.mult).then_inc(c_zd, 1)
                    wait(dve, c_zd, g.done())
                    wait(dve, c_st[g.slot], g.dma_freed())
                    wait(dve, c_sqs, g.freed())
                    n = TAIL if g.fixed and g.index == NG - 1 else GN
                    if n < GN:
                        nc.vector.tensor_tensor(c_h[g.slot][:, n:GN], c_u[g.slot][:, n:GN], c_n[g.slot][:, n:GN], ALU.add)
                    nc.vector.scalar_tensor_tensor(c_h[g.slot][:, 0:n], c_u[g.slot][:, 0:n], 1.0, c_n[g.slot][:, 0:n], ALU.mult, ALU.add,
                                                   accum_out=hsum[:, bass.ds(g.index, 1)]).then_inc(c_hh, 1)

            run_pass(dve, gru, 2)
            dve.wait_ge(c_sqs, NG)
            dve.wait_ge(c_hh, NG)
            nc.vector.tensor_reduce(bn[:, 0:1], hsum[:], AX_X, ALU.add)
            link(nc.vector.tensor_reduce(bn[:, 1:2], hsq[:], AX_X, ALU.add))
            link(nc.vector.tensor_scalar(bn[:, 0:1], bn[:, 0:1], 1.0 / N, None, ALU.mult))
            link(nc.vector.tensor_tensor(bn[:, 4:5], bn[:, 0:1], bn[:, 0:1], ALU.mult))
            link(nc.vector.scalar_tensor_tensor(bn[:, 4:5], bn[:, 1:2], 1.0 / N, bn[:, 4:5], ALU.mult, ALU.subtract))
            nc.vector.tensor_scalar(bn[:, 2:3], bn[:, 4:5], 0.0, None, ALU.max).then_inc(bn_v, 1)
            dve.wait_ge(bn_r, 1)
            link(nc.vector.reciprocal(bn[:, 4:5], bn[:, 3:4]))
            link(nc.vector.tensor_tensor(bn[:, 5:6], gb_sb[:, 0:1], bn[:, 4:5], ALU.mult))
            link(nc.vector.tensor_tensor(bn[:, 7:8], bn[:, 5:6], bn[:, 0:1], ALU.mult))
            nc.vector.tensor_tensor(bn[:, 6:7], gb_sb[:, 1:2], bn[:, 7:8], ALU.subtract).then_inc(bn_ok, 1)

            def final(group_of):
                if g := group_of(0):
                    wait(dve, o_iny[g.slot], g.dma())
                    wait(dve, o_b, g.done())
                    wait(dve, o_tr, g.freed())
                    nc.vector.tensor_tensor(c_u[g.slot][:], c_t[g.slot][:], o_y[g.slot][:], ALU.add).then_inc(o_q, 1)
                if g := group_of(1):
                    wait(dve, o_tr, g.done())
                    wait(dve, o_oo, g.freed())
                    normaliser_a(g, lambda j: bank[g.slot][:, j * D:(j + 1) * D], o_s6, o_sd, o_dq, o_var)
                if g := group_of(1):
                    normaliser_b(g, o_root, o_dq, o_rs)

            run_pass(dve, final, 1)

        @block.tensor
        def _(pe):
            def count_edges(i, first, last):
                for c in range(4):
                    pe.wait_ge(oh_ready, i * 4 + (c + 1))
                    nc.tensor.matmul(bank[0][:, 0:NT], oh_lo[:, c, :], oh_hi[:, c, :], start=first and c == 0,
                                     stop=last and c == 3, skip_group_check=True).then_inc(oh_used, 1)

            count_edges(0, True, False)
            with pe.Fori(1, ET // 4 - 1) as i:
                count_edges(i, False, False)
            count_edges(ET // 4 - 1, False, True)
            pe.wait_ge(consts, CONSTS)
            pe.wait_ge(cnt_copied, 1)
            for c in range(QC):
                last = nc.tensor.matmul(bank[1][0:QT, c:c + 1], cnt[:, c * QT:(c + 1) * QT], ones[:, 0:1], start=True, stop=True)
            last.then_inc(tile_cnts, 1)
            pe.wait_ge(tile_cnts_sb, 1)
            for c in range(QC):
                for b in range(c):
                    nc.tensor.matmul(bank[2][0:QT, c:c + 1], ones[0:QT, 0:QT], tile_cnt[0:QT, b:b + 1], start=(b == 0), stop=False)
                last = nc.tensor.matmul(bank[2][0:QT, c:c + 1], before[0:QT, 0:QT], tile_cnt[0:QT, c:c + 1], start=(c == 0), stop=True)
            last.then_inc(starts, 1)
            pe.wait_ge(windows_f, 1)
            for win, b in ((win_sf, 3), (win_df, 4)):
                for c in range(QC):
                    last = nc.tensor.transpose(bank[b][:, c * QT:(c + 1) * QT], win[0:QT, c, :], ident[0:QT, 0:QT])
            last.then_inc(windows_T, 1)
            pe.wait_ge(held_rows, 1)
            nc.tensor.matmul(bank[5][:, 0:1], ones[:], held[:], start=True, stop=True).then_inc(held_sum, 1)
            pe.wait_ge(w_loaded, 16 * W_LOADS)
            pe.wait_ge(ready, 1)
            general_tensor(pe, 0, D)

            def sums(g, buf, made, landed, agg, own=None):
                wait(pe, made, g.done())
                wait(pe, landed[g.slot], g.dma(J))
                if own is not None:
                    nc.tensor.matmul(bank[g.slot][:], ident[:], own, start=True, stop=False, skip_group_check=True)
                for j in range(J):
                    last = nc.tensor.matmul(bank[g.slot][:, j * D:(j + 1) * D], onehot[g.slot][:, j, :], buf[g.slot][:, j, :],
                                            start=own is None, stop=True, skip_group_check=own is not None)
                last.then_inc(agg, 1)

            def conv(group_of):
                if g := group_of(0):
                    wait(pe, a_sum, g.freed())
                    sums(g, gath, a_oh, a_ga, a_agg)
                if g := group_of(1):
                    wait(pe, a_scaled, g.done())
                    wait(pe, a_trc, g.done() - 1)
                    for j in range(J):
                        last = nc.tensor.transpose(bank[2][:, j * P:(j + 1) * P], a_s[g.slot][:, j * D:(j + 1) * D], ident[:])
                    last.then_inc(a_tr, 1)
                if g := group_of(2):
                    wait(pe, a_relu, g.done())
                    wait(pe, a_outc, g.freed())
                    for j in range(J):
                        for k in range(2):
                            last = nc.tensor.matmul(bank[5 + g.slot][:, j * D:(j + 1) * D], a_h[g.slot][:, k, j * P:(j + 1) * P],
                                                    w2_sb[:, k, :], start=(k == 0), stop=(k == 1))
                    last.then_inc(a_out, 1)
                if g := group_of(1):
                    wait(pe, a_trc, g.done())
                    wait(pe, a_relu, g.done() - 1)
                    for k in range(2):
                        last = nc.tensor.matmul(bank[3 + k][:], w1_sb[:, k * P:(k + 1) * P], a_T[g.slot][:], start=True, stop=True)
                    last.then_inc(a_hid, 1)

            run_pass(pe, conv, 2)
            pe.wait_ge(a_outc, NG)
            general_tensor(pe, 1, D)

            def norm(group_of):
                if g := group_of(0):
                    wait(pe, n_ing[g.slot], g.dma())
                    wait(pe, n_zz, g.freed())
                    sums(g, gath, n_oh, n_ga, n_agg, own=n_g[g.slot][:])
                if g := group_of(3):
                    wait(pe, n_mc, g.done() - 1)
                    wait(pe, n_rc, g.done() - 1)
                    wait(pe, n_trc, g.done())
                    for j in range(J):
                        nc.tensor.matmul(bank[4 + j // 2][:, (j % 2) * DM:(j % 2 + 1) * DM], n_T[g.slot][:, j * P:(j + 1) * P], wm_sb[:],
                                         start=True, stop=True)
                    nc.tensor.matmul(bank[6][0:1, :], wm_sb[:, D + 1:DM], n_T[g.slot][:], start=True, stop=True).then_inc(n_mm, 1)
                if g := group_of(2):
                    wait(pe, n_yy, g.done())
                    wait(pe, n_trc, g.freed())
                    for j in range(J):
                        last = nc.tensor.transpose(bank[2 + g.slot][:, j * P:(j + 1) * P], n_y[g.slot][:, j, :], ident[:])
                    last.then_inc(n_tr, 1)

            run_pass(pe, norm, 3)
            pe.wait_ge(n_mc, NG)
            pe.wait_ge(n_rc, NG)
            general_tensor(pe, 2, DM)

            def gru(group_of):
                if g := group_of(1):
                    wait(pe, c_aT, g.freed())
                    wait(pe, c_oh, g.done())
                    for j in range(J):
                        last = nc.tensor.matmul(bank[g.slot][:, j * P:(j + 1) * P], gathm[g.slot][:, j, 0:D], onehot[g.slot][:, j, :],
                                                start=True, stop=True)
                    last.then_inc(c_agg, 1)
                if g := group_of(2):
                    y, a = c_y[g.slot][:], c_a[g.slot][:]
                    wait(pe, c_iny[g.slot], g.dma())
                    wait(pe, c_t1, g.done() - 1)
                    nc.tensor.matmul(bank[4][:], whh_sb[:, 2 * D:3 * D], y, start=True, stop=True).then_inc(c_ph, 1)
                    wait(pe, c_aT, g.done())
                    wait(pe, c_rs, g.done() - 1)
                    nc.tensor.matmul(bank[2][:], whh_sb[:, 0:D], y, start=True, stop=False)
                    nc.tensor.matmul(bank[2][:], wih_sb[:, 0:D], a, start=False, stop=True).then_inc(c_pr, 1)
                    wait(pe, c_t2, g.done() - 1)
                    nc.tensor.matmul(bank[5][:], wih_sb[:, 2 * D:3 * D], a, start=True, stop=True).then_inc(c_pi, 1)
                    wait(pe, c_zs, g.done() - 1)
                    nc.tensor.matmul(bank[3][:], whh_sb[:, D:2 * D], y, start=True, stop=False)
                    nc.tensor.matmul(bank[3][:], wih_sb[:, D:2 * D], a, start=False, stop=True).then_inc(c_pz, 1)

            run_pass(pe, gru, 2)
            pe.wait_ge(c_aT, NG)

            def final(group_of):
                if g := group_of(0):
                    wait(pe, o_q, g.done())
                    wait(pe, o_oo, g.freed())
                    for j in range(J):
                        last = nc.tensor.transpose(bank[g.slot][:, j * D:(j + 1) * D], c_u[g.slot][:, j * P:(j + 1) * P], ident[:])
                    last.then_inc(o_tr, 1)

            run_pass(pe, final, 0)


_INS = ["x", "src", "dst", "W1", "b1", "W2", "b2", "W_msg", "b_msg", "W_att", "b_att", "W_ih", "b_ih", "W_hh", "b_hh", "gamma", "beta"]


def kernel(**inputs):
    import concourse.bacc as bacc
    from concourse.bass_utils import run_bass_kernel_spmd

    a = {k.split("gnn_")[-1]: np.asarray(v) for k, v in inputs.items()}
    x = np.zeros((NP, D), a["x"].dtype)
    x[:N] = a["x"]
    x = np.ascontiguousarray(x.reshape(NG, J, P, D).transpose(0, 2, 1, 3)).reshape(NG, P, J * D)
    src, dst = np.zeros(EL, a["src"].dtype), np.full(EL, PAD_DST, a["dst"].dtype)
    src[:E], dst[:E] = a["src"], a["dst"]

    def columns(v):
        return np.ascontiguousarray(v.reshape(-1, P).T)

    arrays = {
        "x": x, "src": src, "dst": dst, "W1": a["W1"], "b1": columns(a["b1"]), "W2": a["W2"], "b2": a["b2"],
        "W_msg": a["W_msg"], "b_msg": a["b_msg"], "W_att": a["W_att"], "b_att": a["b_att"],
        "W_ih": np.ascontiguousarray(a["W_ih"].T), "b_ih": columns(a["b_ih"]),
        "W_hh": np.ascontiguousarray(a["W_hh"].T), "b_hh": columns(a["b_hh"]),
        "gamma": columns(a["gamma"]), "beta": columns(a["beta"]),
    }
    nc = bacc.Bacc("TRN2", target_bir_lowering=False, num_devices=1)
    args = [nc.dram_tensor(f"in_{k}", arrays[k].shape, mybir.dt.from_np(arrays[k].dtype), kind="ExternalInput").ap() for k in _INS]
    result = nc.dram_tensor("out_y", [NG, P, J * D], F32, kind="ExternalOutput").ap()
    build_gnn(nc, *args, result)
    r = run_bass_kernel_spmd(nc, [{f"in_{k}": np.ascontiguousarray(arrays[k]) for k in _INS}], core_ids=[0])
    y = r.results[0]["out_y"].reshape(NG, P, J, D).transpose(0, 2, 1, 3).reshape(NP, D)
    return np.ascontiguousarray(y[:N])
```

```python
from contextlib import ExitStack

import concourse.bass as bass
import numpy as np
from concourse import mybir

N = 50000
E = 25000
D = 128
P = 128
J = 4
GN = J * P
NG = -(-N // GN)
NP = NG * GN
NT = NG * J
TAIL = N - (NG - 1) * GN
U = 4
HS = 7
HU = 2 * HS
ET = -(-E // P)
EP = ET * P
EL = EP + P
QC = 4
QT = NT // QC
DM = D + 2
PAD_DST = 65535
SKIP = 1 << 20
SURE = 1e30
LN_EPS = 1e-5
BN_EPS = 1e-5

ALU = mybir.AluOpType
ACT = mybir.ActivationFunctionType
AX_X = mybir.AxisListType.X
F32 = mybir.dt.float32
I32 = mybir.dt.int32
F16 = mybir.dt.float16
BF16 = mybir.dt.bfloat16


class Group:

    def __init__(self, i, c):
        self.i, self.c = i, c
        self.index = i * U + c
        self.fixed = isinstance(i, int)

    def slot(self, k):
        return self.c % k

    def done(self):
        return self.i * U + (self.c + 1)

    def freed(self, k):
        return self.i * U + (self.c + 1 - k)

    def dma(self, k, n=1):
        return self.i * (16 * n * (U // k)) + 16 * n * (self.c // k + 1)

    def dma_freed(self, k, n=1):
        return self.i * (16 * n * (U // k)) + 16 * n * (self.c // k)


def groups_of_slot(u, k):
    return len(range(u, NG, k))


def wait_all_dmas(eng, slots, n=1):
    for u, sem in enumerate(slots):
        eng.wait_ge(sem, 16 * n * groups_of_slot(u, len(slots)))


def wait(eng, sem, value):
    if isinstance(value, int) and value <= 0:
        return
    eng.wait_ge(sem, value)


def in_register(eng, value):
    return value if isinstance(value, int) else eng.to_reg(value)


def run_pass(eng, step, lag):
    def at(i, u):
        def group_of(stage_lag):
            g = Group(i, u - stage_lag)
            return None if g.fixed and not 0 <= g.index < NG else g
        return group_of

    first = -(-(lag + U) // U)
    last = NG // U
    for i in range(first):
        for u in range(U):
            step(at(i, u))
    with eng.Fori(first, last) as i:
        for u in range(U):
            step(at(i, u))
    for t in range(last * U, NG + lag):
        step(at(t // U, t % U))


def build_gnn(nc, x, src, dst, w1, b1, w2, b2, wmsg, bmsg, watt, batt, wih, bih, whh, bhh, gamma, beta, out):
    ctx = ExitStack()
    with ctx:
        def sb(name, shape, dt=F32):
            return ctx.enter_context(nc.sbuf_tensor(name, shape, dt))

        def sem(name):
            return ctx.enter_context(nc.semaphore(name))

        def sems(name, k):
            return [sem(f"{name}{u}") for u in range(k)]

        XP = nc.dram_tensor("XP", [NG, P, J * D], F32).ap()
        G2 = nc.dram_tensor("G2", [NG, P, J * D], F32).ap()
        MT = nc.dram_tensor("MT", [NG, P, J * DM], F32).ap()
        SUM = nc.dram_tensor("SUM", [NG, P, J * D], F32).ap()
        SUMM = nc.dram_tensor("SUMM", [NG, P, J * DM], F32).ap()
        OWN = nc.dram_tensor("OWN", [NG, P, J * D], F32).ap()
        YT = nc.dram_tensor("YT", [NG, P, GN], F32).ap()
        HT = nc.dram_tensor("HT", [NG, P, GN], F32).ap()
        AD = nc.dram_tensor("AD", [NG, P, J], F32).ap()
        xp_rows = XP.rearrange("g p (j d) -> (g p j) d", d=D)
        g2_rows = G2.rearrange("g p (j d) -> (g p j) d", d=D)
        mt_rows = MT.rearrange("g p (j d) -> (g p j) d", d=DM)
        sum_rows = SUM.rearrange("g p (j d) -> (g p j) d", d=D)
        summ_rows = SUMM.rearrange("g p (j d) -> (g p j) d", d=DM)

        def group_of_table(table, g):
            return table[bass.ds(g.index, 1)].rearrange("a p n -> (a p) n")

        bank = [ctx.enter_context(nc.psum_tensor(f"bank{b}", [P, 512], F32)) for b in range(8)]

        ident = sb("ident", [P, P])
        ones = sb("ones", [P, P])
        before = sb("before", [P, P])
        after = sb("after", [P, P])
        col_n = sb("col_n", [P, P])
        part_n = sb("part_n", [P, 1])
        tile_h = sb("tile_h", [P, NT], F16)
        tile_base = sb("tile_base", [P, NT])
        sum_row = sb("sum_row", [P, NT])
        w1_sb = sb("w1_sb", [P, 2 * P])
        w2_sb = sb("w2_sb", [P, 2, D])
        wm_sb = sb("wm_sb", [P, DM])
        wih_sb = sb("wih_sb", [P, 3 * D])
        whh_sb = sb("whh_sb", [P, 3 * D])
        b1_sb = sb("b1_sb", [P, 2])
        bih_sb = sb("bih_sb", [P, 3])
        bhh_sb = sb("bhh_sb", [P, 3])
        brz_sb = sb("brz_sb", [P, 2])
        gb_sb = sb("gb_sb", [P, 2])
        batt_sb = sb("batt_sb", [P, 1])
        b2_row = sb("b2_row", [P, D])
        bm_row = sb("bm_row", [P, DM])
        eps_sb = sb("eps_sb", [P, 2])

        ROWI = sb("ROWI", [P, NT], I32)
        LOC = sb("LOC", [P, NT])
        DINV = sb("DINV", [P, NT])
        slow = sb("slow", [P, 1])
        fast = sb("fast", [P, 1])
        slow_i = sb("slow_i", [P, 1], I32)

        dst_e = sb("dst_e", [P, ET], I32)
        src_e = sb("src_e", [P, ET], I32)
        hi_i = sb("hi_i", [P, ET], I32)
        lo_i = sb("lo_i", [P, ET], I32)
        hi_f = sb("hi_f", [P, ET])
        lo_f = sb("lo_f", [P, ET])
        oh_hi = sb("oh_hi", [P, HS, NT], BF16)
        oh_lo = sb("oh_lo", [P, HS, P], BF16)
        cnt = sb("cnt", [P, NT])
        deg = sb("deg", [P, NT])
        root = sb("root", [P, NT])
        t_a = sb("t_a", [P, NT])
        t_b = sb("t_b", [P, NT])
        tile_cnt = sb("tile_cnt", [P, QC])
        start_i = sb("start_i", [P, QC], I32)
        win_src = sb("win_src", [P, QC, P], I32)
        win_dst = sb("win_dst", [P, QC, P], I32)
        win_t = sb("win_t", [P, QC, P], I32)
        win_u = sb("win_u", [P, QC, P], I32)
        win_sf = sb("win_sf", [P, QC, P])
        win_df = sb("win_df", [P, QC, P])
        held = sb("held", [P, 1])

        def several(name, n, shape, dt=F32):
            return [sb(f"{name}{u}", shape, dt) for u in range(n)]

        zeros = sb("zeros", [P, J * DM])
        e_src = sb("e_src", [P, ET], I32)
        e_dst = sb("e_dst", [P, ET], I32)
        e_dstf = sb("e_dstf", [P, ET])
        e_rowf = sb("e_rowf", [P, ET])
        one_src = sb("one_src", [P, 1], I32)
        one_tab = sb("one_tab", [P, 1], I32)
        one_out = sb("one_out", [P, 1], I32)
        one_f = sb("one_f", [P, 2])
        e_col = sb("e_col", [P, P])
        e_same = sb("e_same", [P, P])
        e_junk = sb("e_junk", [P, P])
        e_msg = sb("e_msg", [P, DM])
        e_tgt = sb("e_tgt", [P, DM])
        e_sum = sb("e_sum", [P, DM])
        e_new = sb("e_new", [P, DM])
        e_att = sb("e_att", [P, 2])

        def two(name, shape, dt=F32):
            return [sb(f"{name}{u}", shape, dt) for u in range(2)]

        rowi = several("rowi", 4, [P, J], I32)
        scl = several("scl", 4, [P, J])
        scl2 = several("scl2", 4, [P, J])
        loc_g = several("loc_g", 2, [P, J])
        la = several("la", 2, [P, J])
        lg = several("lg", 2, [P, J])
        att = several("att", 2, [P, J])
        ad_out = several("ad_out", 4, [P, J])
        st6 = several("st6", 4, [P, J, 6])
        st_s = several("st_s", 4, [P, J])
        st_d = several("st_d", 4, [P, J])
        st_v = several("st_v", 4, [P, J])
        st_q = several("st_q", 4, [P, J])
        st_r = several("st_r", 4, [P, J])
        st_m = several("st_m", 4, [P, J])
        hsum = sb("hsum", [P, NG])
        hsq = sb("hsq", [P, NG])
        bn = sb("bn", [P, 8])

        gath = several("gath", 4, [P, J, DM])
        onehot = several("onehot", 2, [P, J, P])

        pages = several("page", 28, [P, J * DM])

        def names(*counts):
            left = iter(pages)
            return [[next(left)[:, 0:GN] for _ in range(n)] for n in counts]

        s_x, s_o = names(4, 4)
        a_x, a_xb, a_v, a_s, a_T, a_h0, a_h1, a_g, a_r = names(4, 4, 2, 2, 2, 2, 2, 4, 4)
        n_r, n_z, n_y, n_T = names(4, 4, 4, 4)
        n_m = pages[16:20]
        c_y, c_ad, c_h, c_a, c_r, c_z, c_u, c_n, c_t, c_d, c_e, c_sq, c_junk = names(4, 4, 4, 2, 2, 2, 2, 2, 1, 1, 1, 1, 1)
        o_h, o_y, o_t, o_u, o_o = names(4, 4, 4, 4, 4)

        loaded = sem("loaded")
        w_loaded = sem("w_loaded")
        consts = sem("consts")
        zeroed = sem("zeroed")
        oh_ready = sem("oh_ready")
        oh_used = sem("oh_used")
        deg_plus = sem("deg_plus")
        rooted = sem("rooted")
        cnt_copied = sem("cnt_copied")
        tile_cnts = sem("tile_cnts")
        tile_cnts_sb = sem("tile_cnts_sb")
        starts = sem("starts")
        starts_sb = sem("starts_sb")
        windows = sem("windows")
        windows_f = sem("windows_f")
        windows_T = sem("windows_T")
        held_rows = sem("held_rows")
        held_sum = sem("held_sum")
        dinv_ready = sem("dinv_ready")
        ready = sem("ready")
        dchain = sem("dchain")

        def gathered(n, g):
            return g.dma(4, J) + 16 * J * n * groups_of_slot(g.slot(4), 4)

        block = ctx.enter_context(nc.Block())

        gen = {k: sem("q_" + k) for k in "clear idx colT rows rows2 msg same prod att attd new out place total".split()}

        s_in, s_st = sems("s_in", 4), sems("s_st", 4)
        s_dd, s_done = sem("s_dd"), sem("s_done")
        landed, idx = sems("landed", 4), sem("idx")
        a_in, a_st = sems("a_in", 4), sems("a_st", 4)
        a_oh, a_agg, a_xbs, a_sum, a_scaled, a_tr, a_trc, a_hid, a_relu, a_out, a_gs, a_rs = (
            sem("a_" + k) for k in "oh agg xb sum scaled tr trc hid relu out g r".split())
        n_in, n_st = sems("n_in", 4), sems("n_st", 4)
        n_oh, n_agg, n_dd, n_zz, n_s6, n_sd, n_dq, n_var, n_root, n_rs, n_yy, n_tr, n_trc, n_mm, n_mc, n_ad = (
            sem("n_" + k) for k in "oh agg dd zz s6 sd dq var root rs yy tr trc mm mc ad".split())
        c_iny, c_ina, c_st = sems("c_iny", 4), sems("c_ina", 4), sems("c_st", 4)
        c_dd, c_las, c_ls, c_at, c_oh, c_agg, c_aT, c_pr, c_pz, c_ph, c_pi, c_rs, c_zs, c_t1, c_t2, c_ns, c_ds, c_zd, c_hh, c_sqs = (
            sem("c_" + k) for k in "dd las ls at oh agg aT pr pz ph pi rs zs t1 t2 ns d zd hh sqs".split())
        bn_v, bn_r, bn_ok = sem("bn_v"), sem("bn_r"), sem("bn_ok")
        o_inh, o_iny, o_st = sems("o_inh", 4), sems("o_iny", 4), sems("o_st", 4)
        o_b, o_q, o_tr, o_s6, o_sd, o_dq, o_var, o_root, o_rs, o_oo = (sem("o_" + k) for k in "b q tr s6 sd dq var root rs oo".split())

        W_LOADS = 15
        CONSTS = 9
        CLEARS = 1

        def general_clear(sp, n, table, width):
            flag = sp.value_load(slow_i[0:1, 0:1], min_val=0, max_val=1)
            with sp.If(flag > 0):
                with sp.Fori(0, NG) as g:
                    sp.dma_start(table[bass.ds(g, 1)].rearrange("a p n -> (a p) n"), zeros[:, 0:J * width])\
                      .then_inc(gen["clear"], 16)

        def general_pool(pool, n, rows, sums, width):
            q = gen
            flag = pool.value_load(slow_i[0:1, 0:1], min_val=0, max_val=1)
            with pool.If(flag > 0):
                pool.wait_ge(q["clear"], 16 * NG * (n + 1))
                last_row = pool.to_reg(NP - 1)
                with pool.Fori(0, ET) as t:
                    tiles = in_register(pool, t + (n * ET + 1))
                    pool.wait_ge(ready, 1)
                    pool.wait_ge(q["idx"], tiles)
                    pool.indirect_dma_start(e_msg[:, 0:width], None, rows, bass.IndirectOffsetOnAxis(ap=one_src[:, 0:1], axis=0),
                                            bounds_check=last_row, oob_is_err=False).then_inc(q["rows"], 16)
                    pool.indirect_dma_start(e_sum[:, 0:width], None, sums, bass.IndirectOffsetOnAxis(ap=one_tab[:, 0:1], axis=0),
                                            bounds_check=last_row, oob_is_err=False).then_inc(q["rows2"], 16)
                    if n == 2:
                        pool.indirect_dma_start(e_tgt[:, 0:width], None, rows, bass.IndirectOffsetOnAxis(ap=one_tab[:, 0:1], axis=0),
                                                bounds_check=last_row, oob_is_err=False).then_inc(q["attd"], 16)
                    pool.wait_ge(ready, 1)
                    pool.wait_ge(q["new"], tiles)
                    pool.indirect_dma_start(sums, bass.IndirectOffsetOnAxis(ap=one_out[:, 0:1], axis=0), e_new[:, 0:width], None,
                                            bounds_check=last_row, oob_is_err=False).then_inc(q["out"], 16)
                pool.wait_ge(q["out"], 16 * ET * (n + 1))

        def general_act(act, n):
            flag = act.value_load(slow_i[0:1, 0:1], min_val=0, max_val=1)
            with act.If(flag > 0):
                q = gen
                with act.Fori(0, ET) as t:
                    act.wait_ge(q["msg"], t + 1)
                    nc.scalar.activation(e_att[:, 1:2], e_att[:, 0:1], ACT.Sigmoid, bias=batt_sb[:, 0:1]).then_inc(q["att"], 1)

        def general_tensor(pe, n, width):
            flag = pe.value_load(slow_i[0:1, 0:1], min_val=0, max_val=1)
            q = gen
            with pe.If(flag > 0):
                with pe.Fori(0, ET) as t:
                    pe.wait_ge(q["idx"], t + (n * ET + 1))
                    nc.tensor.transpose(bank[5][:, 0:P], e_col[:], ident[:]).then_inc(q["colT"], 1)
                    pe.wait_ge(q["same"], t + (n * ET + 1))
                    nc.tensor.matmul(bank[6][:, 0:width], e_same[:], e_msg[:, 0:width], start=True, stop=True).then_inc(q["prod"], 1)

        def general_vector(dve, n, width, link):
            flag = dve.value_load(slow_i[0:1, 0:1], min_val=0, max_val=1)
            q = gen
            with dve.If(flag > 0):
                with dve.Fori(0, ET) as t:
                    nc.vector.tensor_copy(one_src[:], e_src[:, bass.ds(t, 1)])
                    nc.vector.tensor_copy(one_tab[:], e_dst[:, bass.ds(t, 1)])
                    nc.vector.tensor_copy(one_f[:, 0:1], e_dstf[:, bass.ds(t, 1)])
                    nc.vector.tensor_scalar(e_col[:], ones[:], e_dstf[:, bass.ds(t, 1)], None, ALU.mult).then_inc(q["idx"], 1)
                    dve.wait_ge(q["colT"], t + (n * ET + 1))
                    dve.wait_ge(q["idx"], t + (n * ET + 1))
                    nc.vector.tensor_scalar(e_same[:], bank[5][:, 0:P], one_f[:, 0:1], None, ALU.is_equal).then_inc(q["place"], 1)
                    dve.wait_ge(q["place"], t * 3 + (3 * n * ET + 1))
                    nc.vector.tensor_tensor_reduce(e_junk[:], e_same[:], after[:], 1.0, 0.0, ALU.mult, ALU.add, one_f[:, 1:2]).then_inc(q["place"], 1)
                    dve.wait_ge(q["place"], t * 3 + (3 * n * ET + 2))
                    nc.vector.scalar_tensor_tensor(one_out[:], one_f[:, 1:2], float(SKIP), e_rowf[:, bass.ds(t, 1)], ALU.mult, ALU.add)\
                      .then_inc(q["place"], 1)
                    dve.wait_ge(q["rows"], t * 16 + (16 * n * ET + 16))
                    dve.wait_ge(q["rows2"], t * 16 + (16 * n * ET + 16))
                    if n == 2:
                        dve.wait_ge(q["attd"], t * 16 + 16)
                        nc.vector.tensor_tensor(e_att[:, 0:1], e_msg[:, D:D + 1], e_tgt[:, D + 1:DM], ALU.add).then_inc(q["msg"], 1)
                        dve.wait_ge(q["msg"], t + 1)
                        dve.wait_ge(q["att"], t + 1)
                        nc.vector.tensor_scalar(e_msg[:, 0:width], e_msg[:, 0:width], e_att[:, 1:2], None, ALU.mult).then_inc(q["same"], 1)
                    else:
                        dve.wait_ge(q["place"], t * 3 + (3 * n * ET + 3))
                        nc.vector.tensor_copy(one_f[:, 1:2], one_f[:, 0:1]).then_inc(q["same"], 1)
                    dve.wait_ge(q["prod"], t + (n * ET + 1))
                    nc.vector.tensor_tensor(e_new[:, 0:width], e_sum[:, 0:width], bank[6][:, 0:width], ALU.add).then_inc(q["total"], 1)
                    dve.wait_ge(q["total"], t + (n * ET + 1))
                    if n == 2:
                        nc.vector.memset(e_new[:, D:D + 1], SURE).then_inc(q["new"], 1)
                    else:
                        nc.vector.memset(one_f[:, 1:2], 0.0).then_inc(q["new"], 1)
                    dve.wait_ge(q["out"], t * 16 + (16 * n * ET + 16))

        @block.sync
        def _(sp):
            sp.dma_start(dst_e[:], dst[0:EP].rearrange("(p k) -> p k", p=P)).then_inc(loaded, 16)
            sp.dma_start(src_e[:], src[0:EP].rearrange("(p k) -> p k", p=P)).then_inc(loaded, 16)
            for t, a in ((w1_sb, w1), (wih_sb, wih), (whh_sb, whh), (b1_sb, b1), (bih_sb, bih), (bhh_sb, bhh)):
                sp.dma_start(t[:], a).then_inc(w_loaded, 16)
            sp.dma_start(w2_sb[:], w2.rearrange("(k p) o -> p k o", k=2)).then_inc(w_loaded, 16)
            sp.dma_start(wm_sb[:, 0:D], wmsg).then_inc(w_loaded, 16)
            sp.dma_start(wm_sb[:, D:D + 1], watt[0:D]).then_inc(w_loaded, 16)
            sp.dma_start(wm_sb[:, D + 1:DM], watt[D:2 * D]).then_inc(w_loaded, 16)
            sp.dma_start(gb_sb[:, 0:1], gamma).then_inc(w_loaded, 16)
            sp.dma_start(gb_sb[:, 1:2], beta).then_inc(w_loaded, 16)
            sp.dma_start(batt_sb[:], batt.partition_broadcast(P)).then_inc(w_loaded, 16)
            sp.dma_start(b2_row[:], b2.partition_broadcast(P)).then_inc(w_loaded, 16)
            sp.wait_ge(zeroed, CLEARS)
            sp.dma_start(bm_row[:, 0:D], bmsg.partition_broadcast(P)).then_inc(w_loaded, 16)

            def scale(group_of):
                if g := group_of(0):
                    k = g.slot(4)
                    wait(sp, s_done, g.freed(4))
                    sp.dma_start(s_x[k], group_of_table(x, g)).then_inc(s_in[k], 16)
                if g := group_of(3):
                    k = g.slot(4)
                    wait(sp, s_done, g.done())
                    sp.dma_start(group_of_table(XP, g), s_o[k]).then_inc(s_st[k], 16)

            run_pass(sp, scale, 3)
            wait_all_dmas(sp, s_st)
            sp.wait_ge(ready, 1)
            general_clear(sp, 0, SUM, D)

            def conv(group_of):
                if g := group_of(0):
                    k = g.slot(4)
                    wait(sp, a_sum, g.freed(4))
                    sp.dma_start(a_x[k], group_of_table(x, g)).then_inc(a_in[k], 16)
                if g := group_of(6):
                    k = g.slot(4)
                    wait(sp, a_gs, g.done())
                    sp.dma_start(group_of_table(G2, g), a_g[k]).then_inc(a_st[k], 16)
                    wait(sp, a_rs, g.done())
                    sp.dma_start(group_of_table(OWN, g), a_r[k]).then_inc(a_st[k], 16)

            run_pass(sp, conv, 6)
            wait_all_dmas(sp, a_st, 2)
            general_clear(sp, 1, SUM, D)

            def norm(group_of):
                if g := group_of(0):
                    k = g.slot(4)
                    wait(sp, n_zz, g.freed(4))
                    sp.dma_start(n_r[k], group_of_table(OWN, g)).then_inc(n_in[k], 16)
                if g := group_of(7):
                    k = g.slot(4)
                    wait(sp, n_trc, g.done())
                    sp.dma_start(group_of_table(YT, g), n_T[k]).then_inc(n_st[k], 16)
                    wait(sp, n_mc, g.done())
                    sp.dma_start(group_of_table(MT, g), n_m[k][:]).then_inc(n_st[k], 16)
                    wait(sp, n_ad, g.done())
                    sp.dma_start(group_of_table(AD, g), ad_out[k][:]).then_inc(n_st[k], 16)

            run_pass(sp, norm, 7)
            wait_all_dmas(sp, n_st, 3)
            general_clear(sp, 2, SUMM, DM)

            def gru(group_of):
                if g := group_of(0):
                    k = g.slot(4)
                    wait(sp, c_las, g.freed(4))
                    sp.dma_start(c_ad[k], AD[bass.ds(g.index, 1)].rearrange("a p j -> a (p j)").to_broadcast([P, GN]))\
                      .then_inc(c_ina[k], 16)
                if g := group_of(2):
                    k = g.slot(4)
                    wait(sp, c_ds, g.freed(4))
                    wait(sp, c_pz, g.freed(4))
                    sp.dma_start(c_y[k], group_of_table(YT, g)).then_inc(c_iny[k], 16)
                if g := group_of(7):
                    k = g.slot(4)
                    wait(sp, c_hh, g.done())
                    sp.dma_start(group_of_table(HT, g), c_h[k]).then_inc(c_st[k], 16)

            run_pass(sp, gru, 7)
            wait_all_dmas(sp, c_st)
            sp.wait_ge(c_sqs, NG)

            def final(group_of):
                if g := group_of(0):
                    k = g.slot(4)
                    wait(sp, o_b, g.freed(4))
                    sp.dma_start(o_h[k], group_of_table(HT, g)).then_inc(o_inh[k], 16)
                    wait(sp, o_q, g.freed(4))
                    sp.dma_start(o_y[k], group_of_table(YT, g)).then_inc(o_iny[k], 16)
                if g := group_of(8):
                    k = g.slot(4)
                    wait(sp, o_oo, g.done())
                    sp.dma_start(group_of_table(out, g), o_o[k]).then_inc(o_st[k], 16)

            run_pass(sp, final, 8)
            wait_all_dmas(sp, o_st)

        @block.gpsimd
        def _(pool):
            exact = dict(allow_small_or_imprecise_dtypes=True)
            nc.gpsimd.iota(tile_h[:], [[1, NT]], base=0, channel_multiplier=0, **exact).then_inc(consts, 1)
            nc.gpsimd.iota(col_n[:], [[1, P]], base=0, channel_multiplier=0, **exact).then_inc(consts, 1)
            nc.gpsimd.iota(part_n[:], [[0, 1]], base=0, channel_multiplier=1, **exact).then_inc(consts, 1)
            nc.gpsimd.iota(tile_base[:], [[P, NT]], base=0, channel_multiplier=0, **exact).then_inc(consts, 1)
            nc.gpsimd.iota(sum_row[:], [[GN, NG], [1, J]], base=0, channel_multiplier=J, **exact).then_inc(consts, 1)
            nc.gpsimd.memset(ones[:], 1.0).then_inc(consts, 1)
            pool.wait_ge(consts, 6)
            for m, op, base, step in ((ident, ALU.is_equal, 0, -1), (before, ALU.is_gt, 0, 1)):
                nc.gpsimd.affine_select(out=m[:], in_=ones[:], compare_op=op, fill=0.0, base=base,
                                        pattern=[[step, P]], channel_multiplier=-step).then_inc(consts, 1)
            nc.gpsimd.affine_select(out=after[:], in_=ones[:], compare_op=ALU.is_gt, fill=0.0, base=0,
                                    pattern=[[-1, P]], channel_multiplier=1).then_inc(consts, 1)

            pool.wait_ge(starts_sb, 1)
            for arr, win in ((src, win_src), (dst, win_dst)):
                flat = arr.rearrange("(a b) -> a b", b=1)
                for c in range(QC):
                    nc.gpsimd.indirect_dma_start(win[0:QT, c, :], None, flat,
                                                 bass.IndirectOffsetOnAxis(ap=start_i[0:QT, c:c + 1], axis=0)).then_inc(windows, 16)

            def gathers(n, table, sum_table, width, used_rows):
                last_row = pool.to_reg(NP - 1)

                def step(group_of, rows):
                    g = group_of(0)
                    k = g.slot(4)
                    pool.wait_ge(ready, 1)
                    wait(pool, landed[k], gathered(n, g) - 16 * J)
                    nc.gpsimd.tensor_copy(rowi[k][:], ROWI[:, bass.ds(g.index * J, J)]).then_inc(idx, 1)
                    copied, used = in_register(pool, g.done() + n * NG), in_register(pool, g.freed(4))
                    pool.wait_ge(ready, 1)
                    wait(pool, idx, copied)
                    wait(pool, used_rows, used)
                    for j in range(J):
                        nc.gpsimd.indirect_dma_start(gath[k][:, j, 0:width], None, rows,
                                                     bass.IndirectOffsetOnAxis(ap=rowi[k][:, j:j + 1], axis=0),
                                                     bounds_check=last_row, oob_is_err=False).then_inc(landed[k], 16)

                flag = pool.value_load(slow_i[0:1, 0:1], min_val=0, max_val=1)
                with pool.If(flag < 1):
                    run_pass(pool, lambda group_of: step(group_of, table), 0)
                with pool.If(flag > 0):
                    run_pass(pool, lambda group_of: step(group_of, sum_table), 0)
                for u in range(4):
                    pool.wait_ge(landed[u], 16 * J * (n + 1) * groups_of_slot(u, 4))

            pool.wait_ge(ready, 1)
            wait_all_dmas(pool, s_st)
            general_pool(pool, 0, xp_rows, sum_rows, D)
            gathers(0, xp_rows, sum_rows, D, a_agg)
            wait_all_dmas(pool, a_st, 2)
            general_pool(pool, 1, g2_rows, sum_rows, D)
            pool.wait_ge(a_agg, NG)
            gathers(1, g2_rows, sum_rows, D, n_agg)
            wait_all_dmas(pool, n_st, 3)
            general_pool(pool, 2, mt_rows, summ_rows, DM)
            pool.wait_ge(n_agg, NG)
            gathers(2, mt_rows, summ_rows, DM, c_agg)

        @block.scalar
        def _(act):
            act.wait_ge(w_loaded, 16 * W_LOADS)
            act.wait_ge(deg_plus, 1)
            nc.scalar.activation(root[:], deg[:], ACT.Sqrt).then_inc(rooted, 1)
            act.wait_ge(dinv_ready, 1)

            def scale(group_of):
                if g := group_of(0):
                    k = g.slot(4)
                    wait(act, s_done, g.freed(4))
                    nc.scalar.activation(scl[k][:], DINV[:, bass.ds(g.index * J, J)], ACT.Copy).then_inc(s_dd, 1)
                    wait(act, s_in[k], g.dma(4))
                    wait(act, s_st[k], g.dma_freed(4))
                    wait(act, s_dd, g.done())
                    for j in range(J):
                        last = nc.scalar.activation(s_o[k][:, j * D:(j + 1) * D], s_x[k][:, j * D:(j + 1) * D],
                                                    ACT.Copy, scale=scl[k][:, j:j + 1])
                    last.then_inc(s_done, 1)

            run_pass(act, scale, 0)
            wait_all_dmas(act, s_st)

            def conv(group_of):
                if g := group_of(4):
                    k = g.slot(2)
                    wait(act, a_out, g.freed(2))
                    wait(act, a_hid, g.done())
                    for h, rows in enumerate((a_h0, a_h1)):
                        last = nc.scalar.activation(rows[k], bank[3 + h][:], ACT.Relu, bias=b1_sb[:, h:h + 1])
                    last.then_inc(a_relu, 1)
                if g := group_of(2):
                    k = g.slot(2)
                    wait(act, a_tr, g.done())
                    wait(act, a_hid, g.freed(2))
                    nc.scalar.activation(a_T[k], bank[2][:], ACT.Copy).then_inc(a_trc, 1)
                if g := group_of(1):
                    k = g.slot(2)
                    wait(act, a_sum, g.done())
                    wait(act, a_tr, g.freed(2))
                    for j in range(J):
                        last = nc.scalar.activation(a_s[k][:, j * D:(j + 1) * D], a_v[k][:, j * D:(j + 1) * D],
                                                    ACT.Copy, scale=scl[g.slot(4)][:, j:j + 1])
                    last.then_inc(a_scaled, 1)

            run_pass(act, conv, 4)
            wait_all_dmas(act, a_st, 2)

            def norm(group_of):
                if g := group_of(3):
                    k = g.slot(4)
                    wait(act, n_rs, g.done())
                    wait(act, n_tr, g.freed(4))
                    for j in range(J):
                        last = nc.scalar.activation(n_y[k][:, j * D:(j + 1) * D], n_z[k][:, j * D:(j + 1) * D], ACT.Identity,
                                                    bias=st_m[k][:, j:j + 1], scale=st_r[k][:, j:j + 1])
                    last.then_inc(n_yy, 1)
                if g := group_of(4):
                    k = g.slot(4)
                    wait(act, n_tr, g.done())
                    wait(act, n_st[k], g.dma_freed(4, 3))
                    wait(act, n_mm, g.freed(4))
                    nc.scalar.activation(n_T[k], bank[2 + g.slot(2)][:], ACT.Copy).then_inc(n_trc, 1)
                if g := group_of(2):
                    k = g.slot(4)
                    wait(act, n_var, g.done())
                    nc.scalar.activation(st_q[k][:], st_v[k][:], ACT.Sqrt, bias=eps_sb[:, 0:1], scale=1.0 / D).then_inc(n_root, 1)

            run_pass(act, norm, 4)
            wait_all_dmas(act, n_st, 3)
            general_act(act, 2)

            def gru(group_of):
                if g := group_of(4):
                    k = g.slot(2)
                    wait(act, c_t2, g.done())
                    wait(act, c_hh, g.freed(2))
                    nc.scalar.activation(c_n[k], c_u[k], ACT.Tanh, bias=bih_sb[:, 2:3]).then_inc(c_ns, 1)
                if g := group_of(2):
                    k = g.slot(2)
                    wait(act, c_agg, g.done())
                    wait(act, c_pz, g.freed(2))
                    nc.scalar.activation(c_a[k], bank[k][:], ACT.Copy).then_inc(c_aT, 1)
                if g := group_of(3):
                    k = g.slot(2)
                    wait(act, c_pr, g.done())
                    wait(act, c_t1, g.freed(2))
                    nc.scalar.activation(c_r[k], bank[2][:], ACT.Sigmoid, bias=brz_sb[:, 0:1]).then_inc(c_rs, 1)
                if g := group_of(0):
                    k = g.slot(2)
                    wait(act, c_ls, g.done())
                    wait(act, c_oh, g.freed(2))
                    nc.scalar.activation(att[k][:], lg[k][:], ACT.Sigmoid, bias=batt_sb[:, 0:1]).then_inc(c_at, 1)
                if g := group_of(3):
                    k = g.slot(2)
                    wait(act, c_pz, g.done())
                    wait(act, c_zd, g.freed(2))
                    nc.scalar.activation(c_z[k], bank[3][:], ACT.Sigmoid, bias=brz_sb[:, 1:2]).then_inc(c_zs, 1)
                if g := group_of(5):
                    k = g.slot(4)
                    wait(act, c_hh, g.done())
                    wait(act, c_sqs, g.done() - 1)
                    n = TAIL if g.fixed and g.index == NG - 1 else GN
                    nc.scalar.activation(c_sq[0][:, 0:n], c_h[k][:, 0:n], ACT.Square,
                                         accum_out=hsq[:, bass.ds(g.index, 1)]).then_inc(c_sqs, 1)

            act.wait_ge(bn_ok, 1)
            run_pass(act, gru, 5)
            act.wait_ge(bn_v, 1)
            nc.scalar.activation(bn[:, 3:4], bn[:, 2:3], ACT.Sqrt, bias=eps_sb[:, 1:2]).then_inc(bn_r, 1)
            act.wait_ge(bn_ok, 2)
            wait_all_dmas(act, c_st)

            def final(group_of):
                if g := group_of(0):
                    k = g.slot(4)
                    wait(act, o_inh[k], g.dma(4))
                    wait(act, o_q, g.freed(4))
                    nc.scalar.activation(o_t[k], o_h[k], ACT.Identity, bias=bn[:, 6:7], scale=bn[:, 5:6]).then_inc(o_b, 1)
                if g := group_of(5):
                    k = g.slot(4)
                    wait(act, o_rs, g.done())
                    wait(act, o_st[k], g.dma_freed(4))
                    for j in range(J):
                        last = nc.scalar.activation(o_o[k][:, j * D:(j + 1) * D], bank[k][:, j * D:(j + 1) * D], ACT.Identity,
                                                    bias=st_m[k][:, j:j + 1], scale=st_r[k][:, j:j + 1])
                    last.then_inc(o_oo, 1)
                if g := group_of(4):
                    k = g.slot(4)
                    wait(act, o_var, g.done())
                    nc.scalar.activation(st_q[k][:], st_v[k][:], ACT.Sqrt, bias=eps_sb[:, 0:1], scale=1.0 / D).then_inc(o_root, 1)

            run_pass(act, final, 5)

        @block.vector
        def _(dve):
            count = [0]

            def link(ins):
                count[0] += 1
                ins.then_inc(dchain, 1)
                dve.wait_ge(dchain, count[0])

            nc.vector.memset(bm_row[:, D:DM], 0.0).then_inc(zeroed, 1)
            nc.vector.memset(eps_sb[:, 0:1], LN_EPS)
            link(nc.vector.memset(eps_sb[:, 1:2], BN_EPS))
            dve.wait_ge(loaded, 32)
            nc.vector.tensor_scalar(hi_i[:], dst_e[:], 7, None, ALU.logical_shift_right)
            link(nc.vector.tensor_scalar(lo_i[:], dst_e[:], P - 1, None, ALU.bitwise_and))
            nc.vector.tensor_copy(hi_f[:], hi_i[:])
            link(nc.vector.tensor_copy(lo_f[:], lo_i[:]))
            dve.wait_ge(consts, CONSTS)

            def one_hots(i):
                for c in range(HU):
                    if c % 2 == 0:
                        wait(dve, oh_used, i * HU + (c + 2 - HS))
                    s = c % HS
                    nc.vector.tensor_scalar(oh_hi[:, s, :], tile_h[:], hi_f[:, bass.ds(i * HU + c, 1)], None, ALU.is_equal)
                    nc.vector.tensor_scalar(oh_lo[:, s, :], tile_h[:, 0:P], lo_f[:, bass.ds(i * HU + c, 1)], None, ALU.is_equal)\
                      .then_inc(oh_ready, 1)

            one_hots(0)
            with dve.Fori(1, ET // HU) as i:
                one_hots(i)
            dve.wait_ge(oh_used, ET)
            nc.vector.tensor_scalar(deg[:], bank[0][:, 0:NT], 1.0, None, ALU.add).then_inc(deg_plus, 1)
            nc.vector.tensor_copy(cnt[:], bank[0][:, 0:NT]).then_inc(cnt_copied, 1)
            dve.wait_ge(rooted, 1)
            dve.wait_ge(deg_plus, 1)
            link(nc.vector.reciprocal(DINV[:], root[:]))
            link(nc.vector.tensor_tensor(t_a[:], DINV[:], DINV[:], ALU.mult))
            link(nc.vector.tensor_tensor(t_b[:], t_a[:], deg[:], ALU.mult))
            link(nc.vector.tensor_scalar(t_a[:], t_b[:], -0.5, 1.5, ALU.mult, ALU.add))
            nc.vector.tensor_tensor(DINV[:], DINV[:], t_a[:], ALU.mult).then_inc(dinv_ready, 1)
            dve.wait_ge(tile_cnts, 1)
            nc.vector.tensor_copy(tile_cnt[0:QT, :], bank[1][0:QT, 0:QC]).then_inc(tile_cnts_sb, 1)
            dve.wait_ge(starts, 1)
            nc.vector.tensor_copy(start_i[0:QT, :], bank[2][0:QT, 0:QC]).then_inc(starts_sb, 1)
            dve.wait_ge(windows, 16 * 2 * QC)
            q = slice(0, QT)

            def table_row(to, of, tmp):
                link(nc.vector.tensor_scalar(to, of, P - 1, 2, ALU.bitwise_and, ALU.logical_shift_left))
                link(nc.vector.tensor_scalar(tmp, of, 7, J - 1, ALU.logical_shift_right, ALU.bitwise_and))
                link(nc.vector.tensor_tensor(to, to, tmp, ALU.bitwise_or))
                link(nc.vector.tensor_scalar(tmp, of, 9, 9, ALU.logical_shift_right, ALU.logical_shift_left))
                link(nc.vector.tensor_tensor(to, to, tmp, ALU.bitwise_or))

            table_row(win_t[q], win_src[q], win_u[q])
            nc.vector.tensor_copy(win_sf[q], win_t[q])
            nc.vector.tensor_copy(win_df[q], win_dst[q]).then_inc(windows_f, 1)
            dve.wait_ge(windows_T, 1)
            link(nc.vector.tensor_tensor(LOC[:], bank[4][:, 0:NT], tile_base[:], ALU.subtract))
            link(nc.vector.tensor_scalar(t_a[:], LOC[:], 0.0, None, ALU.is_ge))
            link(nc.vector.scalar_tensor_tensor(t_b[:], LOC[:], float(P), t_a[:], ALU.is_lt, ALU.mult))
            nc.vector.tensor_reduce(held[:], t_b[:], AX_X, ALU.add).then_inc(held_rows, 1)
            link(nc.vector.scalar_tensor_tensor(t_a[:], t_b[:], -float(SKIP), bank[3][:, 0:NT], ALU.mult, ALU.add))
            link(nc.vector.tensor_scalar(t_a[:], t_a[:], float(SKIP), None, ALU.add))
            dve.wait_ge(held_sum, 1)
            nc.vector.tensor_scalar(slow[:], bank[5][:, 0:1], float(E), None, ALU.not_equal)
            nc.vector.tensor_scalar(slow_i[:], bank[5][:, 0:1], float(E), None, ALU.not_equal)
            link(nc.vector.tensor_scalar(fast[:], bank[5][:, 0:1], float(E), None, ALU.is_equal))
            link(nc.vector.tensor_scalar(t_b[:], sum_row[:], slow[:, 0:1], None, ALU.mult))
            link(nc.vector.scalar_tensor_tensor(ROWI[:], t_a[:], fast[:, 0:1], t_b[:], ALU.mult, ALU.add))
            link(nc.vector.tensor_scalar(held[:], part_n[:], slow[:, 0:1], None, ALU.mult))
            link(nc.vector.tensor_scalar(LOC[:], LOC[:], fast[:, 0:1], held[:, 0:1], ALU.mult, ALU.add))
            dve.wait_ge(w_loaded, 16 * W_LOADS)
            nc.vector.tensor_tensor(brz_sb[:], bih_sb[:, 0:2], bhh_sb[:, 0:2], ALU.add).then_inc(bn_ok, 1)
            table_row(e_src[:], src_e[:], hi_i[:])
            table_row(e_dst[:], dst_e[:], hi_i[:])
            nc.vector.tensor_copy(e_rowf[:], e_dst[:])
            link(nc.vector.tensor_copy(e_dstf[:], dst_e[:]))
            for rows in (*gath, zeros, e_msg, e_sum, e_tgt):
                nc.vector.memset(rows[:], 0.0)
            nc.vector.memset(held[:], 0.0).then_inc(ready, 1)

            general_vector(dve, 0, D, link)
            wait_all_dmas(dve, s_st)

            tile_of_slot = col_n[:].unsqueeze(1).to_broadcast([P, J, P])
            row_b2 = b2_row[:].unsqueeze(1).to_broadcast([P, J, D])

            def by_tile(rows):
                return rows.rearrange("p (j d) -> p j d", j=J)

            def one_hot(g, used, made):
                wait(dve, used, g.freed(2))
                nc.vector.tensor_tensor(onehot[g.slot(2)][:], tile_of_slot,
                                        LOC[:, bass.ds(g.index * J, J)].unsqueeze(2).to_broadcast([P, J, P]),
                                        ALU.is_equal).then_inc(made, 1)

            def conv(group_of):
                if g := group_of(0):
                    one_hot(g, a_agg, a_oh)
                if g := group_of(5):
                    k = g.slot(4)
                    nc.vector.tensor_copy(scl2[k][:], DINV[:, bass.ds(g.index * J, J)]).then_inc(n_dd, 1)
                    wait(dve, a_out, g.done())
                    wait(dve, a_st[k], g.dma_freed(4, 2))
                    nc.vector.tensor_tensor(by_tile(a_g[k]), by_tile(bank[5 + g.slot(2)][:]),
                                            DINV[:, bass.ds(g.index * J, J)].unsqueeze(2).to_broadcast([P, J, D]),
                                            ALU.mult).then_inc(a_gs, 1)
                    wait(dve, a_xbs, g.done())
                    wait(dve, n_dd, g.done())
                    wait(dve, a_gs, g.done())
                    for j in range(J):
                        own = slice(j * D, (j + 1) * D)
                        last = nc.vector.scalar_tensor_tensor(a_r[k][:, own], a_g[k][:, own], scl2[k][:, j:j + 1],
                                                              a_xb[k][:, own], ALU.mult, ALU.add)
                    last.then_inc(a_rs, 1)
                if g := group_of(1):
                    k = g.slot(4)
                    wait(dve, a_scaled, g.freed(4))
                    nc.vector.tensor_copy(scl[k][:], DINV[:, bass.ds(g.index * J, J)]).then_inc(s_dd, 1)
                    wait(dve, a_in[k], g.dma(4))
                    wait(dve, a_rs, g.freed(4))
                    nc.vector.tensor_tensor(by_tile(a_xb[k]), by_tile(a_x[k]), row_b2, ALU.add).then_inc(a_xbs, 1)
                    wait(dve, s_dd, g.done() + NG)
                    wait(dve, a_agg, g.done())
                    wait(dve, a_scaled, g.freed(2))
                    for j in range(J):
                        own = slice(j * D, (j + 1) * D)
                        last = nc.vector.scalar_tensor_tensor(a_v[g.slot(2)][:, own], a_x[k][:, own], scl[k][:, j:j + 1],
                                                              bank[g.slot(2)][:, own], ALU.mult, ALU.add)
                    last.then_inc(a_sum, 1)

            run_pass(dve, conv, 5)
            general_vector(dve, 1, D, link)
            wait_all_dmas(dve, a_st, 2)

            def norm(group_of):
                if g := group_of(1):
                    k = g.slot(4)
                    wait(dve, n_in[k], g.dma(4))
                    wait(dve, n_agg, g.done())
                    wait(dve, n_dd, g.done() + NG)
                    wait(dve, n_yy, g.freed(4))
                    for j in range(J):
                        own = slice(j * D, (j + 1) * D)
                        last = nc.vector.scalar_tensor_tensor(n_z[k][:, own], bank[g.slot(2)][:, own], scl2[k][:, j:j + 1],
                                                              n_r[k][:, own], ALU.mult, ALU.add)
                    last.then_inc(n_zz, 1)
                if g := group_of(0):
                    one_hot(g, n_agg, n_oh)
                    k = g.slot(4)
                    wait(dve, n_zz, g.freed(4))
                    nc.vector.tensor_copy(scl2[k][:], DINV[:, bass.ds(g.index * J, J)]).then_inc(n_dd, 1)
                if g := group_of(6):
                    k = g.slot(4)
                    wait(dve, n_mm, g.done())
                    wait(dve, n_st[k], g.dma_freed(4, 3))
                    m = by_tile(n_m[k][:])
                    for h in range(2):
                        last = nc.vector.tensor_tensor(m[:, 2 * h:2 * h + 2, :],
                                                       bank[4 + 2 * g.slot(2) + h][:, 0:2 * DM].rearrange("p (j d) -> p j d", j=2),
                                                       bm_row[:].unsqueeze(1).to_broadcast([P, 2, DM]), ALU.add)
                    last.then_inc(n_mc, 1)
                if g := group_of(1):
                    k = g.slot(4)
                    wait(dve, n_zz, g.done())
                    row_stats(g, lambda j: n_z[k][:, j * D:(j + 1) * D], n_s6, n_yy)
                normaliser(group_of(1), group_of(2), n_s6, n_sd, n_root, n_dq, n_var, n_rs)
                if g := group_of(6):
                    k = g.slot(4)
                    wait(dve, n_mc, g.done())
                    nc.vector.tensor_copy(ad_out[k][:], by_tile(n_m[k][:])[:, :, D + 1:DM].rearrange("p j a -> p (j a)")).then_inc(n_ad, 1)

            def row_stats(g, rows_of, s6, used):
                k = g.slot(4)
                wait(dve, used, g.freed(4))
                for j in range(J):
                    last = nc.vector.bn_stats(st6[k][:, j, :], rows_of(j))
                last.then_inc(s6, 1)

            def normaliser(g, e, s6, sd, rooted_, dq, var, rs):
                if e:
                    k = e.slot(4)
                    wait(dve, rooted_, e.done())
                    nc.vector.reciprocal(st_r[k][:], st_q[k][:]).then_inc(dq, 1)
                if g:
                    k = g.slot(4)
                    wait(dve, s6, g.done())
                    part = [st6[k][:, :, n:n + 1].rearrange("p j a -> p (j a)") for n in range(6)]
                    nc.vector.tensor_tensor(st_d[k][:], part[1], part[4], ALU.subtract).then_inc(sd, 1)
                    nc.vector.tensor_tensor(st_s[k][:], part[1], part[4], ALU.add)
                    nc.vector.tensor_tensor(st_v[k][:], part[2], part[5], ALU.add)
                    wait(dve, sd, g.i * (2 * U) + (2 * g.c + 1))
                    nc.vector.tensor_tensor(st_d[k][:], st_d[k][:], st_d[k][:], ALU.mult).then_inc(sd, 1)
                if e:
                    k = e.slot(4)
                    wait(dve, dq, e.done())
                    nc.vector.scalar_tensor_tensor(st_m[k][:], st_s[k][:], -0.5, st_r[k][:], ALU.mult, ALU.mult).then_inc(rs, 1)
                if g:
                    k = g.slot(4)
                    wait(dve, sd, g.i * (2 * U) + (2 * g.c + 2))
                    nc.vector.scalar_tensor_tensor(st_v[k][:], st_d[k][:], D / 4.0, st_v[k][:], ALU.mult, ALU.add).then_inc(var, 1)

            run_pass(dve, norm, 6)
            general_vector(dve, 2, DM, link)
            wait_all_dmas(dve, n_st, 3)

            def gru(group_of):
                if g := group_of(1):
                    k = g.slot(2)
                    wait(dve, c_at, g.done())
                    wait(dve, c_agg, g.freed(2))
                    for j in range(J):
                        last = nc.vector.tensor_scalar(onehot[k][:, j, :], col_n[:], loc_g[k][:, j:j + 1],
                                                       att[k][:, j:j + 1], ALU.is_equal, ALU.mult)
                    last.then_inc(c_oh, 1)
                if g := group_of(0):
                    k = g.slot(2)
                    wait(dve, c_oh, g.freed(2))
                    nc.vector.tensor_copy(loc_g[k][:], LOC[:, bass.ds(g.index * J, J)]).then_inc(c_dd, 1)
                if g := group_of(3):
                    k = g.slot(2)
                    wait(dve, c_rs, g.done())
                    wait(dve, c_ph, g.done())
                    wait(dve, c_t2, g.done() - 1)
                    nc.vector.scalar_tensor_tensor(c_t[0], bank[4][:], bhh_sb[:, 2:3], c_r[k], ALU.add, ALU.mult).then_inc(c_t1, 1)
                if g := group_of(0):
                    k = g.slot(2)
                    wait(dve, c_ina[g.slot(4)], g.dma(4))
                    wait(dve, c_dd, g.done())
                    wait(dve, c_las, g.done() - 1)
                    by_row = c_ad[g.slot(4)].rearrange("p (n j) -> p n j", j=J)
                    for j in range(J):
                        last = nc.vector.scalar_tensor_tensor(c_junk[0][:, j * P:(j + 1) * P], col_n[:], loc_g[k][:, j:j + 1],
                                                              by_row[:, :, j:j + 1].rearrange("p n a -> p (n a)"), ALU.is_equal, ALU.mult,
                                                              accum_out=la[k][:, j:j + 1])
                    last.then_inc(c_las, 1)
                if g := group_of(3):
                    k = g.slot(2)
                    wait(dve, c_t1, g.done())
                    wait(dve, c_pi, g.done())
                    wait(dve, c_ns, g.freed(2))
                    nc.vector.tensor_tensor(c_u[k], c_t[0], bank[5][:], ALU.add).then_inc(c_t2, 1)
                if g := group_of(4):
                    k = g.slot(2)
                    wait(dve, c_ns, g.done())
                    wait(dve, c_zd, g.done() - 1)
                    nc.vector.tensor_tensor(c_d[0], c_y[g.slot(4)], c_n[k], ALU.subtract).then_inc(c_ds, 1)
                if g := group_of(0):
                    k = g.slot(2)
                    wait(dve, c_las, g.done())
                    wait(dve, landed[g.slot(4)], gathered(2, g))
                    wait(dve, c_at, g.freed(2))
                    nc.vector.tensor_tensor(lg[k][:], la[k][:],
                                            gath[g.slot(4)][:, :, D:D + 1].rearrange("p j a -> p (j a)"), ALU.add).then_inc(c_ls, 1)
                if g := group_of(4):
                    k = g.slot(2)
                    wait(dve, c_ds, g.done())
                    wait(dve, c_zs, g.done())
                    wait(dve, c_hh, g.done() - 1)
                    nc.vector.tensor_tensor(c_e[0], c_d[0], c_z[k], ALU.mult).then_inc(c_zd, 1)
                    wait(dve, c_zd, g.done())
                    wait(dve, c_st[g.slot(4)], g.dma_freed(4))
                    wait(dve, c_sqs, g.freed(4))
                    h = c_h[g.slot(4)]
                    n = TAIL if g.fixed and g.index == NG - 1 else GN
                    if n < GN:
                        nc.vector.tensor_tensor(h[:, n:GN], c_e[0][:, n:GN], c_n[k][:, n:GN], ALU.add)
                    nc.vector.scalar_tensor_tensor(h[:, 0:n], c_e[0][:, 0:n], 1.0, c_n[k][:, 0:n], ALU.mult, ALU.add,
                                                   accum_out=hsum[:, bass.ds(g.index, 1)]).then_inc(c_hh, 1)

            run_pass(dve, gru, 4)
            dve.wait_ge(c_sqs, NG)
            dve.wait_ge(c_hh, NG)
            nc.vector.tensor_reduce(bn[:, 0:1], hsum[:], AX_X, ALU.add)
            link(nc.vector.tensor_reduce(bn[:, 1:2], hsq[:], AX_X, ALU.add))
            link(nc.vector.tensor_scalar(bn[:, 0:1], bn[:, 0:1], 1.0 / N, None, ALU.mult))
            link(nc.vector.tensor_tensor(bn[:, 4:5], bn[:, 0:1], bn[:, 0:1], ALU.mult))
            link(nc.vector.scalar_tensor_tensor(bn[:, 4:5], bn[:, 1:2], 1.0 / N, bn[:, 4:5], ALU.mult, ALU.subtract))
            nc.vector.tensor_scalar(bn[:, 2:3], bn[:, 4:5], 0.0, None, ALU.max).then_inc(bn_v, 1)
            dve.wait_ge(bn_r, 1)
            link(nc.vector.reciprocal(bn[:, 4:5], bn[:, 3:4]))
            link(nc.vector.tensor_tensor(bn[:, 5:6], gb_sb[:, 0:1], bn[:, 4:5], ALU.mult))
            link(nc.vector.tensor_tensor(bn[:, 7:8], bn[:, 5:6], bn[:, 0:1], ALU.mult))
            nc.vector.tensor_tensor(bn[:, 6:7], gb_sb[:, 1:2], bn[:, 7:8], ALU.subtract).then_inc(bn_ok, 1)
            wait_all_dmas(dve, c_st)

            def final(group_of):
                if g := group_of(3):
                    k = g.slot(4)
                    wait(dve, o_tr, g.done())
                    row_stats(g, lambda j: bank[k][:, j * D:(j + 1) * D], o_s6, o_oo)
                normaliser(group_of(3), group_of(4), o_s6, o_sd, o_root, o_dq, o_var, o_rs)
                if g := group_of(1):
                    k = g.slot(4)
                    wait(dve, o_iny[k], g.dma(4))
                    wait(dve, o_b, g.done())
                    wait(dve, o_tr, g.freed(4))
                    nc.vector.tensor_tensor(o_u[k], o_t[k], o_y[k], ALU.add).then_inc(o_q, 1)

            run_pass(dve, final, 4)

        @block.tensor
        def _(pe):
            def count_edges(i, first, last):
                for c in range(HU):
                    pe.wait_ge(oh_ready, i * HU + (c + 1))
                    nc.tensor.matmul(bank[0][:, 0:NT], oh_lo[:, c % HS, :], oh_hi[:, c % HS, :], start=first and c == 0,
                                     stop=last and c == HU - 1, skip_group_check=True).then_inc(oh_used, 1)

            count_edges(0, True, False)
            with pe.Fori(1, ET // HU - 1) as i:
                count_edges(i, False, False)
            count_edges(ET // HU - 1, False, True)
            pe.wait_ge(consts, CONSTS)
            pe.wait_ge(cnt_copied, 1)
            for c in range(QC):
                last = nc.tensor.matmul(bank[1][0:QT, c:c + 1], cnt[:, c * QT:(c + 1) * QT], ones[:, 0:1], start=True, stop=True)
            last.then_inc(tile_cnts, 1)
            pe.wait_ge(tile_cnts_sb, 1)
            for c in range(QC):
                for b in range(c):
                    nc.tensor.matmul(bank[2][0:QT, c:c + 1], ones[0:QT, 0:QT], tile_cnt[0:QT, b:b + 1], start=(b == 0), stop=False)
                last = nc.tensor.matmul(bank[2][0:QT, c:c + 1], before[0:QT, 0:QT], tile_cnt[0:QT, c:c + 1], start=(c == 0), stop=True)
            last.then_inc(starts, 1)
            pe.wait_ge(windows_f, 1)
            for win, b in ((win_sf, 3), (win_df, 4)):
                for c in range(QC):
                    last = nc.tensor.transpose(bank[b][:, c * QT:(c + 1) * QT], win[0:QT, c, :], ident[0:QT, 0:QT])
            last.then_inc(windows_T, 1)
            pe.wait_ge(held_rows, 1)
            nc.tensor.matmul(bank[5][:, 0:1], ones[:], held[:], start=True, stop=True).then_inc(held_sum, 1)
            pe.wait_ge(w_loaded, 16 * W_LOADS)
            pe.wait_ge(ready, 1)
            general_tensor(pe, 0, D)

            def sums(n, g, made, agg):
                k = g.slot(2)
                wait(pe, made, g.done())
                wait(pe, landed[g.slot(4)], gathered(n, g))
                for j in range(J):
                    last = nc.tensor.matmul(bank[k][:, j * D:(j + 1) * D], onehot[k][:, j, :], gath[g.slot(4)][:, j, 0:D],
                                            start=True, stop=True)
                last.then_inc(agg, 1)

            def conv(group_of):
                if g := group_of(0):
                    wait(pe, a_sum, g.freed(2))
                    sums(0, g, a_oh, a_agg)
                if g := group_of(2):
                    wait(pe, a_scaled, g.done())
                    wait(pe, a_trc, g.done() - 1)
                    for j in range(J):
                        last = nc.tensor.transpose(bank[2][:, j * P:(j + 1) * P], a_s[g.slot(2)][:, j * D:(j + 1) * D], ident[:])
                    last.then_inc(a_tr, 1)
                if g := group_of(3):
                    wait(pe, a_trc, g.done())
                    wait(pe, a_relu, g.done() - 1)
                    for h in range(2):
                        last = nc.tensor.matmul(bank[3 + h][:], w1_sb[:, h * P:(h + 1) * P], a_T[g.slot(2)], start=True, stop=True)
                    last.then_inc(a_hid, 1)
                if g := group_of(4):
                    k = g.slot(2)
                    wait(pe, a_relu, g.done())
                    wait(pe, a_gs, g.freed(2))
                    for j in range(J):
                        for h, rows in enumerate((a_h0, a_h1)):
                            last = nc.tensor.matmul(bank[5 + k][:, j * D:(j + 1) * D], rows[k][:, j * P:(j + 1) * P],
                                                    w2_sb[:, h, :], start=(h == 0), stop=(h == 1))
                    last.then_inc(a_out, 1)

            run_pass(pe, conv, 4)
            pe.wait_ge(a_gs, NG)
            general_tensor(pe, 1, D)

            def norm(group_of):
                if g := group_of(0):
                    wait(pe, n_zz, g.freed(2))
                    sums(1, g, n_oh, n_agg)
                if g := group_of(3):
                    k = g.slot(2)
                    wait(pe, n_yy, g.done())
                    wait(pe, n_trc, g.freed(2))
                    for j in range(J):
                        last = nc.tensor.transpose(bank[2 + k][:, j * P:(j + 1) * P], n_y[g.slot(4)][:, j * D:(j + 1) * D], ident[:])
                    last.then_inc(n_tr, 1)
                if g := group_of(5):
                    wait(pe, n_mc, g.freed(2))
                    wait(pe, n_trc, g.done())
                    for j in range(J):
                        last = nc.tensor.matmul(bank[4 + 2 * g.slot(2) + j // 2][:, (j % 2) * DM:(j % 2 + 1) * DM],
                                                n_T[g.slot(4)][:, j * P:(j + 1) * P], wm_sb[:], start=True, stop=True)
                    last.then_inc(n_mm, 1)

            run_pass(pe, norm, 5)
            pe.wait_ge(n_mc, NG)
            general_tensor(pe, 2, DM)

            def gru(group_of):
                if g := group_of(3):
                    k = g.slot(2)
                    y, a = c_y[g.slot(4)], c_a[k]
                    wait(pe, c_iny[g.slot(4)], g.dma(4))
                    wait(pe, c_rs, g.done() - 1)
                    nc.tensor.matmul(bank[2][:], whh_sb[:, 0:D], y, start=True, stop=False)
                    wait(pe, c_aT, g.done())
                    nc.tensor.matmul(bank[2][:], wih_sb[:, 0:D], a, start=False, stop=True).then_inc(c_pr, 1)
                    wait(pe, c_t1, g.done() - 1)
                    nc.tensor.matmul(bank[4][:], whh_sb[:, 2 * D:3 * D], y, start=True, stop=True).then_inc(c_ph, 1)
                    wait(pe, c_t2, g.done() - 1)
                    nc.tensor.matmul(bank[5][:], wih_sb[:, 2 * D:3 * D], a, start=True, stop=True).then_inc(c_pi, 1)
                    wait(pe, c_zs, g.done() - 1)
                    nc.tensor.matmul(bank[3][:], whh_sb[:, D:2 * D], y, start=True, stop=False)
                    nc.tensor.matmul(bank[3][:], wih_sb[:, D:2 * D], a, start=False, stop=True).then_inc(c_pz, 1)
                if g := group_of(1):
                    k = g.slot(2)
                    wait(pe, c_aT, g.freed(2))
                    wait(pe, c_oh, g.done())
                    wait(pe, landed[g.slot(4)], gathered(2, g))
                    for j in range(J):
                        last = nc.tensor.matmul(bank[k][:, j * P:(j + 1) * P], gath[g.slot(4)][:, j, 0:D], onehot[k][:, j, :],
                                                start=True, stop=True)
                    last.then_inc(c_agg, 1)

            run_pass(pe, gru, 3)
            for gates in (c_aT, c_rs, c_t1, c_zs):
                pe.wait_ge(gates, NG)

            def final(group_of):
                if g := group_of(2):
                    k = g.slot(4)
                    wait(pe, o_q, g.done())
                    wait(pe, o_oo, g.freed(4))
                    for j in range(J):
                        last = nc.tensor.transpose(bank[k][:, j * D:(j + 1) * D], o_u[k][:, j * P:(j + 1) * P], ident[:])
                    last.then_inc(o_tr, 1)

            run_pass(pe, final, 2)


_INS = ["x", "src", "dst", "W1", "b1", "W2", "b2", "W_msg", "b_msg", "W_att", "b_att", "W_ih", "b_ih", "W_hh", "b_hh", "gamma", "beta"]


def kernel(**inputs):
    import concourse.bacc as bacc
    from concourse.bass_utils import run_bass_kernel_spmd

    a = {k.split("gnn_")[-1]: np.asarray(v) for k, v in inputs.items()}
    x = np.zeros((NP, D), a["x"].dtype)
    x[:N] = a["x"]
    x = np.ascontiguousarray(x.reshape(NG, J, P, D).transpose(0, 2, 1, 3)).reshape(NG, P, J * D)
    src, dst = np.zeros(EL, a["src"].dtype), np.full(EL, PAD_DST, a["dst"].dtype)
    src[:E], dst[:E] = a["src"], a["dst"]

    def columns(v):
        return np.ascontiguousarray(v.reshape(-1, P).T)

    arrays = {
        "x": x, "src": src, "dst": dst, "W1": a["W1"], "b1": columns(a["b1"]), "W2": a["W2"], "b2": a["b2"],
        "W_msg": a["W_msg"], "b_msg": a["b_msg"], "W_att": a["W_att"], "b_att": a["b_att"],
        "W_ih": np.ascontiguousarray(a["W_ih"].T), "b_ih": columns(a["b_ih"]),
        "W_hh": np.ascontiguousarray(a["W_hh"].T), "b_hh": columns(a["b_hh"]),
        "gamma": columns(a["gamma"]), "beta": columns(a["beta"]),
    }
    nc = bacc.Bacc("TRN2", target_bir_lowering=False, num_devices=1)
    args = [nc.dram_tensor(f"in_{k}", arrays[k].shape, mybir.dt.from_np(arrays[k].dtype), kind="ExternalInput").ap() for k in _INS]
    result = nc.dram_tensor("out_y", [NG, P, J * D], F32, kind="ExternalOutput").ap()
    build_gnn(nc, *args, result)
    r = run_bass_kernel_spmd(nc, [{f"in_{k}": np.ascontiguousarray(arrays[k]) for k in _INS}], core_ids=[0])
    y = r.results[0]["out_y"].reshape(NG, P, J, D).transpose(0, 2, 1, 3).reshape(NP, D)
    return np.ascontiguousarray(y[:N])
```

```python
from contextlib import ExitStack

import concourse.bass as bass
import numpy as np
from concourse import mybir

N = 50000
E = 25000
D = 128
P = 128
J = 4
GN = J * P
NG = -(-N // GN)
NP = NG * GN
NT = NG * J
TAIL = N - (NG - 1) * GN
U = 4
KEPT = 54
FREE = NG - KEPT
HS = 7
HU = 2 * HS
ET = -(-E // P)
EP = ET * P
EL = EP + P
QC = 4
QT = NT // QC
DM = D + 2
PAD_DST = 65535
SKIP = 1 << 20
SURE = 1e30
LN_EPS = 1e-5
BN_EPS = 1e-5

ALU = mybir.AluOpType
ACT = mybir.ActivationFunctionType
AX_X = mybir.AxisListType.X
F32 = mybir.dt.float32
I32 = mybir.dt.int32
F16 = mybir.dt.float16
BF16 = mybir.dt.bfloat16


class Group:

    def __init__(self, i, c, kept=None):
        self.i, self.c = i, c
        self.index = i * U + c
        self.fixed = isinstance(i, int)
        self.kept = self.index >= FREE if self.fixed else kept

    def slot(self, k):
        return self.c % k

    def done(self):
        return self.i * U + (self.c + 1)

    def freed(self, k):
        return self.i * U + (self.c + 1 - k)

    def dma(self, k, n=1):
        return self.i * (16 * n * (U // k)) + 16 * n * (self.c // k + 1)

    def dma_freed(self, k, n=1):
        return self.i * (16 * n * (U // k)) + 16 * n * (self.c // k)


def groups_of_slot(u, k):
    return len(range(u, NG, k))


def wait_all_dmas(eng, slots, n=1, groups=NG):
    for u, sem in enumerate(slots):
        eng.wait_ge(sem, 16 * n * len(range(u, groups, len(slots))))


def wait(eng, sem, value):
    if isinstance(value, int) and value <= 0:
        return
    eng.wait_ge(sem, value)


def in_register(eng, value):
    return value if isinstance(value, int) else eng.to_reg(value)


def run_pass(eng, step, lag, kept_only=False):
    def at(i, u, kept=None):
        def group_of(stage_lag):
            g = Group(i, u - stage_lag, kept)
            return None if g.fixed and not (FREE if kept_only else 0) <= g.index < NG else g
        return group_of

    first, border, last = -(-(lag + U) // U), FREE // U, NG // U
    if not kept_only:
        for t in range(first * U):
            step(at(t // U, t % U))
        with eng.Fori(first, border) as i:
            for u in range(U):
                step(at(i, u, False))
    for t in range(border * U, (border + first) * U):
        step(at(t // U, t % U))
    with eng.Fori(border + first, last) as i:
        for u in range(U):
            step(at(i, u, True))
    for t in range(last * U, NG + lag):
        step(at(t // U, t % U))


def build_gnn(nc, x, src, dst, w1, b1, w2, b2, wmsg, bmsg, watt, batt, wih, bih, whh, bhh, gamma, beta, out):
    ctx = ExitStack()
    with ctx:
        def sb(name, shape, dt=F32):
            return ctx.enter_context(nc.sbuf_tensor(name, shape, dt))

        def sem(name):
            return ctx.enter_context(nc.semaphore(name))

        def sems(name, k):
            return [sem(f"{name}{u}") for u in range(k)]

        XP = nc.dram_tensor("XP", [NG, P, J * D], F32).ap()
        G2 = nc.dram_tensor("G2", [NG, P, J * D], F32).ap()
        MT = nc.dram_tensor("MT", [NG, P, J * DM], F32).ap()
        SUM = nc.dram_tensor("SUM", [NG, P, J * D], F32).ap()
        SUMM = nc.dram_tensor("SUMM", [NG, P, J * DM], F32).ap()
        OWN = nc.dram_tensor("OWN", [NG, P, J * D], F32).ap()
        YT = nc.dram_tensor("YT", [NG, P, GN], F32).ap()
        HT = nc.dram_tensor("HT", [NG, P, GN], F32).ap()
        AD = nc.dram_tensor("AD", [NG, P, J], F32).ap()
        xp_rows = XP.rearrange("g p (j d) -> (g p j) d", d=D)
        g2_rows = G2.rearrange("g p (j d) -> (g p j) d", d=D)
        mt_rows = MT.rearrange("g p (j d) -> (g p j) d", d=DM)
        sum_rows = SUM.rearrange("g p (j d) -> (g p j) d", d=D)
        summ_rows = SUMM.rearrange("g p (j d) -> (g p j) d", d=DM)

        def group_of_table(table, g):
            return table[bass.ds(g.index, 1)].rearrange("a p n -> (a p) n")

        bank = [ctx.enter_context(nc.psum_tensor(f"bank{b}", [P, 512], F32)) for b in range(8)]

        bank_r, bank_n = (bank[2], bank[6]), (bank[5], bank[7])

        ident = sb("ident", [P, P])
        ones = sb("ones", [P, P])
        scale_diag = sb("scale_diag", [P, P])
        before = sb("before", [P, P])
        after = sb("after", [P, P])
        col_n = sb("col_n", [P, P])
        part_n = sb("part_n", [P, 1])
        tile_h = sb("tile_h", [P, NT], F16)
        tile_base = sb("tile_base", [P, NT])
        sum_row = sb("sum_row", [P, NT])
        w1_sb = sb("w1_sb", [P, 2 * P])
        w2_sb = sb("w2_sb", [P, 2, D])
        wm_sb = sb("wm_sb", [P, DM])
        wih_sb = sb("wih_sb", [P, 3 * D])
        whh_sb = sb("whh_sb", [P, 3 * D])
        b1_sb = sb("b1_sb", [P, 2])
        bih_sb = sb("bih_sb", [P, 3])
        bhh_sb = sb("bhh_sb", [P, 3])
        brz_sb = sb("brz_sb", [P, 2])
        gb_sb = sb("gb_sb", [P, 2])
        batt_sb = sb("batt_sb", [P, 1])
        b2_row = sb("b2_row", [P, D])
        bm_row = sb("bm_row", [P, DM])
        eps_sb = sb("eps_sb", [P, 2])

        ROWI = sb("ROWI", [P, NT], I32)
        LOC = sb("LOC", [P, NT])
        DINV = sb("DINV", [P, NT])
        slow = sb("slow", [P, 1])
        fast = sb("fast", [P, 1])
        slow_i = sb("slow_i", [P, 1], I32)

        def several(name, n, shape, dt=F32):
            return [sb(f"{name}{u}", shape, dt) for u in range(n)]

        zeros = sb("zeros", [P, J * DM])
        e_src = sb("e_src", [P, ET], I32)
        e_dst = sb("e_dst", [P, ET], I32)
        e_dstf = sb("e_dstf", [P, ET])
        e_rowf = sb("e_rowf", [P, ET])
        one_src = sb("one_src", [P, 1], I32)
        one_tab = sb("one_tab", [P, 1], I32)
        one_out = sb("one_out", [P, 1], I32)
        one_f = sb("one_f", [P, 2])
        e_col = sb("e_col", [P, P])
        e_same = sb("e_same", [P, P])
        e_junk = sb("e_junk", [P, P])
        e_msg = sb("e_msg", [P, DM])
        e_tgt = sb("e_tgt", [P, DM])
        e_sum = sb("e_sum", [P, DM])
        e_new = sb("e_new", [P, DM])
        e_att = sb("e_att", [P, 2])

        def two(name, shape, dt=F32):
            return [sb(f"{name}{u}", shape, dt) for u in range(2)]

        rowi = several("rowi", 2, [P, 2 * J], I32)
        scl = several("scl", 4, [P, J])
        scl2 = several("scl2", 4, [P, J])
        loc_g = several("loc_g", 2, [P, J])
        la = several("la", 2, [P, J])
        lg = several("lg", 2, [P, J])
        att = several("att", 2, [P, J])
        ad_out = several("ad_out", 4, [P, J])
        st6 = several("st6", 4, [P, J, 6])
        st_s = several("st_s", 4, [P, J])
        st_d = several("st_d", 4, [P, J])
        st_v = several("st_v", 4, [P, J])
        st_q = several("st_q", 4, [P, J])
        st_r = several("st_r", 4, [P, J])
        st_m = several("st_m", 4, [P, J])
        hsum = sb("hsum", [P, NG])
        hsq = sb("hsq", [P, NG])
        bn = sb("bn", [P, 8])

        gath = several("gath", 4, [P, J, DM])
        onehot = several("onehot", 2, [P, J, P])

        keep = sb("keep", [P, KEPT * GN])

        def kept(g, at=0, n=GN):
            return keep[:, bass.ds((g.index - FREE) * GN + at, n)]

        first_steps = ExitStack()

        def early(name, shape, dt=F32):
            return first_steps.enter_context(nc.sbuf_tensor(name, shape, dt))

        dst_e = early("dst_e", [P, ET], I32)
        src_e = early("src_e", [P, ET], I32)
        hi_i = early("hi_i", [P, ET], I32)
        lo_i = early("lo_i", [P, ET], I32)
        hi_f = early("hi_f", [P, ET])
        lo_f = early("lo_f", [P, ET])
        oh_hi = early("oh_hi", [P, HS, NT], BF16)
        oh_lo = early("oh_lo", [P, HS, P], BF16)
        cnt = early("cnt", [P, NT])
        deg = early("deg", [P, NT])
        root = early("root", [P, NT])
        t_a = early("t_a", [P, NT])
        t_b = early("t_b", [P, NT])
        tile_cnt = early("tile_cnt", [P, QC])
        start_i = early("start_i", [P, QC], I32)
        win_src = early("win_src", [P, QC, P], I32)
        win_dst = early("win_dst", [P, QC, P], I32)
        win_t = early("win_t", [P, QC, P], I32)
        win_u = early("win_u", [P, QC, P], I32)
        win_sf = early("win_sf", [P, QC, P])
        win_df = early("win_df", [P, QC, P])
        held = early("held", [P, 1])
        first_steps.close()

        pages = several("page", 28, [P, J * DM])[::-1]

        def names(*counts):
            left = iter(pages)
            return [[next(left)[:, 0:GN] for _ in range(n)] for n in counts]

        s_x, s_o = names(4, 4)
        a_x, a_xb, a_v, a_s, a_T, a_h0, a_h1, a_g, a_r = names(4, 4, 2, 2, 2, 2, 2, 4, 4)
        n_r, n_z, n_y, n_T = names(4, 4, 4, 4)
        n_m = pages[16:20]
        c_y, c_ad, c_h, c_a, c_r, c_z, c_u, c_n, c_t, c_d, c_e, c_sq, c_junk = names(4, 4, 4, 2, 2, 2, 2, 2, 1, 1, 2, 1, 1)
        o_h, o_y, o_t, o_o = names(4, 4, 4, 4)

        loaded = sem("loaded")
        w_loaded = sem("w_loaded")
        consts = sem("consts")
        zeroed = sem("zeroed")
        oh_ready = sem("oh_ready")
        oh_used = sem("oh_used")
        deg_plus = sem("deg_plus")
        rooted = sem("rooted")
        cnt_copied = sem("cnt_copied")
        tile_cnts = sem("tile_cnts")
        tile_cnts_sb = sem("tile_cnts_sb")
        starts = sem("starts")
        starts_sb = sem("starts_sb")
        windows = sem("windows")
        windows_f = sem("windows_f")
        windows_T = sem("windows_T")
        held_rows = sem("held_rows")
        held_sum = sem("held_sum")
        dinv_ready = sem("dinv_ready")
        ready = sem("ready")
        dchain = sem("dchain")

        def gathered(n, g):
            return g.dma(4, J) + 16 * J * n * groups_of_slot(g.slot(4), 4)

        block = ctx.enter_context(nc.Block())

        gen = {k: sem("q_" + k) for k in "clear idx colT rows rows2 msg same prod att attd new out place total".split()}

        s_in, s_st = sems("s_in", 4), sems("s_st", 4)
        s_dd, s_done, s_half, kept_in = sem("s_dd"), sem("s_done"), sem("s_half"), sem("kept_in")
        landed, idx = sems("landed", 4), sem("idx")
        a_in, a_st = sems("a_in", 4), sems("a_st", 4)
        a_oh, a_agg, a_xbs, a_sum, a_scaled, a_tr, a_trc, a_hid, a_relu, a_out, a_gs, a_rs = (
            sem("a_" + k) for k in "oh agg xb sum scaled tr trc hid relu out g r".split())
        n_in, n_st = sems("n_in", 4), sems("n_st", 4)
        n_oh, n_agg, n_dd, n_zz, n_s6, n_sd, n_dq, n_var, n_root, n_rs, n_yy, n_tr, n_trc, n_mm, n_mc, n_ad, n_hn, n_hk = (
            sem("n_" + k) for k in "oh agg dd zz s6 sd dq var root rs yy tr trc mm mc ad hn hk".split())
        c_iny, c_ina, c_st = sems("c_iny", 4), sems("c_ina", 4), sems("c_st", 4)
        c_dd, c_las, c_ls, c_at, c_wt, c_oh, c_agg, c_aT, c_pr, c_pz, c_ph, c_pi, c_rs, c_zs, c_t1, c_t2, c_ns, c_ds, c_zd, c_hh, c_sqs = (
            sem("c_" + k) for k in "dd las ls at wt oh agg aT pr pz ph pi rs zs t1 t2 ns d zd hh sqs".split())
        bn_v, bn_r, bn_ok = sem("bn_v"), sem("bn_r"), sem("bn_ok")
        o_inh, o_iny, o_st = sems("o_inh", 4), sems("o_iny", 4), sems("o_st", 4)
        o_q, o_tr, o_s6, o_sd, o_dq, o_var, o_root, o_rs, o_oo = (sem("o_" + k) for k in "q tr s6 sd dq var root rs oo".split())

        W_LOADS = 15
        CONSTS = 9
        CLEARS = 1

        def general_clear(sp, n, table, width):
            flag = sp.value_load(slow_i[0:1, 0:1], min_val=0, max_val=1)
            with sp.If(flag > 0):
                with sp.Fori(0, NG) as g:
                    sp.dma_start(table[bass.ds(g, 1)].rearrange("a p n -> (a p) n"), zeros[:, 0:J * width])\
                      .then_inc(gen["clear"], 16)

        def general_pool(pool, n, rows, sums, width):
            q = gen
            flag = pool.value_load(slow_i[0:1, 0:1], min_val=0, max_val=1)
            with pool.If(flag > 0):
                pool.wait_ge(q["clear"], 16 * NG * (n + 1))
                last_row = pool.to_reg(NP - 1)
                with pool.Fori(0, ET) as t:
                    tiles = in_register(pool, t + (n * ET + 1))
                    pool.wait_ge(ready, 1)
                    pool.wait_ge(q["idx"], tiles)
                    pool.indirect_dma_start(e_msg[:, 0:width], None, rows, bass.IndirectOffsetOnAxis(ap=one_src[:, 0:1], axis=0),
                                            bounds_check=last_row, oob_is_err=False).then_inc(q["rows"], 16)
                    pool.indirect_dma_start(e_sum[:, 0:width], None, sums, bass.IndirectOffsetOnAxis(ap=one_tab[:, 0:1], axis=0),
                                            bounds_check=last_row, oob_is_err=False).then_inc(q["rows2"], 16)
                    if n == 2:
                        pool.indirect_dma_start(e_tgt[:, 0:width], None, rows, bass.IndirectOffsetOnAxis(ap=one_tab[:, 0:1], axis=0),
                                                bounds_check=last_row, oob_is_err=False).then_inc(q["attd"], 16)
                    pool.wait_ge(ready, 1)
                    pool.wait_ge(q["new"], tiles)
                    pool.indirect_dma_start(sums, bass.IndirectOffsetOnAxis(ap=one_out[:, 0:1], axis=0), e_new[:, 0:width], None,
                                            bounds_check=last_row, oob_is_err=False).then_inc(q["out"], 16)
                pool.wait_ge(q["out"], 16 * ET * (n + 1))

        def general_act(act, n):
            flag = act.value_load(slow_i[0:1, 0:1], min_val=0, max_val=1)
            with act.If(flag > 0):
                q = gen
                with act.Fori(0, ET) as t:
                    act.wait_ge(q["msg"], t + 1)
                    nc.scalar.activation(e_att[:, 1:2], e_att[:, 0:1], ACT.Sigmoid, bias=batt_sb[:, 0:1]).then_inc(q["att"], 1)

        def general_tensor(pe, n, width):
            flag = pe.value_load(slow_i[0:1, 0:1], min_val=0, max_val=1)
            q = gen
            with pe.If(flag > 0):
                with pe.Fori(0, ET) as t:
                    pe.wait_ge(q["idx"], t + (n * ET + 1))
                    nc.tensor.transpose(bank[5][:, 0:P], e_col[:], ident[:]).then_inc(q["colT"], 1)
                    pe.wait_ge(q["same"], t + (n * ET + 1))
                    nc.tensor.matmul(bank[6][:, 0:width], e_same[:], e_msg[:, 0:width], start=True, stop=True).then_inc(q["prod"], 1)

        def general_vector(dve, n, width, link):
            flag = dve.value_load(slow_i[0:1, 0:1], min_val=0, max_val=1)
            q = gen
            with dve.If(flag > 0):
                with dve.Fori(0, ET) as t:
                    nc.vector.tensor_copy(one_src[:], e_src[:, bass.ds(t, 1)])
                    nc.vector.tensor_copy(one_tab[:], e_dst[:, bass.ds(t, 1)])
                    nc.vector.tensor_copy(one_f[:, 0:1], e_dstf[:, bass.ds(t, 1)])
                    nc.vector.tensor_scalar(e_col[:], ones[:], e_dstf[:, bass.ds(t, 1)], None, ALU.mult).then_inc(q["idx"], 1)
                    dve.wait_ge(q["colT"], t + (n * ET + 1))
                    dve.wait_ge(q["idx"], t + (n * ET + 1))
                    nc.vector.tensor_scalar(e_same[:], bank[5][:, 0:P], one_f[:, 0:1], None, ALU.is_equal).then_inc(q["place"], 1)
                    dve.wait_ge(q["place"], t * 3 + (3 * n * ET + 1))
                    nc.vector.tensor_tensor_reduce(e_junk[:], e_same[:], after[:], 1.0, 0.0, ALU.mult, ALU.add, one_f[:, 1:2])\
                      .then_inc(q["place"], 1)
                    dve.wait_ge(q["place"], t * 3 + (3 * n * ET + 2))
                    nc.vector.scalar_tensor_tensor(one_out[:], one_f[:, 1:2], float(SKIP), e_rowf[:, bass.ds(t, 1)], ALU.mult, ALU.add)\
                      .then_inc(q["place"], 1)
                    dve.wait_ge(q["rows"], t * 16 + (16 * n * ET + 16))
                    dve.wait_ge(q["rows2"], t * 16 + (16 * n * ET + 16))
                    if n == 2:
                        dve.wait_ge(q["attd"], t * 16 + 16)
                        nc.vector.tensor_tensor(e_att[:, 0:1], e_msg[:, D:D + 1], e_tgt[:, D + 1:DM], ALU.add).then_inc(q["msg"], 1)
                        dve.wait_ge(q["msg"], t + 1)
                        dve.wait_ge(q["att"], t + 1)
                        nc.vector.tensor_scalar(e_msg[:, 0:width], e_msg[:, 0:width], e_att[:, 1:2], None, ALU.mult).then_inc(q["same"], 1)
                    else:
                        dve.wait_ge(q["place"], t * 3 + (3 * n * ET + 3))
                        nc.vector.tensor_copy(one_f[:, 1:2], one_f[:, 0:1]).then_inc(q["same"], 1)
                    dve.wait_ge(q["prod"], t + (n * ET + 1))
                    nc.vector.tensor_tensor(e_new[:, 0:width], e_sum[:, 0:width], bank[6][:, 0:width], ALU.add).then_inc(q["total"], 1)
                    dve.wait_ge(q["total"], t + (n * ET + 1))
                    if n == 2:
                        nc.vector.memset(e_new[:, D:D + 1], SURE).then_inc(q["new"], 1)
                    else:
                        nc.vector.memset(one_f[:, 1:2], 0.0).then_inc(q["new"], 1)
                    dve.wait_ge(q["out"], t * 16 + (16 * n * ET + 16))

        @block.sync
        def _(sp):
            sp.dma_start(dst_e[:], dst[0:EP].rearrange("(p k) -> p k", p=P)).then_inc(loaded, 16)
            sp.dma_start(src_e[:], src[0:EP].rearrange("(p k) -> p k", p=P)).then_inc(loaded, 16)
            for t, a in ((w1_sb, w1), (wih_sb, wih), (whh_sb, whh), (b1_sb, b1), (bih_sb, bih), (bhh_sb, bhh)):
                sp.dma_start(t[:], a).then_inc(w_loaded, 16)
            sp.dma_start(w2_sb[:], w2.rearrange("(k p) o -> p k o", k=2)).then_inc(w_loaded, 16)
            sp.dma_start(wm_sb[:, 0:D], wmsg).then_inc(w_loaded, 16)
            sp.dma_start(wm_sb[:, D:D + 1], watt[0:D]).then_inc(w_loaded, 16)
            sp.dma_start(wm_sb[:, D + 1:DM], watt[D:2 * D]).then_inc(w_loaded, 16)
            sp.dma_start(gb_sb[:, 0:1], gamma).then_inc(w_loaded, 16)
            sp.dma_start(gb_sb[:, 1:2], beta).then_inc(w_loaded, 16)
            sp.dma_start(batt_sb[:], batt.partition_broadcast(P)).then_inc(w_loaded, 16)
            sp.dma_start(b2_row[:], b2.partition_broadcast(P)).then_inc(w_loaded, 16)
            sp.wait_ge(zeroed, CLEARS)
            sp.dma_start(bm_row[:, 0:D], bmsg.partition_broadcast(P)).then_inc(w_loaded, 16)

            with sp.Fori(0, KEPT) as i:
                sp.dma_start(keep[:, bass.ds(i * GN, GN)], x[bass.ds(i + FREE, 1)].rearrange("a p n -> (a p) n")).then_inc(kept_in, 16)

            def scale(group_of):
                if (g := group_of(0)) and not g.kept:
                    k = g.slot(4)
                    wait(sp, s_done, g.freed(4))
                    sp.dma_start(s_x[k], group_of_table(x, g)).then_inc(s_in[k], 16)
                if g := group_of(3):
                    k = g.slot(4)
                    done, half = in_register(sp, g.done()), in_register(sp, g.done() - FREE)
                    wait(sp, s_done, done)
                    if g.kept:
                        wait(sp, s_half, half)
                    sp.dma_start(group_of_table(XP, g), s_o[k]).then_inc(s_st[k], 16)

            run_pass(sp, scale, 3)
            wait_all_dmas(sp, s_st)
            sp.wait_ge(ready, 1)
            general_clear(sp, 0, SUM, D)

            def conv(group_of):
                if (g := group_of(0)) and not g.kept:
                    k = g.slot(4)
                    wait(sp, a_xbs, g.freed(4))
                    sp.dma_start(a_x[k], group_of_table(x, g)).then_inc(a_in[k], 16)
                if g := group_of(6):
                    k = g.slot(4)
                    wait(sp, a_gs, g.done())
                    sp.dma_start(group_of_table(G2, g), a_g[k]).then_inc(a_st[k], 16)
                    wait(sp, a_rs, g.done())
                    sp.dma_start(group_of_table(OWN, g), a_r[k]).then_inc(a_st[k], 16)

            run_pass(sp, conv, 6)
            wait_all_dmas(sp, a_st, 2)
            general_clear(sp, 1, SUM, D)

            def norm(group_of):
                if g := group_of(0):
                    k = g.slot(4)
                    wait(sp, n_zz, g.freed(4))
                    sp.dma_start(n_r[k], group_of_table(OWN, g)).then_inc(n_in[k], 16)
                if g := group_of(7):
                    k = g.slot(4)
                    wait(sp, n_trc, g.done())
                    sp.dma_start(group_of_table(YT, g), n_T[k]).then_inc(n_st[k], 16)
                    wait(sp, n_mc, g.done())
                    sp.dma_start(group_of_table(MT, g), n_m[k][:]).then_inc(n_st[k], 16)
                    wait(sp, n_ad, g.done())
                    sp.dma_start(group_of_table(AD, g), ad_out[k][:]).then_inc(n_st[k], 16)

            run_pass(sp, norm, 7)
            wait_all_dmas(sp, n_st, 3)
            general_clear(sp, 2, SUMM, DM)

            def gru(group_of):
                if g := group_of(0):
                    k = g.slot(4)
                    wait(sp, c_las, g.freed(4))
                    sp.dma_start(c_ad[k], AD[bass.ds(g.index, 1)].rearrange("a p j -> a (p j)").to_broadcast([P, GN]))\
                      .then_inc(c_ina[k], 16)
                if g := group_of(2):
                    k = g.slot(4)
                    wait(sp, c_ds, g.freed(4))
                    wait(sp, c_pz, g.freed(4))
                    sp.dma_start(c_y[k], group_of_table(YT, g)).then_inc(c_iny[k], 16)
                if (g := group_of(7)) and not g.kept:
                    k = g.slot(4)
                    wait(sp, c_hh, g.done())
                    sp.dma_start(group_of_table(HT, g), c_h[k]).then_inc(c_st[k], 16)

            run_pass(sp, gru, 7)
            wait_all_dmas(sp, c_st, 1, FREE)
            sp.wait_ge(c_sqs, NG)

            def final(group_of):
                if g := group_of(0):
                    k = g.slot(4)
                    if not g.kept:
                        wait(sp, o_tr, g.freed(4))
                        sp.dma_start(o_h[k], group_of_table(HT, g)).then_inc(o_inh[k], 16)
                    wait(sp, o_q, g.freed(4))
                    if g.kept:
                        wait(sp, o_tr, g.freed(4))
                    sp.dma_start(o_y[k], group_of_table(YT, g)).then_inc(o_iny[k], 16)
                if g := group_of(7):
                    k = g.slot(4)
                    wait(sp, o_oo, g.done())
                    sp.dma_start(group_of_table(out, g), o_o[k]).then_inc(o_st[k], 16)

            run_pass(sp, final, 7)
            wait_all_dmas(sp, o_st)

        @block.gpsimd
        def _(pool):
            exact = dict(allow_small_or_imprecise_dtypes=True)
            nc.gpsimd.iota(tile_h[:], [[1, NT]], base=0, channel_multiplier=0, **exact).then_inc(consts, 1)
            nc.gpsimd.iota(col_n[:], [[1, P]], base=0, channel_multiplier=0, **exact).then_inc(consts, 1)
            nc.gpsimd.iota(part_n[:], [[0, 1]], base=0, channel_multiplier=1, **exact).then_inc(consts, 1)
            nc.gpsimd.iota(tile_base[:], [[P, NT]], base=0, channel_multiplier=0, **exact).then_inc(consts, 1)
            nc.gpsimd.iota(sum_row[:], [[GN, NG], [1, J]], base=0, channel_multiplier=J, **exact).then_inc(consts, 1)
            nc.gpsimd.memset(ones[:], 1.0).then_inc(consts, 1)
            pool.wait_ge(consts, 6)
            for m, op, base, step in ((ident, ALU.is_equal, 0, -1), (before, ALU.is_gt, 0, 1)):
                nc.gpsimd.affine_select(out=m[:], in_=ones[:], compare_op=op, fill=0.0, base=base,
                                        pattern=[[step, P]], channel_multiplier=-step).then_inc(consts, 1)
            nc.gpsimd.affine_select(out=after[:], in_=ones[:], compare_op=ALU.is_gt, fill=0.0, base=0,
                                    pattern=[[-1, P]], channel_multiplier=1).then_inc(consts, 1)

            pool.wait_ge(starts_sb, 1)
            for arr, win in ((src, win_src), (dst, win_dst)):
                flat = arr.rearrange("(a b) -> a b", b=1)
                for c in range(QC):
                    nc.gpsimd.indirect_dma_start(win[0:QT, c, :], None, flat,
                                                 bass.IndirectOffsetOnAxis(ap=start_i[0:QT, c:c + 1], axis=0)).then_inc(windows, 16)

            def gathers(n, table, sum_table, width, used_rows):
                last_row = pool.to_reg(NP - 1)

                def step(group_of, rows):
                    g = group_of(0)
                    k = g.slot(4)
                    pair = rowi[k // 2]
                    copied = in_register(pool, g.i * (U // 2) + (g.c // 2 + 1) + n * (NG // 2))
                    used = in_register(pool, g.freed(4))
                    if k % 2 == 0:
                        reads = in_register(pool, gathered(n, g) - 16 * J)
                        reads2 = in_register(pool, gathered(n, Group(g.i, g.c + 1)) - 16 * J)
                        pool.wait_ge(ready, 1)
                        wait(pool, landed[k], reads)
                        wait(pool, landed[k + 1], reads2)
                        nc.gpsimd.tensor_copy(pair[:], ROWI[:, bass.ds(g.index * J, 2 * J)]).then_inc(idx, 1)
                    pool.wait_ge(ready, 1)
                    if k % 2 == 0:
                        wait(pool, idx, copied)
                    wait(pool, used_rows, used)
                    for j in range(J):
                        nc.gpsimd.indirect_dma_start(gath[k][:, j, 0:width], None, rows,
                                                     bass.IndirectOffsetOnAxis(ap=pair[:, k % 2 * J + j:k % 2 * J + j + 1], axis=0),
                                                     bounds_check=last_row, oob_is_err=False).then_inc(landed[k], 16)

                flag = pool.value_load(slow_i[0:1, 0:1], min_val=0, max_val=1)
                with pool.If(flag < 1):
                    run_pass(pool, lambda group_of: step(group_of, table), 0)
                with pool.If(flag > 0):
                    run_pass(pool, lambda group_of: step(group_of, sum_table), 0)
                for u in range(4):
                    pool.wait_ge(landed[u], 16 * J * (n + 1) * groups_of_slot(u, 4))

            pool.wait_ge(ready, 1)
            wait_all_dmas(pool, s_st)
            general_pool(pool, 0, xp_rows, sum_rows, D)
            gathers(0, xp_rows, sum_rows, D, a_agg)
            wait_all_dmas(pool, a_st, 2)
            general_pool(pool, 1, g2_rows, sum_rows, D)
            pool.wait_ge(a_agg, NG)
            gathers(1, g2_rows, sum_rows, D, n_agg)
            wait_all_dmas(pool, n_st, 3)
            general_pool(pool, 2, mt_rows, summ_rows, DM)
            pool.wait_ge(n_agg, NG)
            gathers(2, mt_rows, summ_rows, DM, c_agg)

        @block.scalar
        def _(act):
            act.wait_ge(w_loaded, 16 * W_LOADS)
            act.wait_ge(deg_plus, 1)
            nc.scalar.activation(root[:], deg[:], ACT.Sqrt).then_inc(rooted, 1)
            act.wait_ge(dinv_ready, 1)
            act.wait_ge(kept_in, 16 * KEPT)

            def scale(group_of):
                if g := group_of(0):
                    k = g.slot(4)
                    wait(act, s_done, g.freed(4))
                    if g.kept:
                        wait(act, s_half, g.freed(4) - FREE)
                    nc.scalar.activation(scl[k][:], DINV[:, bass.ds(g.index * J, J)], ACT.Copy).then_inc(s_dd, 1)
                    if not g.kept:
                        wait(act, s_in[k], g.dma(4))
                    wait(act, s_st[k], g.dma_freed(4))
                    wait(act, s_dd, g.done())
                    for j in range(3 if g.kept else 0, J):
                        own = slice(j * D, (j + 1) * D)
                        last = nc.scalar.activation(s_o[k][:, own], kept(g, j * D, D) if g.kept else s_x[k][:, own],
                                                    ACT.Copy, scale=scl[k][:, j:j + 1])
                    last.then_inc(s_done, 1)

            run_pass(act, scale, 0)
            wait_all_dmas(act, s_st)

            def conv(group_of):
                if g := group_of(4):
                    k = g.slot(2)
                    wait(act, a_out, g.freed(2))
                    wait(act, a_hid, g.done())
                    for h, rows in enumerate((a_h0, a_h1)):
                        last = nc.scalar.activation(rows[k], bank[3 + h][:], ACT.Relu, bias=b1_sb[:, h:h + 1])
                    last.then_inc(a_relu, 1)
                if g := group_of(2):
                    k = g.slot(2)
                    wait(act, a_tr, g.done())
                    wait(act, a_hid, g.freed(2))
                    nc.scalar.activation(a_T[k], bank[2][:], ACT.Copy).then_inc(a_trc, 1)
                if g := group_of(1):
                    k = g.slot(2)
                    wait(act, a_sum, g.done())
                    wait(act, a_tr, g.freed(2))
                    for j in range(J):
                        last = nc.scalar.activation(a_s[k][:, j * D:(j + 1) * D], a_v[k][:, j * D:(j + 1) * D],
                                                    ACT.Copy, scale=scl[g.slot(4)][:, j:j + 1])
                    last.then_inc(a_scaled, 1)

            run_pass(act, conv, 4)
            wait_all_dmas(act, a_st, 2)

            def norm(group_of):
                if g := group_of(2):
                    k = g.slot(4)
                    wait(act, n_var, g.done())
                    nc.scalar.activation(st_q[k][:], st_v[k][:], ACT.Sqrt, bias=eps_sb[:, 0:1], scale=1.0 / D).then_inc(n_root, 1)
                if (g := group_of(6)) and g.kept:
                    wait(act, n_hn, g.done() - FREE)
                    nc.scalar.activation(kept(g), bank[6 + g.slot(2)][:], ACT.Copy).then_inc(n_hk, 1)
                if g := group_of(3):
                    k = g.slot(4)
                    wait(act, n_rs, g.done())
                    wait(act, n_tr, g.freed(4))
                    for j in range(J):
                        last = nc.scalar.activation(n_y[k][:, j * D:(j + 1) * D], n_z[k][:, j * D:(j + 1) * D], ACT.Identity,
                                                    bias=st_m[k][:, j:j + 1], scale=st_r[k][:, j:j + 1])
                    last.then_inc(n_yy, 1)
                if g := group_of(4):
                    k = g.slot(4)
                    wait(act, n_tr, g.done())
                    wait(act, n_st[k], g.dma_freed(4, 3))
                    wait(act, n_mm, g.freed(4))
                    nc.scalar.activation(n_T[k], bank[2 + g.slot(2)][:], ACT.Copy).then_inc(n_trc, 1)

            run_pass(act, norm, 6)
            wait_all_dmas(act, n_st, 3)
            general_act(act, 2)

            def gru(group_of):
                if g := group_of(4):
                    k = g.slot(2)
                    wait(act, c_pz, g.done())
                    wait(act, c_zd, g.freed(2))
                    nc.scalar.activation(c_z[k], bank[3][:], ACT.Sigmoid, bias=brz_sb[:, 1:2]).then_inc(c_zs, 1)
                if g := group_of(1):
                    k = g.slot(2)
                    wait(act, c_ls, g.done())
                    wait(act, c_wt, g.freed(2))
                    nc.scalar.activation(att[k][:], lg[k][:], ACT.Sigmoid, bias=batt_sb[:, 0:1]).then_inc(c_at, 1)
                if g := group_of(4):
                    k = g.slot(2)
                    wait(act, c_t2, g.done())
                    wait(act, c_hh, g.freed(2))
                    nc.scalar.activation(c_n[k], c_u[k], ACT.Tanh, bias=bih_sb[:, 2:3]).then_inc(c_ns, 1)
                if g := group_of(2):
                    k = g.slot(2)
                    wait(act, c_agg, g.done())
                    wait(act, c_pz, g.freed(2))
                    nc.scalar.activation(c_a[k], bank[k][:], ACT.Copy).then_inc(c_aT, 1)
                if g := group_of(3):
                    k = g.slot(2)
                    wait(act, c_pr, g.done())
                    wait(act, c_t1, g.freed(2))
                    nc.scalar.activation(c_r[k], bank_r[k][:], ACT.Sigmoid, bias=brz_sb[:, 0:1]).then_inc(c_rs, 1)
                if g := group_of(1):
                    k = g.slot(4)
                    wait(act, landed[k], gathered(2, g))
                    wait(act, c_at, g.done())
                    for j in range(J):
                        rows = gath[k][:, j, 0:D]
                        last = nc.scalar.activation(rows, rows, ACT.Copy, scale=att[g.slot(2)][:, j:j + 1])
                    last.then_inc(c_wt, 1)
                if g := group_of(5):
                    k = g.slot(4)
                    wait(act, c_hh, g.done())
                    wait(act, c_sqs, g.done() - 1)
                    n = TAIL if g.fixed and g.index == NG - 1 else GN
                    nc.scalar.activation(c_sq[0][:, 0:n], kept(g, 0, n) if g.kept else c_h[k], ACT.Square,
                                         accum_out=hsq[:, bass.ds(g.index, 1)]).then_inc(c_sqs, 1)

            act.wait_ge(bn_ok, 1)
            run_pass(act, gru, 5)
            act.wait_ge(bn_v, 1)
            nc.scalar.activation(bn[:, 3:4], bn[:, 2:3], ACT.Sqrt, bias=eps_sb[:, 1:2]).then_inc(bn_r, 1)
            act.wait_ge(c_hh, NG)
            wait_all_dmas(act, c_st, 1, FREE)

            def final(group_of):
                if g := group_of(3):
                    k = g.slot(4)
                    wait(act, o_var, g.done())
                    nc.scalar.activation(st_q[k][:], st_v[k][:], ACT.Sqrt, bias=eps_sb[:, 0:1], scale=1.0 / D).then_inc(o_root, 1)
                if g := group_of(4):
                    k = g.slot(4)
                    wait(act, o_rs, g.done())
                    wait(act, o_st[k], g.dma_freed(4))
                    for j in range(J):
                        last = nc.scalar.activation(o_o[k][:, j * D:(j + 1) * D], bank[k][:, j * D:(j + 1) * D], ACT.Identity,
                                                    bias=st_m[k][:, j:j + 1], scale=st_r[k][:, j:j + 1])
                    last.then_inc(o_oo, 1)

            run_pass(act, final, 4)

        @block.vector
        def _(dve):
            count = [0]

            def link(ins):
                count[0] += 1
                ins.then_inc(dchain, 1)
                dve.wait_ge(dchain, count[0])

            nc.vector.memset(bm_row[:, D:DM], 0.0).then_inc(zeroed, 1)
            nc.vector.memset(eps_sb[:, 0:1], LN_EPS)
            link(nc.vector.memset(eps_sb[:, 1:2], BN_EPS))
            dve.wait_ge(loaded, 32)
            nc.vector.tensor_scalar(hi_i[:], dst_e[:], 7, None, ALU.logical_shift_right)
            link(nc.vector.tensor_scalar(lo_i[:], dst_e[:], P - 1, None, ALU.bitwise_and))
            nc.vector.tensor_copy(hi_f[:], hi_i[:])
            link(nc.vector.tensor_copy(lo_f[:], lo_i[:]))
            dve.wait_ge(consts, CONSTS)

            def one_hots(i):
                for c in range(HU):
                    if c % 2 == 0:
                        wait(dve, oh_used, i * HU + (c + 2 - HS))
                    s = c % HS
                    nc.vector.tensor_scalar(oh_hi[:, s, :], tile_h[:], hi_f[:, bass.ds(i * HU + c, 1)], None, ALU.is_equal)
                    nc.vector.tensor_scalar(oh_lo[:, s, :], tile_h[:, 0:P], lo_f[:, bass.ds(i * HU + c, 1)], None, ALU.is_equal)\
                      .then_inc(oh_ready, 1)

            one_hots(0)
            with dve.Fori(1, ET // HU) as i:
                one_hots(i)
            dve.wait_ge(oh_used, ET)
            nc.vector.tensor_scalar(deg[:], bank[0][:, 0:NT], 1.0, None, ALU.add).then_inc(deg_plus, 1)
            nc.vector.tensor_copy(cnt[:], bank[0][:, 0:NT]).then_inc(cnt_copied, 1)
            dve.wait_ge(rooted, 1)
            dve.wait_ge(deg_plus, 1)
            link(nc.vector.reciprocal(DINV[:], root[:]))
            link(nc.vector.tensor_tensor(t_a[:], DINV[:], DINV[:], ALU.mult))
            link(nc.vector.tensor_tensor(t_b[:], t_a[:], deg[:], ALU.mult))
            link(nc.vector.tensor_scalar(t_a[:], t_b[:], -0.5, 1.5, ALU.mult, ALU.add))
            nc.vector.tensor_tensor(DINV[:], DINV[:], t_a[:], ALU.mult).then_inc(dinv_ready, 1)
            dve.wait_ge(tile_cnts, 1)
            nc.vector.tensor_copy(tile_cnt[0:QT, :], bank[1][0:QT, 0:QC]).then_inc(tile_cnts_sb, 1)
            dve.wait_ge(starts, 1)
            nc.vector.tensor_copy(start_i[0:QT, :], bank[2][0:QT, 0:QC]).then_inc(starts_sb, 1)
            dve.wait_ge(windows, 16 * 2 * QC)
            q = slice(0, QT)

            def table_row(to, of, tmp):
                link(nc.vector.tensor_scalar(to, of, P - 1, 2, ALU.bitwise_and, ALU.logical_shift_left))
                link(nc.vector.tensor_scalar(tmp, of, 7, J - 1, ALU.logical_shift_right, ALU.bitwise_and))
                link(nc.vector.tensor_tensor(to, to, tmp, ALU.bitwise_or))
                link(nc.vector.tensor_scalar(tmp, of, 9, 9, ALU.logical_shift_right, ALU.logical_shift_left))
                link(nc.vector.tensor_tensor(to, to, tmp, ALU.bitwise_or))

            table_row(win_t[q], win_src[q], win_u[q])
            nc.vector.tensor_copy(win_sf[q], win_t[q])
            nc.vector.tensor_copy(win_df[q], win_dst[q]).then_inc(windows_f, 1)
            dve.wait_ge(windows_T, 1)
            link(nc.vector.tensor_tensor(LOC[:], bank[4][:, 0:NT], tile_base[:], ALU.subtract))
            link(nc.vector.tensor_scalar(t_a[:], LOC[:], 0.0, None, ALU.is_ge))
            link(nc.vector.scalar_tensor_tensor(t_b[:], LOC[:], float(P), t_a[:], ALU.is_lt, ALU.mult))
            nc.vector.tensor_reduce(held[:], t_b[:], AX_X, ALU.add).then_inc(held_rows, 1)
            link(nc.vector.scalar_tensor_tensor(t_a[:], t_b[:], -float(SKIP), bank[3][:, 0:NT], ALU.mult, ALU.add))
            link(nc.vector.tensor_scalar(t_a[:], t_a[:], float(SKIP), None, ALU.add))
            dve.wait_ge(held_sum, 1)
            nc.vector.tensor_scalar(slow[:], bank[5][:, 0:1], float(E), None, ALU.not_equal)
            nc.vector.tensor_scalar(slow_i[:], bank[5][:, 0:1], float(E), None, ALU.not_equal)
            link(nc.vector.tensor_scalar(fast[:], bank[5][:, 0:1], float(E), None, ALU.is_equal))
            link(nc.vector.tensor_scalar(t_b[:], sum_row[:], slow[:, 0:1], None, ALU.mult))
            link(nc.vector.scalar_tensor_tensor(ROWI[:], t_a[:], fast[:, 0:1], t_b[:], ALU.mult, ALU.add))
            link(nc.vector.tensor_scalar(held[:], part_n[:], slow[:, 0:1], None, ALU.mult))
            link(nc.vector.tensor_scalar(LOC[:], LOC[:], fast[:, 0:1], held[:, 0:1], ALU.mult, ALU.add))
            dve.wait_ge(w_loaded, 16 * W_LOADS)
            nc.vector.tensor_tensor(brz_sb[:], bih_sb[:, 0:2], bhh_sb[:, 0:2], ALU.add).then_inc(bn_ok, 1)
            table_row(e_src[:], src_e[:], hi_i[:])
            table_row(e_dst[:], dst_e[:], hi_i[:])
            nc.vector.tensor_copy(e_rowf[:], e_dst[:])
            link(nc.vector.tensor_copy(e_dstf[:], dst_e[:]))
            for rows in (*gath, zeros, e_msg, e_sum, e_tgt):
                nc.vector.memset(rows[:], 0.0)
            nc.vector.memset(held[:], 0.0).then_inc(ready, 1)

            def scale(group_of):
                if g := group_of(0):
                    k = g.slot(4)
                    wait(dve, s_dd, g.done())
                    wait(dve, s_st[k], g.dma_freed(4))
                    for j in range(3):
                        last = nc.vector.tensor_scalar(s_o[k][:, j * D:(j + 1) * D], kept(g, j * D, D),
                                                       scl[k][:, j:j + 1], None, ALU.mult)
                    last.then_inc(s_half, 1)

            dve.wait_ge(kept_in, 16 * KEPT)
            run_pass(dve, scale, 0, kept_only=True)
            general_vector(dve, 0, D, link)
            wait_all_dmas(dve, s_st)

            tile_of_slot = col_n[:].unsqueeze(1).to_broadcast([P, J, P])
            row_b2 = b2_row[:].unsqueeze(1).to_broadcast([P, J, D])

            def by_tile(rows):
                return rows.rearrange("p (j d) -> p j d", j=J)

            def one_hot(g, used, made):
                wait(dve, used, g.freed(2))
                nc.vector.tensor_tensor(onehot[g.slot(2)][:], tile_of_slot,
                                        LOC[:, bass.ds(g.index * J, J)].unsqueeze(2).to_broadcast([P, J, P]),
                                        ALU.is_equal).then_inc(made, 1)

            def conv(group_of):
                if g := group_of(0):
                    one_hot(g, a_agg, a_oh)
                if g := group_of(1):
                    k = g.slot(4)
                    wait(dve, a_scaled, g.freed(4))
                    nc.vector.tensor_copy(scl[k][:], DINV[:, bass.ds(g.index * J, J)]).then_inc(s_dd, 1)
                    if not g.kept:
                        wait(dve, a_in[k], g.dma(4))
                    wait(dve, s_dd, g.done() + NG)
                    wait(dve, a_agg, g.done())
                    wait(dve, a_scaled, g.freed(2))
                    for j in range(J):
                        own = slice(j * D, (j + 1) * D)
                        rows = kept(g, j * D, D) if g.kept else a_x[k][:, own]
                        last = nc.vector.scalar_tensor_tensor(a_v[g.slot(2)][:, own], rows, scl[k][:, j:j + 1],
                                                              bank[g.slot(2)][:, own], ALU.mult, ALU.add)
                    last.then_inc(a_sum, 1)
                if g := group_of(5):
                    k = g.slot(4)
                    nc.vector.tensor_copy(scl2[k][:], DINV[:, bass.ds(g.index * J, J)]).then_inc(n_dd, 1)
                    wait(dve, a_out, g.done())
                    wait(dve, a_st[k], g.dma_freed(4, 2))
                    nc.vector.tensor_tensor(by_tile(a_g[k]), by_tile(bank[5 + g.slot(2)][:]),
                                            DINV[:, bass.ds(g.index * J, J)].unsqueeze(2).to_broadcast([P, J, D]),
                                            ALU.mult).then_inc(a_gs, 1)
                    wait(dve, a_xbs, g.done())
                    wait(dve, n_dd, g.done())
                    wait(dve, a_gs, g.done())
                    for j in range(J):
                        own = slice(j * D, (j + 1) * D)
                        last = nc.vector.scalar_tensor_tensor(a_r[k][:, own], a_g[k][:, own], scl2[k][:, j:j + 1],
                                                              a_xb[k][:, own], ALU.mult, ALU.add)
                    last.then_inc(a_rs, 1)
                if g := group_of(1):
                    k = g.slot(4)
                    wait(dve, a_rs, g.freed(4))
                    nc.vector.tensor_tensor(by_tile(a_xb[k]), by_tile(kept(g) if g.kept else a_x[k]), row_b2, ALU.add).then_inc(a_xbs, 1)

            run_pass(dve, conv, 5)
            general_vector(dve, 1, D, link)
            wait_all_dmas(dve, a_st, 2)

            def norm(group_of):
                if g := group_of(1):
                    k = g.slot(4)
                    wait(dve, n_in[k], g.dma(4))
                    wait(dve, n_agg, g.done())
                    wait(dve, n_dd, g.done() + NG)
                    wait(dve, n_yy, g.freed(4))
                    for j in range(J):
                        own = slice(j * D, (j + 1) * D)
                        last = nc.vector.scalar_tensor_tensor(n_z[k][:, own], bank[g.slot(2)][:, own], scl2[k][:, j:j + 1],
                                                              n_r[k][:, own], ALU.mult, ALU.add)
                    last.then_inc(n_zz, 1)
                if g := group_of(0):
                    one_hot(g, n_agg, n_oh)
                    k = g.slot(4)
                    wait(dve, n_zz, g.freed(4))
                    nc.vector.tensor_copy(scl2[k][:], DINV[:, bass.ds(g.index * J, J)]).then_inc(n_dd, 1)
                if g := group_of(6):
                    k = g.slot(4)
                    wait(dve, n_mm, g.done())
                    wait(dve, n_st[k], g.dma_freed(4, 3))
                    m = by_tile(n_m[k][:])
                    for h in range(2):
                        last = nc.vector.tensor_tensor(m[:, 2 * h:2 * h + 2, :],
                                                       bank[4 + h][:, 0:2 * DM].rearrange("p (j d) -> p j d", j=2),
                                                       bm_row[:].unsqueeze(1).to_broadcast([P, 2, DM]), ALU.add)
                    last.then_inc(n_mc, 1)
                if g := group_of(1):
                    k = g.slot(4)
                    wait(dve, n_zz, g.done())
                    row_stats(g, lambda j: n_z[k][:, j * D:(j + 1) * D], n_s6, n_yy)
                normaliser(group_of(1), group_of(2), n_s6, n_sd, n_root, n_dq, n_var, n_rs)
                if g := group_of(6):
                    k = g.slot(4)
                    wait(dve, n_mc, g.done())
                    nc.vector.tensor_copy(ad_out[k][:], by_tile(n_m[k][:])[:, :, D + 1:DM].rearrange("p j a -> p (j a)")).then_inc(n_ad, 1)

            def row_stats(g, rows_of, s6, used):
                k = g.slot(4)
                wait(dve, used, g.freed(4))
                for j in range(J):
                    last = nc.vector.bn_stats(st6[k][:, j, :], rows_of(j))
                last.then_inc(s6, 1)

            def normaliser(g, e, s6, sd, rooted_, dq, var, rs):
                if e:
                    k = e.slot(4)
                    wait(dve, rooted_, e.done())
                    nc.vector.reciprocal(st_r[k][:], st_q[k][:]).then_inc(dq, 1)
                if g:
                    k = g.slot(4)
                    wait(dve, s6, g.done())
                    part = [st6[k][:, :, n:n + 1].rearrange("p j a -> p (j a)") for n in range(6)]
                    nc.vector.tensor_tensor(st_d[k][:], part[1], part[4], ALU.subtract).then_inc(sd, 1)
                    nc.vector.tensor_tensor(st_s[k][:], part[1], part[4], ALU.add)
                    nc.vector.tensor_tensor(st_v[k][:], part[2], part[5], ALU.add)
                    wait(dve, sd, g.i * (2 * U) + (2 * g.c + 1))
                    nc.vector.tensor_tensor(st_d[k][:], st_d[k][:], st_d[k][:], ALU.mult).then_inc(sd, 1)
                if e:
                    k = e.slot(4)
                    wait(dve, dq, e.done())
                    nc.vector.scalar_tensor_tensor(st_m[k][:], st_s[k][:], -0.5, st_r[k][:], ALU.mult, ALU.mult).then_inc(rs, 1)
                if g:
                    k = g.slot(4)
                    wait(dve, sd, g.i * (2 * U) + (2 * g.c + 2))
                    nc.vector.scalar_tensor_tensor(st_v[k][:], st_d[k][:], D / 4.0, st_v[k][:], ALU.mult, ALU.add).then_inc(var, 1)

            run_pass(dve, norm, 6)
            general_vector(dve, 2, DM, link)
            wait_all_dmas(dve, n_st, 3)
            dve.wait_ge(n_hk, KEPT)

            def gru(group_of):
                if g := group_of(1):
                    one_hot(g, c_agg, c_oh)
                if g := group_of(0):
                    k = g.slot(2)
                    wait(dve, c_las, g.freed(2))
                    nc.vector.tensor_copy(loc_g[k][:], LOC[:, bass.ds(g.index * J, J)]).then_inc(c_dd, 1)
                if g := group_of(3):
                    k = g.slot(2)
                    wait(dve, c_rs, g.done())
                    if not g.kept:
                        wait(dve, c_ph, g.done())
                    wait(dve, c_t2, g.done() - 1)
                    nc.vector.scalar_tensor_tensor(c_t[0], kept(g) if g.kept else bank[4][:], bhh_sb[:, 2:3], c_r[k],
                                                   ALU.add, ALU.mult).then_inc(c_t1, 1)
                if g := group_of(0):
                    k = g.slot(2)
                    wait(dve, c_ina[g.slot(4)], g.dma(4))
                    wait(dve, c_dd, g.done())
                    wait(dve, c_las, g.done() - 1)
                    by_row = c_ad[g.slot(4)].rearrange("p (n j) -> p n j", j=J)
                    for j in range(J):
                        last = nc.vector.scalar_tensor_tensor(c_junk[0][:, j * P:(j + 1) * P], col_n[:], loc_g[k][:, j:j + 1],
                                                              by_row[:, :, j:j + 1].rearrange("p n a -> p (n a)"), ALU.is_equal, ALU.mult,
                                                              accum_out=la[k][:, j:j + 1])
                    last.then_inc(c_las, 1)
                if g := group_of(3):
                    k = g.slot(2)
                    wait(dve, c_t1, g.done())
                    wait(dve, c_pi, g.done())
                    wait(dve, c_ns, g.freed(2))
                    nc.vector.tensor_tensor(c_u[k], c_t[0], bank_n[k][:], ALU.add).then_inc(c_t2, 1)
                if g := group_of(4):
                    k = g.slot(2)
                    wait(dve, c_ns, g.done())
                    wait(dve, c_zd, g.done() - 1)
                    nc.vector.tensor_tensor(c_d[0], c_y[g.slot(4)], c_n[k], ALU.subtract).then_inc(c_ds, 1)
                if g := group_of(0):
                    k = g.slot(2)
                    wait(dve, c_las, g.done())
                    wait(dve, landed[g.slot(4)], gathered(2, g))
                    wait(dve, c_at, g.freed(2))
                    nc.vector.tensor_tensor(lg[k][:], la[k][:],
                                            gath[g.slot(4)][:, :, D:D + 1].rearrange("p j a -> p (j a)"), ALU.add).then_inc(c_ls, 1)
                if g := group_of(4):
                    k = g.slot(2)
                    wait(dve, c_ds, g.done())
                    wait(dve, c_zs, g.done())
                    nc.vector.tensor_tensor(c_e[k], c_d[0], c_z[k], ALU.mult).then_inc(c_zd, 1)
                    wait(dve, c_zd, g.done())
                    if not g.kept:
                        wait(dve, c_st[g.slot(4)], g.dma_freed(4))
                        wait(dve, c_sqs, g.freed(4))
                    n = TAIL if g.fixed and g.index == NG - 1 else GN
                    if n < GN:
                        nc.vector.tensor_tensor(kept(g, n, GN - n), c_e[k][:, n:GN], c_n[k][:, n:GN], ALU.add)
                    h = kept(g, 0, n) if g.kept else c_h[g.slot(4)]
                    nc.vector.scalar_tensor_tensor(h, c_e[k][:, 0:n], 1.0, c_n[k][:, 0:n], ALU.mult, ALU.add,
                                                   accum_out=hsum[:, bass.ds(g.index, 1)]).then_inc(c_hh, 1)

            run_pass(dve, gru, 4)
            dve.wait_ge(c_sqs, NG)
            dve.wait_ge(c_hh, NG)
            nc.vector.tensor_reduce(bn[:, 0:1], hsum[:], AX_X, ALU.add)
            link(nc.vector.tensor_reduce(bn[:, 1:2], hsq[:], AX_X, ALU.add))
            link(nc.vector.tensor_scalar(bn[:, 0:1], bn[:, 0:1], 1.0 / N, None, ALU.mult))
            link(nc.vector.tensor_tensor(bn[:, 4:5], bn[:, 0:1], bn[:, 0:1], ALU.mult))
            link(nc.vector.scalar_tensor_tensor(bn[:, 4:5], bn[:, 1:2], 1.0 / N, bn[:, 4:5], ALU.mult, ALU.subtract))
            nc.vector.tensor_scalar(bn[:, 2:3], bn[:, 4:5], 0.0, None, ALU.max).then_inc(bn_v, 1)
            dve.wait_ge(bn_r, 1)
            link(nc.vector.reciprocal(bn[:, 4:5], bn[:, 3:4]))
            link(nc.vector.tensor_tensor(bn[:, 5:6], gb_sb[:, 0:1], bn[:, 4:5], ALU.mult))
            link(nc.vector.tensor_tensor(bn[:, 7:8], bn[:, 5:6], bn[:, 0:1], ALU.mult))
            link(nc.vector.tensor_tensor(bn[:, 6:7], gb_sb[:, 1:2], bn[:, 7:8], ALU.subtract))
            nc.vector.tensor_scalar(scale_diag[:], ident[:], bn[:, 5:6], None, ALU.mult).then_inc(bn_ok, 1)
            wait_all_dmas(dve, c_st, 1, FREE)

            def final(group_of):
                if g := group_of(2):
                    k = g.slot(4)
                    wait(dve, o_tr, g.done())
                    row_stats(g, lambda j: bank[k][:, j * D:(j + 1) * D], o_s6, o_oo)
                normaliser(group_of(2), group_of(3), o_s6, o_sd, o_root, o_dq, o_var, o_rs)
                if g := group_of(0):
                    k = g.slot(4)
                    wait(dve, o_tr, g.freed(4))
                    if g.kept:
                        nc.vector.tensor_scalar(o_t[k], kept(g), bn[:, 5:6], bn[:, 6:7], ALU.mult, ALU.add).then_inc(o_q, 1)
                    else:
                        wait(dve, o_iny[k], g.dma(4))
                        nc.vector.tensor_scalar(o_t[k], o_y[k], bn[:, 6:7], None, ALU.add).then_inc(o_q, 1)

            run_pass(dve, final, 3)

        @block.tensor
        def _(pe):
            def count_edges(i, first, last):
                for c in range(HU):
                    pe.wait_ge(oh_ready, i * HU + (c + 1))
                    nc.tensor.matmul(bank[0][:, 0:NT], oh_lo[:, c % HS, :], oh_hi[:, c % HS, :], start=first and c == 0,
                                     stop=last and c == HU - 1, skip_group_check=True).then_inc(oh_used, 1)

            count_edges(0, True, False)
            with pe.Fori(1, ET // HU - 1) as i:
                count_edges(i, False, False)
            count_edges(ET // HU - 1, False, True)
            pe.wait_ge(consts, CONSTS)
            pe.wait_ge(cnt_copied, 1)
            for c in range(QC):
                last = nc.tensor.matmul(bank[1][0:QT, c:c + 1], cnt[:, c * QT:(c + 1) * QT], ones[:, 0:1], start=True, stop=True)
            last.then_inc(tile_cnts, 1)
            pe.wait_ge(tile_cnts_sb, 1)
            for c in range(QC):
                for b in range(c):
                    nc.tensor.matmul(bank[2][0:QT, c:c + 1], ones[0:QT, 0:QT], tile_cnt[0:QT, b:b + 1], start=(b == 0), stop=False)
                last = nc.tensor.matmul(bank[2][0:QT, c:c + 1], before[0:QT, 0:QT], tile_cnt[0:QT, c:c + 1], start=(c == 0), stop=True)
            last.then_inc(starts, 1)
            pe.wait_ge(windows_f, 1)
            for win, b in ((win_sf, 3), (win_df, 4)):
                for c in range(QC):
                    last = nc.tensor.transpose(bank[b][:, c * QT:(c + 1) * QT], win[0:QT, c, :], ident[0:QT, 0:QT])
            last.then_inc(windows_T, 1)
            pe.wait_ge(held_rows, 1)
            nc.tensor.matmul(bank[5][:, 0:1], ones[:], held[:], start=True, stop=True).then_inc(held_sum, 1)
            pe.wait_ge(w_loaded, 16 * W_LOADS)
            pe.wait_ge(ready, 1)
            general_tensor(pe, 0, D)

            def sums(n, g, made, agg):
                k = g.slot(2)
                wait(pe, made, g.done())
                wait(pe, landed[g.slot(4)], gathered(n, g))
                for j in range(J):
                    last = nc.tensor.matmul(bank[k][:, j * D:(j + 1) * D], onehot[k][:, j, :], gath[g.slot(4)][:, j, 0:D],
                                            start=True, stop=True)
                last.then_inc(agg, 1)

            def conv(group_of):
                if g := group_of(0):
                    wait(pe, a_sum, g.freed(2))
                    sums(0, g, a_oh, a_agg)
                if g := group_of(2):
                    wait(pe, a_scaled, g.done())
                    wait(pe, a_trc, g.done() - 1)
                    for j in range(J):
                        last = nc.tensor.transpose(bank[2][:, j * P:(j + 1) * P], a_s[g.slot(2)][:, j * D:(j + 1) * D], ident[:])
                    last.then_inc(a_tr, 1)
                if g := group_of(3):
                    wait(pe, a_trc, g.done())
                    wait(pe, a_relu, g.done() - 1)
                    for h in range(2):
                        last = nc.tensor.matmul(bank[3 + h][:], w1_sb[:, h * P:(h + 1) * P], a_T[g.slot(2)], start=True, stop=True)
                    last.then_inc(a_hid, 1)
                if g := group_of(4):
                    k = g.slot(2)
                    wait(pe, a_relu, g.done())
                    wait(pe, a_gs, g.freed(2))
                    for j in range(J):
                        for h, rows in enumerate((a_h0, a_h1)):
                            last = nc.tensor.matmul(bank[5 + k][:, j * D:(j + 1) * D], rows[k][:, j * P:(j + 1) * P],
                                                    w2_sb[:, h, :], start=(h == 0), stop=(h == 1))
                    last.then_inc(a_out, 1)

            run_pass(pe, conv, 4)
            pe.wait_ge(a_gs, NG)
            general_tensor(pe, 1, D)

            def norm(group_of):
                if g := group_of(0):
                    wait(pe, n_zz, g.freed(2))
                    sums(1, g, n_oh, n_agg)
                if g := group_of(3):
                    k = g.slot(2)
                    wait(pe, n_yy, g.done())
                    wait(pe, n_trc, g.freed(2))
                    for j in range(J):
                        last = nc.tensor.transpose(bank[2 + k][:, j * P:(j + 1) * P], n_y[g.slot(4)][:, j * D:(j + 1) * D], ident[:])
                    last.then_inc(n_tr, 1)
                if g := group_of(5):
                    wait(pe, n_trc, g.done())
                    if g.kept:
                        wait(pe, n_hk, g.freed(2) - FREE)
                        nc.tensor.matmul(bank[6 + g.slot(2)][:], whh_sb[:, 2 * D:3 * D], n_T[g.slot(4)],
                                         start=True, stop=True).then_inc(n_hn, 1)
                    wait(pe, n_mc, g.done() - 1)
                    for j in range(J):
                        last = nc.tensor.matmul(bank[4 + j // 2][:, (j % 2) * DM:(j % 2 + 1) * DM],
                                                n_T[g.slot(4)][:, j * P:(j + 1) * P], wm_sb[:], start=True, stop=True)
                    last.then_inc(n_mm, 1)

            run_pass(pe, norm, 5)
            pe.wait_ge(n_mc, NG)
            pe.wait_ge(n_hk, KEPT)
            general_tensor(pe, 2, DM)

            def gru(group_of):
                if g := group_of(3):
                    k = g.slot(2)
                    y, a = c_y[g.slot(4)], c_a[k]
                    wait(pe, c_iny[g.slot(4)], g.dma(4))
                    wait(pe, c_rs, g.freed(2))
                    nc.tensor.matmul(bank_r[k][:], whh_sb[:, 0:D], y, start=True, stop=False)
                    wait(pe, c_aT, g.done())
                    nc.tensor.matmul(bank_r[k][:], wih_sb[:, 0:D], a, start=False, stop=True).then_inc(c_pr, 1)
                    if not g.kept:
                        wait(pe, c_t1, g.done() - 1)
                        nc.tensor.matmul(bank[4][:], whh_sb[:, 2 * D:3 * D], y, start=True, stop=True).then_inc(c_ph, 1)
                    wait(pe, c_t2, g.freed(2))
                    nc.tensor.matmul(bank_n[k][:], wih_sb[:, 2 * D:3 * D], a, start=True, stop=True).then_inc(c_pi, 1)
                    wait(pe, c_zs, g.done() - 1)
                    nc.tensor.matmul(bank[3][:], whh_sb[:, D:2 * D], y, start=True, stop=False)
                    nc.tensor.matmul(bank[3][:], wih_sb[:, D:2 * D], a, start=False, stop=True).then_inc(c_pz, 1)
                if g := group_of(1):
                    k = g.slot(2)
                    wait(pe, c_aT, g.freed(2))
                    wait(pe, c_oh, g.done())
                    wait(pe, c_wt, g.done())
                    for j in range(J):
                        last = nc.tensor.matmul(bank[k][:, j * P:(j + 1) * P], gath[g.slot(4)][:, j, 0:D], onehot[k][:, j, :],
                                                start=True, stop=True)
                    last.then_inc(c_agg, 1)

            run_pass(pe, gru, 3)
            for gates in (c_aT, c_rs, c_t1, c_t2, c_zs):
                pe.wait_ge(gates, NG)
            pe.wait_ge(bn_ok, 2)

            def final(group_of):
                if g := group_of(1):
                    k = g.slot(4)
                    wait(pe, o_q, g.done())
                    wait(pe, o_iny[k], g.dma(4))
                    if not g.kept:
                        wait(pe, o_inh[k], g.dma(4))
                    wait(pe, o_oo, g.freed(4))
                    for j in range(J):
                        tile = slice(j * P, (j + 1) * P)
                        nc.tensor.matmul(bank[k][:, tile], (o_y if g.kept else o_h)[k][:, tile], (ident if g.kept else scale_diag)[:],
                                         start=True, stop=False)
                        last = nc.tensor.matmul(bank[k][:, tile], o_t[k][:, tile], ident[:], start=False, stop=True)
                    last.then_inc(o_tr, 1)

            run_pass(pe, final, 1)


_INS = ["x", "src", "dst", "W1", "b1", "W2", "b2", "W_msg", "b_msg", "W_att", "b_att", "W_ih", "b_ih", "W_hh", "b_hh", "gamma", "beta"]


def kernel(**inputs):
    import concourse.bacc as bacc
    from concourse.bass_utils import run_bass_kernel_spmd

    a = {k.split("gnn_")[-1]: np.asarray(v) for k, v in inputs.items()}
    x = np.zeros((NP, D), a["x"].dtype)
    x[:N] = a["x"]
    x = np.ascontiguousarray(x.reshape(NG, J, P, D).transpose(0, 2, 1, 3)).reshape(NG, P, J * D)
    src, dst = np.zeros(EL, a["src"].dtype), np.full(EL, PAD_DST, a["dst"].dtype)
    src[:E], dst[:E] = a["src"], a["dst"]

    def columns(v):
        return np.ascontiguousarray(v.reshape(-1, P).T)

    arrays = {
        "x": x, "src": src, "dst": dst, "W1": a["W1"], "b1": columns(a["b1"]), "W2": a["W2"], "b2": a["b2"],
        "W_msg": a["W_msg"], "b_msg": a["b_msg"], "W_att": a["W_att"], "b_att": a["b_att"],
        "W_ih": np.ascontiguousarray(a["W_ih"].T), "b_ih": columns(a["b_ih"]),
        "W_hh": np.ascontiguousarray(a["W_hh"].T), "b_hh": columns(a["b_hh"]),
        "gamma": columns(a["gamma"]), "beta": columns(a["beta"]),
    }
    nc = bacc.Bacc("TRN2", target_bir_lowering=False, num_devices=1)
    args = [nc.dram_tensor(f"in_{k}", arrays[k].shape, mybir.dt.from_np(arrays[k].dtype), kind="ExternalInput").ap() for k in _INS]
    result = nc.dram_tensor("out_y", [NG, P, J * D], F32, kind="ExternalOutput").ap()
    build_gnn(nc, *args, result)
    r = run_bass_kernel_spmd(nc, [{f"in_{k}": np.ascontiguousarray(arrays[k]) for k in _INS}], core_ids=[0])
    y = r.results[0]["out_y"].reshape(NG, P, J, D).transpose(0, 2, 1, 3).reshape(NP, D)
    return np.ascontiguousarray(y[:N])
```
